# Optimizing a Trainium2 kernel written in Bass

```python
import numpy as np
import jax
import jax.numpy as jnp

def _softmax(x, axis=-1):
    return jax.nn.softmax(x, axis=axis)

def _gelu(x):
    return jax.nn.gelu(x, approximate=True)

def _silu(x):
    return jax.nn.silu(x)

def _sigmoid(x):
    return jax.nn.sigmoid(x)

def _layernorm(x, axis=-1, eps=1e-05):
    m = jnp.mean(x, axis=axis, keepdims=True)
    v = jnp.var(x, axis=axis, keepdims=True)
    return (x - m) / jnp.sqrt(v + eps)

def _scatter_add(tgt, idx, src, axis=0):
    return tgt.at[idx].add(src)

def _segment_sum(src, seg, n):
    return jax.ops.segment_sum(src, seg, n)
kernel_name = 'mk_gps_d1_gnn_r8_1d2c93'

def setup_inputs(seed: int=0):
    np.random.seed(seed)
    _w = jnp.asarray

    def _rec_inputs():
        import jax
        import jax.numpy as jnp
        _gk = jax.random.key(seed)
        x = -6.415e-05 + 1 * jax.random.normal(jax.random.fold_in(_gk, 1), (1250, 1024), jnp.float32)
        _s = jax.random.randint(jax.random.fold_in(_gk, 2), (10000,), 0, 1250, jnp.int32)
        _d = jax.random.randint(jax.random.fold_in(_gk, 3), (10000,), 0, 1250, jnp.int32)
        _loop = jnp.arange(1250, dtype=jnp.int32)
        src = jnp.concatenate([_s, _d, _loop])
        dst = jnp.concatenate([_d, _s, _loop])
        _o = jnp.argsort(dst, stable=True)
        src = src[_o]
        dst = dst[_o]
        edge_type_8 = jax.random.randint(jax.random.fold_in(_gk, 12), (21250,), 0, 8, jnp.int32)
        return (x, src, dst, edge_type_8)
    x, src, dst, edge_type_8 = _rec_inputs()

    def _L0_gnn_setup():
        import jax, jax.numpy as jnp
        import numpy as np
        N, D, R, E = (1250, 1024, 8, 10000)

        def _rgcn(x, edge_index, edge_type, weight, root, bias):
            src, dst = (edge_index[0], edge_index[1])
            msgs = x[src]
            out = x @ root + bias
            n = x.shape[0]
            for r in range(weight.shape[0]):
                mask = (edge_type == r).astype(x.dtype)
                sums = jax.ops.segment_sum(msgs * mask[:, None], dst, num_segments=n)
                cnt = jax.ops.segment_sum(mask, dst, num_segments=n)
                mean = sums / jnp.maximum(cnt, 1.0)[:, None]
                out = out + mean @ weight[r]
            return out
        key = jax.random.key(seed)
        ks = jax.random.split(key, 8)
        s = 1.0 / np.sqrt(D)
        x = jax.random.normal(ks[0], (N, D), dtype=jnp.float32)
        edge_index = jax.random.randint(ks[1], (2, E), 0, N, dtype=jnp.int64)
        edge_type = jax.random.randint(ks[2], (E,), 0, R, dtype=jnp.int64)
        weight = jax.random.normal(ks[3], (R, D, D), dtype=jnp.float32) * s
        root = jax.random.normal(ks[4], (D, D), dtype=jnp.float32) * s
        bias = jnp.zeros((D,), dtype=jnp.float32)
        w_gate = jax.random.normal(ks[5], (2 * D, D), dtype=jnp.float32) * (1.0 / np.sqrt(2 * D))
        b_gate = jnp.zeros((D,), dtype=jnp.float32)
        return {'x': x, 'edge_index': edge_index, 'edge_type': edge_type, 'weight': weight, 'root': root, 'bias': bias, 'w_gate': w_gate, 'b_gate': b_gate}
    _L0_gnn_all = _L0_gnn_setup()
    _L0_gnn_in = {k: v for k, v in _L0_gnn_all.items() if k in ('weight', 'root', 'bias', 'w_gate', 'b_gate')}
    del _L0_gnn_all

    def _L0_mix_setup():
        import jax, jax.numpy as jnp
        import numpy as np
        B, S, H = (4, 512, 1024)
        NH, HD, M = (16, 64, 256)
        key = jax.random.key(seed)
        ks = jax.random.split(key, 10)
        sd = 1.0 / np.sqrt(H)
        return {'x': jax.random.normal(ks[0], (B, S, H), dtype=jnp.float32), 'Wq': jax.random.normal(ks[1], (H, H), dtype=jnp.float32) * sd, 'bq': jnp.zeros((H,), dtype=jnp.float32), 'Wk': jax.random.normal(ks[2], (H, H), dtype=jnp.float32) * sd, 'bk': jnp.zeros((H,), dtype=jnp.float32), 'Wv': jax.random.normal(ks[3], (H, H), dtype=jnp.float32) * sd, 'bv': jnp.zeros((H,), dtype=jnp.float32), 'Wo': jax.random.normal(ks[4], (H, H), dtype=jnp.float32) * sd, 'bo': jnp.zeros((H,), dtype=jnp.float32), 'rf': jax.random.normal(ks[5], (M, HD), dtype=jnp.float32)}
    _L0_mix_all = _L0_mix_setup()
    _L0_mix_in = {k: v for k, v in _L0_mix_all.items() if k in ('Wq', 'bq', 'Wk', 'bk', 'Wv', 'bv', 'Wo', 'bo', 'rf')}
    del _L0_mix_all

    def _L0_ffn_setup():
        import jax, jax.numpy as jnp
        import numpy as np
        SEQ, BATCH, D_IN, D_LAT = (512, 64, 1024, 1024)
        key = jax.random.key(seed)
        ks = jax.random.split(key, 5)
        scale = 0.02
        d_cat = D_IN + D_LAT
        return {'x': jax.random.normal(ks[0], (SEQ, BATCH, D_IN), dtype=jnp.float32), 'W_f': jax.random.normal(ks[1], (D_LAT, d_cat), dtype=jnp.float32) * scale, 'b_f': jnp.zeros((D_LAT,), dtype=jnp.float32), 'W_i': jax.random.normal(ks[2], (D_LAT, d_cat), dtype=jnp.float32) * scale, 'b_i': jnp.zeros((D_LAT,), dtype=jnp.float32), 'W_o': jax.random.normal(ks[3], (D_LAT, d_cat), dtype=jnp.float32) * scale, 'b_o': jnp.zeros((D_LAT,), dtype=jnp.float32), 'W_c': jax.random.normal(ks[4], (D_LAT, d_cat), dtype=jnp.float32) * scale, 'b_c': jnp.zeros((D_LAT,), dtype=jnp.float32)}
    _L0_ffn_all = _L0_ffn_setup()
    _L0_ffn_in = {k: v for k, v in _L0_ffn_all.items() if k in ('W_f', 'b_f', 'W_i', 'b_i', 'W_o', 'b_o', 'W_c', 'b_c')}
    del _L0_ffn_all
    return {'x': x, 'src': src, 'dst': dst, 'edge_type_8': edge_type_8, 'L0_gnn_weight': _L0_gnn_in['weight'], 'L0_gnn_root': _L0_gnn_in['root'], 'L0_gnn_bias': _L0_gnn_in['bias'], 'L0_gnn_w_gate': _L0_gnn_in['w_gate'], 'L0_gnn_b_gate': _L0_gnn_in['b_gate'], 'L0_mix_Wq': _L0_mix_in['Wq'], 'L0_mix_bq': _L0_mix_in['bq'], 'L0_mix_Wk': _L0_mix_in['Wk'], 'L0_mix_bk': _L0_mix_in['bk'], 'L0_mix_Wv': _L0_mix_in['Wv'], 'L0_mix_bv': _L0_mix_in['bv'], 'L0_mix_Wo': _L0_mix_in['Wo'], 'L0_mix_bo': _L0_mix_in['bo'], 'L0_mix_rf': _L0_mix_in['rf'], 'L0_ffn_W_f': _L0_ffn_in['W_f'], 'L0_ffn_b_f': _L0_ffn_in['b_f'], 'L0_ffn_W_i': _L0_ffn_in['W_i'], 'L0_ffn_b_i': _L0_ffn_in['b_i'], 'L0_ffn_W_o': _L0_ffn_in['W_o'], 'L0_ffn_b_o': _L0_ffn_in['b_o'], 'L0_ffn_W_c': _L0_ffn_in['W_c'], 'L0_ffn_b_c': _L0_ffn_in['b_c']}

def reference(x, src, dst, edge_type_8, L0_gnn_weight, L0_gnn_root, L0_gnn_bias, L0_gnn_w_gate, L0_gnn_b_gate, L0_mix_Wq, L0_mix_bq, L0_mix_Wk, L0_mix_bk, L0_mix_Wv, L0_mix_bv, L0_mix_Wo, L0_mix_bo, L0_mix_rf, L0_ffn_W_f, L0_ffn_b_f, L0_ffn_W_i, L0_ffn_b_i, L0_ffn_W_o, L0_ffn_b_o, L0_ffn_W_c, L0_ffn_b_c):
    import jax
    import jax.numpy as jnp

    def _L0_gnn_ref(x, edge_index, edge_type, weight, root, bias, w_gate, b_gate):
        import jax, jax.numpy as jnp
        import numpy as np
        N, D, R, E = (1250, 1024, 8, 10000)

        def _rgcn(x, edge_index, edge_type, weight, root, bias):
            src, dst = (edge_index[0], edge_index[1])
            msgs = x[src]
            out = x @ root + bias
            n = x.shape[0]
            for r in range(weight.shape[0]):
                mask = (edge_type == r).astype(x.dtype)
                sums = jax.ops.segment_sum(msgs * mask[:, None], dst, num_segments=n)
                cnt = jax.ops.segment_sum(mask, dst, num_segments=n)
                mean = sums / jnp.maximum(cnt, 1.0)[:, None]
                out = out + mean @ weight[r]
            return out
        u = _rgcn(x, edge_index, edge_type, weight, root, bias)
        z = jnp.concatenate([u, x], axis=1) @ w_gate + b_gate
        h = jnp.tanh(u) * z + x * (1.0 - z)
        return h

    def _L0_mix_ref(x, Wq, bq, Wk, bk, Wv, bv, Wo, bo, rf):
        import jax, jax.numpy as jnp
        import numpy as np
        B, S, H = (4, 512, 1024)
        NH, HD, M = (16, 64, 256)
        b, s, _ = x.shape
        scale = HD ** (-0.5)
        q = (x @ Wq + bq).reshape(b, s, NH, HD)
        k = (x @ Wk + bk).reshape(b, s, NH, HD)
        v = (x @ Wv + bv).reshape(b, s, NH, HD)
        qf = jax.nn.relu(jnp.einsum('bsnd,md->bsnm', q, rf))
        kf = jax.nn.relu(jnp.einsum('bsnd,md->bsnm', k, rf))
        scores = jnp.einsum('bsnm,bshm->bsnh', qf, kf) * scale
        attn = jax.nn.softmax(scores, axis=-1)
        out = jnp.einsum('bsnh,bshd->bsnd', attn, v).reshape(b, s, NH * HD)
        return out @ Wo + bo

    def _L0_ffn_ref(x, W_f, b_f, W_i, b_i, W_o, b_o, W_c, b_c):
        import jax, jax.numpy as jnp
        import numpy as np
        SEQ, BATCH, D_IN, D_LAT = (512, 64, 1024, 1024)
        d_lat = W_f.shape[0]
        W_all = jnp.concatenate([W_f, W_i, W_o, W_c], axis=0)
        b_all = jnp.concatenate([b_f, b_i, b_o, b_c], axis=0)
        batch = x.shape[1]
        h0 = jnp.zeros((batch, d_lat), dtype=x.dtype)
        c0 = jnp.zeros((batch, d_lat), dtype=x.dtype)

        def step(carry, x_t):
            h, c = carry
            z = jnp.concatenate([h, x_t], axis=-1)
            gates = z @ W_all.T + b_all
            f_t = jax.nn.sigmoid(gates[:, 0 * d_lat:1 * d_lat])
            i_t = jax.nn.sigmoid(gates[:, 1 * d_lat:2 * d_lat])
            o_t = jax.nn.sigmoid(gates[:, 2 * d_lat:3 * d_lat])
            g_t = jnp.tanh(gates[:, 3 * d_lat:4 * d_lat])
            c_t = f_t * c + i_t * g_t
            h_t = o_t * jnp.tanh(c_t)
            return ((h_t, c_t), h_t)
        _, hidden_states = jax.lax.scan(step, (h0, c0), x)
        return hidden_states
    edge_index = jnp.stack([src, dst])
    xn = _layernorm(x, axis=-1)
    x = x + _L0_gnn_ref(xn, edge_index, edge_type_8, L0_gnn_weight, L0_gnn_root, L0_gnn_bias, L0_gnn_w_gate, L0_gnn_b_gate) + _L0_mix_ref(xn[None], L0_mix_Wq, L0_mix_bq, L0_mix_Wk, L0_mix_bk, L0_mix_Wv, L0_mix_bv, L0_mix_Wo, L0_mix_bo, L0_mix_rf)[0]
    x = x + _L0_ffn_ref(_layernorm(x, axis=-1)[None], L0_ffn_W_f, L0_ffn_b_f, L0_ffn_W_i, L0_ffn_b_i, L0_ffn_W_o, L0_ffn_b_o, L0_ffn_W_c, L0_ffn_b_c)[0]
    return x

_drawn_inputs = setup_inputs


def setup_inputs(seed=0):
    import zlib

    import numpy as np

    out = dict(_drawn_inputs(seed))
    spreads = {'L0_gnn_bias': (0.0, 0.1),
     'L0_gnn_b_gate': (0.0, 0.1),
     'L0_mix_bq': (0.0, 0.1),
     'L0_mix_bk': (0.0, 0.1),
     'L0_mix_bv': (0.0, 0.1),
     'L0_mix_bo': (0.0, 0.1),
     'L0_ffn_b_f': (0.0, 0.1),
     'L0_ffn_b_i': (0.0, 0.8),
     'L0_ffn_b_o': (0.0, 0.8),
     'L0_ffn_b_c': (0.0, 0.8)}
    factors = {'L0_ffn_W_i': 5.258, 'L0_ffn_W_o': 4.91}
    for name, (base, spread) in spreads.items():
        noise = np.random.default_rng([zlib.crc32(name.encode()), seed]).standard_normal(out[name].shape)
        drawn = base * np.exp(spread * noise) if base else spread * noise
        out[name] = jnp.asarray(drawn.astype(out[name].dtype))
    for name, factor in factors.items():
        out[name] = (out[name] * factor).astype(out[name].dtype)
    return out
```

```python
from contextlib import ExitStack

import numpy as np
import concourse.bass as bass
from concourse import mybir

F32 = mybir.dt.float32
F32R = mybir.dt.float32r
F16 = mybir.dt.float16
I32 = mybir.dt.int32
U32 = mybir.dt.uint32
ALU = mybir.AluOpType
ACT = mybir.ActivationFunctionType
AX = mybir.AxisListType

P = 128
N = 1250
D = 1024
R = 8
TT = 125
NT = N // TT
KB = D // P
HC = 512
NPAD = 1280
EP, EJ = 125, 180
NB = R * NT
CAP = 3
NC = NB * CAP
NH, HD, M = 16, 64, 256
EPS = 1e-5
SIZE = {F32: 4, F32R: 4, I32: 4, U32: 4, F16: 2}
MID = "Internal"
XS = 1024.0
NEG = -1e30

STEP_QK, STEP_TM, STEP_REL, STEP_GATE, STEP_WO, STEP_LSTM = 0, 4, 10, 26, 28, 30


def mm3(nc, out, a, b, first, last):
    nc.tensor.matmul(out, a[0], b[0], start=first, stop=False)
    nc.tensor.matmul(out, a[0], b[1], start=False, stop=False)
    return nc.tensor.matmul(out, a[1], b[0], start=False, stop=last)


class Chain:

    def __init__(self, eng, sem, base=0):
        self.eng, self.sem, self.base, self.n = eng, sem, base, 0

    def add(self, ins):
        ins.then_inc(self.sem, 1)
        self.n += 1
        return ins

    def wait(self):
        self.eng.wait_ge(self.sem, self.base + self.n)

    def link(self, ins):
        self.add(ins)
        self.wait()


class Memory:

    def __init__(self, nc):
        self.nc = nc
        self.base = (nc.sbuf_base + 63) // 64 * 64
        self.end = nc.sbuf_usable_end
        self.cursor = 0

    def at(self, name, shape, dt, offset):
        size = int(np.prod(shape[1:])) * SIZE[dt]
        assert self.base + offset + size <= self.end, (name, offset, size, self.end - self.base)
        return self.nc.alloc_sbuf_tensor_at(name, shape, dt, offset=self.base + offset)

    def next(self, name, shape, dt):
        t = self.at(name, shape, dt, self.cursor)
        self.cursor += (int(np.prod(shape[1:])) * SIZE[dt] + 31) // 32 * 32
        return t


def phase_project(nc, mem, io, keep):
    half = KB * HC * 4
    whi = [mem.at(f"p_whi{s}", [P, KB, HC], F32R, o) for s, o in enumerate((0, 4 * half))]
    wlo = [mem.at(f"p_wlo{s}", [P, KB, HC], F32R, o) for s, o in enumerate((half, 5 * half))]
    raw = [mem.at(f"p_raw{s}", [P, KB, HC], F32, o) for s, o in enumerate((2 * half, 3 * half))]
    x_all = mem.at("p_x_all", [TT, NT, D], F32, 3 * half)
    xn = [mem.at(f"p_xn{s}", [TT, D], F32, 3 * half + NT * D * 4 + s * D * 4) for s in range(2)]
    mem.cursor = 6 * half
    xT_hi = mem.next("p_xT_hi", [P, KB, N], F32R)
    xT_lo = mem.next("p_xT_lo", [P, KB, N], F32R)
    at_small = mem.cursor
    mem.cursor = at_small + keep["bytes"]
    at_stage = mem.cursor
    stage = [mem.next(f"p_stage{s}", [P, HC], F32) for s in range(4)]
    hl = [mem.at(f"p_hl{s}", [TT, 2 * D], F16, at_stage + s * 4 * D) for s in range(2)]
    at_sort = mem.cursor
    CB = 5
    NCH = NB // CB
    oh_c = mem.next("p_oh_c", [EP, CB, EJ], F16)
    reset = mem.next("p_reset", [EP, CB, EJ], F16)
    scan_c = mem.next("p_scan_c", [EP, CB, EJ], F32)
    after_sort = mem.cursor
    JU, JW = 3, 704
    job = [mem.at(f"p_job{s}", [EP, JU, JW], F16, at_sort + s * JU * JW * 2) for s in range(2)]
    bo_bc = mem.at("p_bo_bc", [TT, D], F32, at_sort)
    mem.cursor = max(after_sort, at_sort + 2 * JU * JW * 2)
    bias_bc = [mem.next(f"p_bias_bc{s}", [TT, HC], F32) for s in range(2)]
    bias_qk = mem.next("p_bias_qk", [P, 2, KB], F32)
    edges = mem.next("p_edges", [EP, 3, EJ], I32)
    k = keep
    at_stats = at_sort + 4 * D
    stats = mem.at("p_stats", [TT, NT, 2, 6], F32, at_stats)
    mv = mem.at("p_mv", [TT, NT, 2], F32, at_stats + 512)
    std = mem.at("p_std", [TT, NT], F32, at_stats + 640)
    rstd = mem.at("p_rstd", [TT, NT], F32, at_stats + 704)
    eps = mem.at("p_eps", [TT, 1], F32, at_stats + 768)
    tot = mem.next("p_tot", [EP, NB], F32)
    tot16 = mem.next("p_tot16", [EP, NB], F16)
    base1 = mem.next("p_base1", [EP, NB], F32)
    tmp = mem.next("p_tmp", [EP, EJ], F32)
    below = mem.next("p_below", [EP, EP], F16)
    ones16 = mem.next("p_ones16", [EP, P], F16)
    zero16 = mem.next("p_zero16", [EP, NC], F16)
    thr = mem.next("p_thr", [EP, 56], F32)
    mx = mem.next("p_mx", [EP, 2], F32)

    with ExitStack() as ctx:
        def sem(name):
            return ctx.enter_context(nc.semaphore("p_" + name))

        ring = ctx.enter_context(nc.psum_tensor("p_ring", [P, 4, HC], F32))
        ps_src = ctx.enter_context(nc.psum_tensor("p_ps_src", [P, HC], F32))
        ps_dst = ctx.enter_context(nc.psum_tensor("p_ps_dst", [P, HC], F32))
        ps_cnt = ctx.enter_context(nc.psum_tensor("p_ps_cnt", [P, HC], F32))
        ps_base = ctx.enter_context(nc.psum_tensor("p_ps_base", [P, HC], F32))
        x_landed = [sem(f"x_landed{i}") for i in range(5)]
        w_landed = [sem(f"w_landed{s}") for s in range(2)]
        bias_landed = [sem(f"bias_landed{s}") for s in range(2)]
        bqk_landed, bo_landed, edges_landed = sem("bqk_landed"), sem("bo_landed"), sem("edges_landed")
        consts, pconst = sem("consts"), sem("pconst")
        w_hi, w_lo = sem("w_hi"), sem("w_lo")
        var_ready, std_ready = sem("var_ready"), sem("std_ready")
        xn_ready, h16_ready, l16_ready = sem("xn_ready"), sem("h16_ready"), sem("l16_ready")
        tr_done, xT_hi_ready, xT_lo_ready = sem("tr_done"), sem("xT_hi_ready"), sem("xT_lo_ready")
        xx_step, xx_stored = sem("xx_step"), sem("xx_stored")
        xn_stored = [sem(f"xn_stored{s}") for s in range(2)]
        hl_stored = [sem(f"hl_stored{s}") for s in range(2)]
        gemm_done, qk_evac, tm_evac = sem("gemm_done"), sem("qk_evac"), sem("tm_evac")
        stored = [sem(f"stored{s}") for s in range(4)]
        pad_zero, pad_stored = sem("pad_zero"), sem("pad_stored")
        dve_step = sem("dve_step")
        tot_ready, base_ready, base_read = sem("tot_ready"), sem("base_ready"), sem("base_read")
        job_ready, job_used, table_done = sem("job_ready"), sem("job_used"), sem("table_done")
        block = ctx.enter_context(nc.Block())

        x_rows = io["x"].rearrange("(t p) d -> p t d", p=TT)
        QK_CH = [(0, 512), (512, 512), (1024, N - 1024)]

        @block.sync
        def _(sp):
            for i in range(5):
                sp.dma_start(x_all[:, 2 * i:2 * i + 2, :], x_rows[:, 2 * i:2 * i + 2, :]).then_inc(x_landed[i], 16)
            sp.dma_start(raw[0][:, :, :], io["w"][0]).then_inc(w_landed[0], 16)
            sp.wait_ge(xx_stored, 16 * NT)
            sp.wait_ge(xn_stored[0], 16 * NT // 2)
            sp.wait_ge(xn_stored[1], 16 * NT // 2)
            sp.wait_ge(xT_lo_ready, NT)
            sp.wait_ge(l16_ready, NT)
            for s in range(1, STEP_REL):
                if s >= 2:
                    sp.wait_ge(w_lo, 4 * (s - 1))
                sp.dma_start(raw[s % 2][:, :, :], io["w"][s]).then_inc(w_landed[s % 2], 16)
                if s >= STEP_TM:
                    m = s - STEP_TM
                    if m >= 2:
                        sp.wait_ge(tm_evac, 4 + NT * (m - 1))
                    sp.dma_start(bias_bc[m % 2][:, :], io["bias_tm"][m:m + 1, :].to_broadcast([TT, HC])
                                 ).then_inc(bias_landed[m % 2], 16)

        def split_hi(s, slot, sem_val):
            nc.scalar.wait_ge(w_landed[slot], sem_val)
            for c in range(4):
                nc.scalar.activation(whi[slot][:, 2 * c:2 * c + 2, :], raw[slot][:, 2 * c:2 * c + 2, :],
                                     ACT.Copy).then_inc(w_hi, 1)

        def split_lo(s, slot):
            for c in range(4):
                nc.vector.wait_ge(w_hi, 4 * s + (c + 1))
                nc.vector.tensor_tensor(wlo[slot][:, 2 * c:2 * c + 2, :], raw[slot][:, 2 * c:2 * c + 2, :],
                                        whi[slot][:, 2 * c:2 * c + 2, :].bitcast(F32), ALU.subtract
                                        ).then_inc(w_lo, 1)

        @block.gpsimd
        def _(pool):
            pool.dma_start(bo_bc[:, :], io["bo"].to_broadcast([TT, D])).then_inc(bo_landed, 16)
            pool.dma_start(bias_qk[:, :, :], io["bias_qk"]).then_inc(bqk_landed, 16)
            pool.iota(k["iota16"][:, :], [[1, 256]], base=0, channel_multiplier=0,
                      allow_small_or_imprecise_dtypes=True).then_inc(pconst, 1)
            pool.iota(thr[:, :], [[CAP * P, 56]], base=0, channel_multiplier=0,
                      allow_small_or_imprecise_dtypes=True).then_inc(pconst, 1)
            pool.memset(k["ident"][:, :], 0.0).then_inc(pconst, 1)
            pool.memset(below[:, :], 1.0).then_inc(pconst, 1)
            pool.memset(ones16[:, :], 1.0).then_inc(pconst, 1)
            pool.memset(zero16[:, :], 0.0).then_inc(pconst, 1)
            pool.memset(stage[0][:, :], 0.0).then_inc(pad_zero, 1)
            pool.wait_ge(pconst, 6)
            pool.affine_select(out=k["ident"][:, :], in_=k["ident"][:, :], compare_op=ALU.not_equal, fill=1.0, base=0,
                               pattern=[[-1, P]], channel_multiplier=1).then_inc(consts, 1)
            pool.affine_select(out=below[:, :], in_=below[:, :], compare_op=ALU.is_ge, fill=0.0, base=-1,
                               pattern=[[1, EP]], channel_multiplier=-1).then_inc(consts, 1)
            pool.wait_ge(pad_zero, 1)
            pad = NPAD - N
            for b in range(2 * KB):
                pool.dma_start(io["qkT"][b * P:(b + 1) * P, N:NPAD], stage[0][:, 0:pad]).then_inc(pad_stored, 16)
            for c in range(2):
                pool.dma_start(io["tm"][N:NPAD, c * HC:(c + 1) * HC], stage[0][0:pad, :]).then_inc(pad_stored, 16)
            pool.wait_ge(bo_landed, 16)
            for t in range(NT):
                pool.wait_ge(xn_ready, t + 1)
                pool.tensor_tensor(x_all[:, t, :], x_all[:, t, :], xn[t % 2][:, :], ALU.add).then_inc(xx_step, 1)
                pool.wait_ge(xx_step, 2 * t + 1)
                pool.tensor_tensor(x_all[:, t, :], x_all[:, t, :], bo_bc[:, :], ALU.add).then_inc(xx_step, 1)
                pool.dma_start(io["xn"][t * TT:(t + 1) * TT, :], xn[t % 2][:, :]).then_inc(xn_stored[t % 2], 16)
                pool.wait_ge(xx_step, 2 * t + 2)
                pool.dma_start(io["xx"][t * TT:(t + 1) * TT, :], x_all[:, t, :]).then_inc(xx_stored, 16)
                pool.wait_ge(l16_ready, t + 1)
                pool.dma_start(io["rows"][t * TT:(t + 1) * TT, :], hl[t % 2][:, :]).then_inc(hl_stored[t % 2], 16)
            with pool.Fori(0, 2) as m:
                for u in range(24):
                    h, dd, c = u // 12, u % 12 // 3, u % 3
                    c0, cn = QK_CH[c]
                    pool.wait_ge(qk_evac, 24 * m + (u + 5))
                    pool.dma_start(io["qkT"][bass.ds(m * D + (4 * h + dd) * P, P), c0:c0 + cn],
                                   stage[u % 4][:, 0:cn]).then_inc(stored[u % 4], 16)
            with pool.Fori(0, 3) as m:
                for u in range(2 * NT):
                    h, t = divmod(u, NT)
                    pool.wait_ge(tm_evac, 2 * NT * m + (u + 5))
                    pool.dma_start(io["tm"][bass.ds(m * NPAD + t * TT, TT), h * HC:(h + 1) * HC],
                                   stage[u % 4][0:TT, :]).then_inc(stored[u % 4], 16)
            for s in range(4):
                pool.wait_ge(stored[s], 16 * ((48 + 60) // 4))

        @block.scalar
        def _(act):
            act.dma_start(edges[:, :, :], io["edges"]).then_inc(edges_landed, 16)
            split_hi(0, 0, 16)
            act.wait_ge(var_ready, 1)
            act.activation(std[:, :], mv[:, :, 1], ACT.Sqrt, bias=eps[:, :]).then_inc(std_ready, 1)
            act.wait_ge(pad_stored, 16 * (2 * KB + 2))
            for t in range(NT):
                act.wait_ge(xn_ready, t + 1)
                if t >= 2:
                    act.wait_ge(hl_stored[t % 2], 16 * (t // 2))
                act.activation(hl[t % 2][:, 0:D], xn[t % 2][:, :], ACT.Copy, scale=XS).then_inc(h16_ready, 1)
                act.wait_ge(tr_done, t + 1)
                act.activation(xT_hi[:, :, t * TT:(t + 1) * TT].rearrange("p (b k) t -> p b k t", b=2),
                               ring[:, 2 * (t % 2):2 * (t % 2) + 2, 0:500].rearrange("p b (k t) -> p b k t", t=TT),
                               ACT.Copy).then_inc(xT_hi_ready, 1)
            split_hi(1, 1, 16)
            act.sem_inc(qk_evac, 4)
            act.wait_ge(bqk_landed, 16)
            for s in range(2):
                act.wait_ge(hl_stored[s], 16 * (NT // 2))
            for m in range(2):
                for h in range(2):
                    for v in range(12):
                        u = 12 * h + v
                        cn = QK_CH[u % 3][1]
                        act.wait_ge(gemm_done, 24 * m + (u + 1))
                        if 24 * m + u >= 4:
                            act.wait_ge(stored[u % 4], 16 * (6 * m + u // 4))
                        act.activation(stage[u % 4][:, 0:cn], ring[:, u % 4, 0:cn], ACT.Identity,
                                       bias=bias_qk[:, m, 4 * h + v // 3:4 * h + v // 3 + 1]).then_inc(qk_evac, 1)
                    split_hi(None, h, 16 * m + 32)
            for s in range(STEP_TM + 2, STEP_REL):
                act.wait_ge(gemm_done, 48 + NT * (s - STEP_TM - 1))
                split_hi(s, s % 2, 16 * (s // 2 + 1))

        @block.vector
        def _(dve):
            ch = Chain(dve, dve_step)
            ch.add(dve.memset(eps[:, :], EPS))
            for t in range(NT):
                if t % 2 == 0:
                    dve.wait_ge(x_landed[t // 2], 16)
                for h in range(2):
                    ch.add(dve.bn_stats(stats[:, t, h, :], x_all[:, t, h * HC:(h + 1) * HC]))
            ch.wait()
            for t in range(NT):
                last = dve.bn_aggr(mv[:, t, :], stats[:, t, :, :].rearrange("p a b -> p (a b)"))
            last.then_inc(var_ready, 1)
            split_lo(0, 0)
            dve.wait_ge(std_ready, 1)
            inverse_root(dve, ch, rstd, std, mv[:, :, 1], EPS)

            def normalise(t):
                if t >= 2:
                    dve.wait_ge(tr_done, t - 1)
                    dve.wait_ge(h16_ready, t - 1)
                    dve.wait_ge(l16_ready, t - 1)
                    dve.wait_ge(xx_step, 2 * t - 3)
                    dve.wait_ge(xn_stored[t % 2], 16 * (t // 2))
                dve.tensor_scalar(xn[t % 2][:, :], x_all[:, t, :], mv[:, t, 0:1], rstd[:, t:t + 1],
                                  ALU.subtract, ALU.mult).then_inc(xn_ready, 1)

            normalise(0)
            for t in range(NT):
                if t + 1 < NT:
                    normalise(t + 1)
                dve.wait_ge(h16_ready, t + 1)
                dve.wait_ge(xn_ready, t + 1)
                dve.scalar_tensor_tensor(hl[t % 2][:, D:2 * D], xn[t % 2][:, :], XS, hl[t % 2][:, 0:D],
                                         ALU.mult, ALU.subtract).then_inc(l16_ready, 1)
                dve.wait_ge(xT_hi_ready, t + 1)
                sl = slice(t * TT, (t + 1) * TT)
                dve.tensor_tensor(xT_lo[:, :, sl].rearrange("p (b k) t -> p b k t", b=2),
                                  ring[:, 2 * (t % 2):2 * (t % 2) + 2, 0:500].rearrange("p b (k t) -> p b k t", t=TT),
                                  xT_hi[:, :, sl].bitcast(F32).rearrange("p (b k) t -> p b k t", b=2),
                                  ALU.subtract).then_inc(xT_lo_ready, 1)
            split_lo(1, 1)

            dve.wait_ge(edges_landed, 16)
            dve.wait_ge(pconst, 2)
            srcf, dl, dl1, bkt, lo, hi, rank = (k[n] for n in ("srcf", "dl", "dl1", "bkt", "lo", "hi", "rank"))
            ch.link(dve.tensor_scalar(srcf[:, :], edges[:, 0, :], 0.0, float(N - 1), ALU.max, ALU.min))
            ch.add(dve.tensor_copy(dl[:, :], edges[:, 1, :]))
            ch.add(dve.tensor_copy(bkt[:, :], edges[:, 2, :]))
            ch.link(dve.memset(tmp[:, :], 0.0))
            for w in range(1, NT):
                ch.link(dve.scalar_tensor_tensor(tmp[:, :], dl[:, :], float(w * TT), tmp[:, :], ALU.is_ge, ALU.add))
            ch.add(dve.scalar_tensor_tensor(dl[:, :], tmp[:, :], float(-TT), dl[:, :], ALU.mult, ALU.add))
            ch.link(dve.scalar_tensor_tensor(bkt[:, :], bkt[:, :], float(NT), tmp[:, :], ALU.mult, ALU.add))
            ch.add(dve.tensor_scalar(dl1[:, :], dl[:, :], 1.0, None, ALU.add))
            dve.wait_ge(xx_step, 2 * NT)
            dve.wait_ge(xn_ready, NT)
            ch.add(dve.memset(reset[:, :, :], 1.0))
            ch.add(dve.memset(rank[:, :], 0.0))
            ch.wait()
            ch.link(dve.memset(reset[:, :, 0:1], 0.0))

            def one_hot_chunk(c):
                return dve.tensor_tensor(oh_c[:, :, :], bkt[:, :].unsqueeze(1).to_broadcast([EP, CB, EJ]),
                                         k["iota16"][0:EP, bass.ds(c * CB, CB)].unsqueeze(2).to_broadcast([EP, CB, EJ]),
                                         ALU.is_equal)

            n0 = ch.n
            with dve.Fori(0, NCH) as c:
                lp = Chain(dve, dve_step, base=2 * c + n0)
                lp.link(one_hot_chunk(c))
                lp.link(dve.reduce_sum(tot[:, bass.ds(c * CB, CB)], oh_c[:, :, :], AX.X))
            ch.n += 2 * NCH
            dve.tensor_copy(tot16[:, :], tot[:, :]).then_inc(tot_ready, 1)
            split_lo(2, 0)
            dve.wait_ge(base_ready, 1)
            ch.add(dve.tensor_scalar(base1[:, :], ps_base[0:EP, 0:NB], 1.0, None, ALU.subtract))
            ch.link(dve.reduce_max(mx[:, 0:1], ps_cnt[0:EP, 0:NB], AX.X))
            ch.link(dve.tensor_scalar(thr[:, :], thr[:, :], mx[:, 0:1], None, ALU.is_lt))
            ch.link(dve.reduce_sum(mx[:, 1:2], thr[:, 1:56], AX.X))
            ch.link(dve.tensor_scalar(k["rounds"][0:EP, :], mx[:, 1:2], 1.0, None, ALU.add))

            def rank_chunks(c0, c1):
                n0 = ch.n
                with dve.Fori(c0, c1) as c:
                    lp = Chain(dve, dve_step, base=6 * c + (n0 - 6 * c0))
                    lp.link(one_hot_chunk(c))
                    lp.link(dve.tensor_tensor_scan(scan_c[:, :, :].rearrange("p b j -> p (b j)"),
                                                   reset[:, :, :].rearrange("p b j -> p (b j)"),
                                                   oh_c[:, :, :].rearrange("p b j -> p (b j)"), 0.0, ALU.mult, ALU.add))
                    lp.link(dve.tensor_tensor(scan_c[:, :, :], scan_c[:, :, :],
                                              base1[:, bass.ds(c * CB, CB)].unsqueeze(2).to_broadcast([EP, CB, EJ]),
                                              ALU.add))
                    lp.link(dve.tensor_tensor(scan_c[:, :, :], scan_c[:, :, :], oh_c[:, :, :], ALU.mult))
                    lp.link(dve.reduce_sum(tmp[:, :], scan_c[:, :, :].rearrange("p b j -> p j b"), AX.X))
                    lp.link(dve.tensor_tensor(rank[:, :], rank[:, :], tmp[:, :], ALU.add))
                ch.n += 6 * (c1 - c0)

            rank_chunks(0, NCH // 2)
            split_lo(3, 1)
            rank_chunks(NCH // 2, NCH)
            slot_of_rank(dve, ch, k, tmp)
            split_lo(4, 0)
            split_lo(5, 1)

            dve.sem_inc(tm_evac, 4)
            dve.sem_inc(job_used, 2)

            def token_major(m, last):
                for h in range(2):
                    dve.wait_ge(bias_landed[h], 16 * m + 16)
                    for t in range(NT):
                        u = NT * h + t
                        dve.wait_ge(job_used, 20 * m + (u + 1))
                        for jj in range(JU):
                            o = one_hots(dve, k, job[u % 2][:, jj, :], 60 * m + (3 * u + jj))
                        o.then_inc(job_ready, 1)
                        dve.wait_ge(gemm_done, 20 * m + (48 + u + 1))
                        dve.wait_ge(stored[u % 4], 80 * m + (16 * (u // 4) + 16 * 12))
                        dve.tensor_tensor(stage[u % 4][0:TT, :], ring[0:TT, u % 4, :], bias_bc[h][:, :], ALU.add
                                          ).then_inc(tm_evac, 1)
                    if not last:
                        split_lo(2 * m + (6 + h), h)

            with dve.Fori(0, 2) as m:
                token_major(m, False)
            token_major(2, True)
            dve.wait_ge(table_done, 1)
            read_table(dve, k, ps_src, ps_dst)
            dve.tensor_scalar(k["rc"][:, :], ps_cnt[0:TT, 0:NB], 1.0, None, ALU.max).then_inc(base_read, 1)
            dve.wait_ge(base_read, 1)
            dve.reciprocal(k["rc"][:, :], k["rc"][:, :])

        @block.tensor
        def _(pe):
            pe.wait_ge(consts, 2)
            for t in range(NT):
                pe.wait_ge(xn_ready, t + 1)
                if t >= 2:
                    pe.wait_ge(xT_lo_ready, t - 1)
                for kb in range(KB):
                    o = nc.tensor.transpose(ring[:, 2 * (t % 2) + kb // 4, (kb % 4) * TT:(kb % 4 + 1) * TT],
                                            xn[t % 2][:, kb * P:(kb + 1) * P], k["ident"][0:TT, 0:TT])
                o.then_inc(tr_done, 1)
            pe.wait_ge(xT_lo_ready, NT)

            for m in range(2):
                for h in range(2):
                    for v in range(12):
                        u = 12 * h + v
                        dd, (c0, cn) = v // 3, QK_CH[v % 3]
                        pe.wait_ge(qk_evac, 24 * m + (u + 1))
                        for kb in range(KB):
                            if v == 0 and kb % 2 == 0:
                                pe.wait_ge(w_lo, 8 * m + (4 * h + kb // 2 + 1))
                            w = slice(dd * P, (dd + 1) * P)
                            o = mm3(nc, ring[:, u % 4, 0:cn], (whi[h][:, kb, w], wlo[h][:, kb, w]),
                                    (xT_hi[:, kb, c0:c0 + cn], xT_lo[:, kb, c0:c0 + cn]), kb == 0, kb == KB - 1)
                        o.then_inc(gemm_done, 1)
                if m == 0:
                    pe.wait_ge(tot_ready, 1)
                    nc.tensor.matmul(ps_cnt[0:EP, 0:NB], ones16[:, 0:EP], tot16[:, :], start=True, stop=True)
                    nc.tensor.matmul(ps_base[0:EP, 0:NB], below[:, :], tot16[:, :], start=True, stop=True
                                     ).then_inc(base_ready, 1)
            pe.wait_ge(qk_evac, 48 + 4)

            def table(out, a, b, start=False, stop=False):
                return nc.tensor.matmul(out, a, b, start=start, stop=stop)

            tables = ((ps_src[0:P, 0:NC], P), (ps_dst[0:P, 0:NC], P), (ps_cnt[0:TT, 0:NB], TT))
            pe.wait_ge(w_lo, 16 + 4)
            for o_, n_ in tables:
                table(o_, zero16[:, 0:n_], zero16[:, 0:o_.shape[1]], start=True)
            with pe.Fori(0, 3) as m:
                for h in range(2):
                    for t in range(NT):
                        u = NT * h + t
                        pe.wait_ge(tm_evac, 20 * m + (u + 1))
                        for kb in range(KB):
                            if t == 0 and kb % 2 == 0:
                                pe.wait_ge(w_lo, 8 * m + (16 + 4 * h + kb // 2 + 1))
                            tk = slice(t * TT, (t + 1) * TT)
                            o = mm3(nc, ring[0:TT, u % 4, :], (xT_hi[:, kb, tk], xT_lo[:, kb, tk]),
                                    (whi[h][:, kb, :], wlo[h][:, kb, :]), kb == 0, kb == KB - 1)
                        o.then_inc(gemm_done, 1)
                        pe.wait_ge(job_ready, 20 * m + (u + 1))
                        for jj in range(JU):
                            o = table_products(nc, job[u % 2][:, jj, :], ps_src, ps_dst, ps_cnt)
                        o.then_inc(job_used, 1)
            for o_, n_ in tables:
                o = table(o_, zero16[:, 0:n_], zero16[:, 0:o_.shape[1]], stop=True)
            o.then_inc(table_done, 1)


def phase_attend(nc, mem, io, k):
    mem.cursor = 0
    CH, G, NCK = P, 16, NPAD // P
    feat = [[mem.next(f"a_feat{s}{j}", [P, 2, CH, NH], F32) for j in range(2)] for s in range(2)]
    qk = [[mem.next(f"a_qk{s}{j}", [P, KB, CH], F32) for j in range(2)] for s in range(2)]
    v2 = [mem.next(f"a_v{s}", [P, G, 2, HD], F32) for s in range(2)]
    msk = [mem.next(f"a_msk{s}", [P, 4, P], F32) for s in range(4)]
    prob = [mem.next(f"a_prob{s}", [P, 4, P], F32) for s in range(4)]
    probT = [mem.next(f"a_probT{s}", [P, 4 * P], F32) for s in range(2)]
    att = [mem.next(f"a_att{s}", [P, KB, CH], F32) for s in range(2)]
    mask = mem.next("a_mask", [P, P], F32)
    rfT = mem.next("a_rfT", [P, M], F32)
    mx = [mem.next(f"a_mx{s}", [P, 4], F32) for s in range(2)]
    sm = [mem.next(f"a_sm{s}", [P, 4], F32) for s in range(2)]
    assert mem.cursor <= 6 * KB * HC * 4 + 2 * KB * N * 4

    with ExitStack() as ctx:
        def sem(name):
            return ctx.enter_context(nc.semaphore("a_" + name))

        ps_f = ctx.enter_context(nc.psum_tensor("a_ps_f", [P, 2, HC], F32))
        ps_s = ctx.enter_context(nc.psum_tensor("a_ps_s", [P, 2, HC], F32))
        ps_t = ctx.enter_context(nc.psum_tensor("a_ps_t", [P, 2, HC], F32))
        ps_o = ctx.enter_context(nc.psum_tensor("a_ps_o", [P, 2, HC], F32))
        landed = [[sem(f"landed{s}{j}") for j in range(4)] for s in range(2)]
        rf_landed, mask_step = sem("rf_landed"), sem("mask_step")
        feat_done, feat_evac = sem("feat_done"), sem("feat_evac")
        s_done, s_read, msk_ready, exp_done, p_ready = (sem(n) for n in
                                                        ("s_done", "s_read", "msk_ready", "exp_done", "p_ready"))
        t_done, t_evac, o_done, o_evac = (sem(n) for n in ("t_done", "t_evac", "o_done", "o_evac"))
        att_stored = [sem(f"att_stored{s}") for s in range(2)]
        att_free = sem("att_free")
        dve_step = sem("dve_step")
        block = ctx.enter_context(nc.Block())

        qk_rows = [io["qkT"][j * D:(j + 1) * D, :].rearrange("(b p) t -> p b t", p=P) for j in range(2)]
        v_rows = io["tm"][0:NPAD, :].rearrange("t (h d) -> (t h) d", d=HD)
        att_rows = io["attnT"].rearrange("(b p) t -> p b t", p=P)

        def load_qk(sp, s, c):
            for j in range(2):
                sp.dma_start(qk[s][j][:, :, :], qk_rows[j][:, :, bass.ds(c * CH, CH)]).then_inc(landed[s][j], 16)

        def load_v(sp, s, c):
            for j in range(2):
                sp.dma_start(v2[s][:, :, j, :], v_rows[bass.ds(c * CH * NH, CH * NH), :]
                             .rearrange("(g p) d -> p g d", p=P)).then_inc(landed[s][2 + j], 16)

        @block.sync
        def _(sp):
            for j in range(2):
                sp.dma_start(rfT[j * HD:(j + 1) * HD, :], io["rfT"]).then_inc(rf_landed, 16)
            for s in range(2):
                load_qk(sp, s, s)
                load_v(sp, s, s)

            def chunk(i, s, last):
                if not last:
                    sp.wait_ge(feat_done, 32 * i + (16 * s + 16))
                    load_qk(sp, s, 2 * i + (s + 2))
                    sp.wait_ge(o_done, 8 * i + (4 * s + 4 + 2))
                    load_v(sp, s, 2 * i + (s + 2))
                sp.wait_ge(o_evac, 8 * i + (4 * s + 4 + 2))
                sp.dma_start(att_rows[:, :, bass.ds((2 * i + s) * CH, CH)], att[s][:, :, :]
                             ).then_inc(att_stored[s], 16)
                sp.wait_ge(att_stored[s], 16 * i + 16)
                sp.sem_inc(att_free, 1)

            with sp.Fori(0, NCK // 2 - 1) as i:
                for s in range(2):
                    chunk(i, s, False)
            for s in range(2):
                chunk(NCK // 2 - 1, s, True)

        @block.gpsimd
        def _(pool):
            pool.memset(mask[:, :], 0.0).then_inc(mask_step, 1)
            pool.wait_ge(mask_step, 1)
            mv_ = mask[:, :].rearrange("p (b h) -> p b h", h=NH)
            pool.affine_select(out=mv_, in_=mv_, compare_op=ALU.is_ge, fill=NEG, base=0,
                               pattern=[[-NH, 8], [0, NH]], channel_multiplier=1).then_inc(mask_step, 1)
            pool.wait_ge(mask_step, 2)
            pool.affine_select(out=mv_, in_=mv_, compare_op=ALU.is_ge, fill=NEG, base=NH - 1,
                               pattern=[[NH, 8], [0, NH]], channel_multiplier=-1).then_inc(mask_step, 1)

        UNITS = [(j, mh, par, kg) for j in range(2) for mh in range(2) for kg in range(2) for par in range(2)]

        @block.scalar
        def _(act):
            act.sem_inc(feat_evac, 2)
            act.sem_inc(t_evac, 2)
            act.sem_inc(exp_done, 4)

            def features(i, s):
                for f, (j, mh, par, kg) in enumerate(UNITS):
                    act.wait_ge(feat_done, 32 * i + (16 * s + f + 1))
                    out = feat[s][j][:, :, :, :].rearrange("p m t (g i r) -> p m g r i t", g=2, r=2)[:, mh, kg, par, :, :]
                    act.activation(out, ps_f[:, f % 2, :].rearrange("p (i t) -> p i t", i=4), ACT.Relu
                                   ).then_inc(feat_evac, 1)

            def chunk(i, s, last):
                for b in range(4):
                    act.wait_ge(msk_ready, 8 * i + (4 * s + b + 1))
                    act.wait_ge(t_done, 8 * i + (4 * s + b + 1))
                    act.activation(prob[b][:, :, :], msk[b][:, :, :], ACT.Exp, scale=HD ** -0.5
                                   ).then_inc(exp_done, 1)
                if not last:
                    features(i + s, 1 - s)
                for b in range(4):
                    act.wait_ge(t_done, 8 * i + (4 * s + b + 1 + 4))
                    act.wait_ge(o_done, 8 * i + (4 * s + b + 1))
                    act.activation(probT[b % 2][:, :], ps_t[:, b % 2, :], ACT.Copy).then_inc(t_evac, 1)

            features(0, 0)
            with act.Fori(0, NCK // 2 - 1) as i:
                for s in range(2):
                    chunk(i, s, False)
            for s in range(2):
                chunk(NCK // 2 - 1, s, s == 1)

        @block.vector
        def _(dve):
            dve.sem_inc(s_read, 2)
            dve.sem_inc(o_evac, 2)
            dve.wait_ge(mask_step, 3)

            def chunk(i, s):
                ch = Chain(dve, dve_step, base=(i * 2 + s) * 12)

                def shift(b):
                    dve.wait_ge(s_done, 8 * i + (4 * s + b + 1))
                    dve.wait_ge(exp_done, 8 * i + (4 * s + b + 1))
                    dve.tensor_tensor(msk[b][:, :, :], ps_s[:, b % 2, :].rearrange("p (g c) -> p g c", g=4),
                                      mask[:, :].unsqueeze(1).to_broadcast([P, 4, P]), ALU.add).then_inc(s_read, 1)
                    dve.wait_ge(s_read, 8 * i + (4 * s + b + 3))
                    ch.link(dve.reduce_max(mx[b % 2][:, :], msk[b][:, :, :], AX.X))
                    dve.tensor_tensor(msk[b][:, :, :], msk[b][:, :, :],
                                      mx[b % 2][:, :].unsqueeze(2).to_broadcast([P, 4, P]), ALU.subtract
                                      ).then_inc(msk_ready, 1)

                def normalise(b):
                    dve.wait_ge(exp_done, 8 * i + (4 * s + b + 1 + 4))
                    ch.link(dve.reduce_sum(sm[b % 2][:, :], prob[b][:, :, :], AX.X))
                    ch.link(dve.reciprocal(sm[b % 2][:, :], sm[b % 2][:, :]))
                    dve.tensor_tensor(prob[b][:, :, :], prob[b][:, :, :],
                                      sm[b % 2][:, :].unsqueeze(2).to_broadcast([P, 4, P]), ALU.mult
                                      ).then_inc(p_ready, 1)

                shift(0)
                shift(1)
                normalise(0)
                shift(2)
                normalise(1)
                shift(3)
                normalise(2)
                normalise(3)
                assert ch.n == 12
                dve.wait_ge(att_free, 2 * i + (s + 1))
                for b in range(4):
                    dve.wait_ge(o_done, 8 * i + (4 * s + b + 3))
                    for r in range(2):
                        src = ps_o[:, b % 2, :].rearrange("p (x a r) -> p r x a", r=2, a=KB)
                        rows = slice(r * HD, (r + 1) * HD)
                        o = dve.tensor_copy(att[s][rows, :, b * 32:(b + 1) * 32].rearrange("p a x -> p x a"),
                                            src[rows, r, :, :])
                    o.then_inc(o_evac, 1)

            dve.sem_inc(att_free, 2)
            with dve.Fori(0, NCK // 2) as i:
                for s in range(2):
                    chunk(i, s)

        @block.tensor
        def _(pe):
            pe.sem_inc(t_done, 4)
            pe.sem_inc(o_done, 2)
            pe.wait_ge(rf_landed, 32)

            def features(i, s):
                for f, (j, mh, par, kg) in enumerate(UNITS):
                    if f % 8 == 0:
                        pe.wait_ge(landed[s][f // 8], 16 * i + 16)
                    pe.wait_ge(feat_evac, 32 * i + (16 * s + f + 1))
                    rows = slice(par * HD, (par + 1) * HD)
                    for n in range(4):
                        o = nc.tensor.matmul(ps_f[:, f % 2, n * CH:(n + 1) * CH], rfT[rows, mh * P:(mh + 1) * P],
                                             qk[s][j][rows, 4 * kg + n, :], start=True, stop=True)
                    o.then_inc(feat_done, 1)

            def chunk(i, s, last):
                pe.wait_ge(feat_evac, 32 * i + (16 * s + 16 + 2))
                for b in range(4):
                    pe.wait_ge(s_read, 8 * i + (4 * s + b + 1))
                    for n in range(4):
                        t0 = (4 * b + n) * 8
                        for mh in range(2):
                            o = nc.tensor.matmul(ps_s[:, b % 2, n * P:(n + 1) * P],
                                                 feat[s][0][:, mh, t0:t0 + 8, :].rearrange("p t h -> p (t h)"),
                                                 feat[s][1][:, mh, t0:t0 + 8, :].rearrange("p t h -> p (t h)"),
                                                 start=(mh == 0), stop=(mh == 1))
                    o.then_inc(s_done, 1)
                if not last:
                    features(i + s, 1 - s)

                def turn(b):
                    pe.wait_ge(p_ready, 8 * i + (4 * s + b + 1))
                    pe.wait_ge(t_evac, 8 * i + (4 * s + b + 1))
                    for n in range(4):
                        o = nc.tensor.transpose(ps_t[:, b % 2, n * P:(n + 1) * P], prob[b][:, n, :],
                                                k["ident"][:, :])
                    o.then_inc(t_done, 1)

                def weigh(b):
                    if b == 0:
                        for j in range(2):
                            pe.wait_ge(landed[s][2 + j], 16 * i + 16)
                    pe.wait_ge(t_evac, 8 * i + (4 * s + b + 3))
                    pe.wait_ge(o_evac, 8 * i + (4 * s + b + 1))
                    for n in range(4):
                        o = nc.tensor.matmul(ps_o[:, b % 2, n * P:(n + 1) * P],
                                             v2[s][:, 4 * b + n, :, :].rearrange("p a d -> p (a d)"),
                                             probT[b % 2][:, n * P:(n + 1) * P], start=True, stop=True)
                    o.then_inc(o_done, 1)

                turn(0)
                for b in range(4):
                    if b < 3:
                        turn(b + 1)
                    weigh(b)

            features(0, 0)
            with pe.Fori(0, NCK // 2 - 1) as i:
                for s in range(2):
                    chunk(i, s, False)
            for s in range(2):
                chunk(NCK // 2 - 1, s, s == 1)

def phase_relate(nc, mem, io, k):
    half = KB * HC * 4
    whi = [mem.at(f"r_whi{s}", [P, KB, HC], F32R, o) for s, o in enumerate((0, 4 * half))]
    wlo = [mem.at(f"r_wlo{s}", [P, KB, HC], F32R, o) for s, o in enumerate((half, 5 * half))]
    raw = [mem.at(f"r_raw{s}", [P, KB, HC], F32, o) for s, o in enumerate((2 * half, 3 * half))]
    mem.cursor = 6 * half
    u = mem.next("r_u", [TT, NT, D], F32)
    sT_hi = [mem.next(f"r_sT_hi{s}", [P, KB * TT], F32R) for s in range(2)]
    sT_lo = [mem.next(f"r_sT_lo{s}", [P, KB * TT], F32R) for s in range(2)]
    rows = [mem.next("r_rows0", [P, CAP, 2 * D], F16)]
    oh = [mem.next(f"r_oh{s}", [P, CAP, TT], F16) for s in range(2)]
    src = [mem.next(f"r_src{s}", [P, CAP], U32) for s in range(2)]
    job = [mem.next(f"r_job{s}", [EP, 704], F16) for s in range(2)]
    zero16 = mem.next("r_zero16", [EP, NC], F16)
    tmp = mem.next("r_tmp", [EP, EJ], F32)
    assert mem.cursor <= k["start"]
    mem.cursor = k["start"] + k["bytes"]
    rows.append(mem.next("r_rows1", [P, CAP, 2 * D], F16))
    NW = NB + 2
    MAXR = -(-EP * EJ // (CAP * P))

    with ExitStack() as ctx:
        def sem(name):
            return ctx.enter_context(nc.semaphore("r_" + name))

        ring = ctx.enter_context(nc.psum_tensor("r_ring", [P, 4, HC], F32))
        ps_a = [ctx.enter_context(nc.psum_tensor(f"r_ps_a{s}", [P, 2, HC], F32)) for s in range(2)]
        w_landed = [sem(f"w_landed{s}") for s in range(2)]
        rows_landed = [sem(f"rows_landed{s}") for s in range(2)]
        u_landed = sem("u_landed")
        w_hi, w_lo = sem("w_hi"), sem("w_lo")
        slots_ready, sums_done, hi_ready, lo_ready = sem("slots_ready"), sem("sums_done"), sem("hi_ready"), sem("lo_ready")
        gemm_done, u_added = sem("gemm_done"), sem("u_added")
        dve_step, job_ready, job_used, table_done, table_read = (
            sem(n) for n in ("dve_step", "job_ready", "job_used", "table_done", "table_read"))
        waited = sem("waited")
        block = ctx.enter_context(nc.Block())
        w_rows = io["w"].rearrange("s p b n -> (s p) (b n)")

        def rounds_of(eng):
            return eng.value_load(k["rounds"][0:1, 0:1], min_val=1, max_val=MAXR)

        @block.sync
        def _(sp):
            sp.dma_start(u[:, :, :], io["tm"][NPAD:NPAD + N, :].rearrange("(t p) d -> p t d", p=TT)
                         ).then_inc(u_landed, 16)

            def load(r, h):
                sp.dma_start(raw[h][:, :, :].rearrange("p b n -> p (b n)"),
                             w_rows[bass.ds((STEP_REL + h) * P + r * 2 * P, P), :]).then_inc(w_landed[h], 16)

            for h in range(2):
                load(0, h)
            n = rounds_of(sp)
            with sp.Fori(0, n) as rd:
                with sp.Fori(0, R - 1) as r:
                    for h in range(2):
                        sp.wait_ge(w_lo, 64 * rd + 8 * r + (4 * h + 4))
                        load(r + 1, h)
                for h in range(2):
                    sp.wait_ge(w_lo, 64 * rd + (8 * (R - 1) + 4 * h + 4))
                    load(0, h)
            for h in range(2):
                sp.wait_ge(w_landed[h], 16 * R * n + 16)
                sp.sem_inc(waited, 1)

        @block.gpsimd
        def _(pool):
            n = rounds_of(pool)

            def gather(a, slot):
                pool.wait_ge(slots_ready, a + 1)
                pool.sem_inc(waited, 1)
                for c in range(CAP):
                    pool.indirect_dma_start(out=rows[slot][:, c, :], out_offset=None, in_=io["rows"],
                                            in_offset=bass.IndirectOffsetOnAxis(src[slot][:, c:c + 1], 0)
                                            ).then_inc(rows_landed[slot], 16)

            with pool.Fori(0, n) as rd:
                with pool.Fori(0, NW // 2) as i:
                    for s in range(2):
                        gather(NW * rd + 2 * i + s, s)

        @block.scalar
        def _(act):
            act.sem_inc(sums_done, 2)
            n = rounds_of(act)

            def high(a, g, slot):
                act.wait_ge(sums_done, a + 3)
                act.wait_ge(lo_ready, a + 1)
                act.wait_ge(gemm_done, g + 1)
                act.activation(sT_hi[slot][:, :].rearrange("p (b x) -> p b x", b=2), ps_a[slot][:, :, 0:4 * TT],
                               ACT.Copy, scale=1 / XS).then_inc(hi_ready, 1)

            with act.Fori(0, n) as rd:
                high(NW * rd, NB * rd, 0)
                with act.Fori(0, R) as r:
                    act.wait_ge(gemm_done, NB * rd + NT * r + 2)
                    for h in range(2):
                        act.wait_ge(w_landed[h], 128 * rd + 16 * r + 16)
                        for c in range(4):
                            act.activation(whi[h][:, 2 * c:2 * c + 2, :], raw[h][:, 2 * c:2 * c + 2, :], ACT.Copy
                                           ).then_inc(w_hi, 1)
                    for w in range(NT):
                        high(NW * rd + NT * r + (w + 1), NB * rd + NT * r + (w + 1), (w + 1) % 2)
                high(NW * rd + (NB + 1), NB * rd + (NB + 1), 1)

        @block.vector
        def _(dve):
            dve.sem_inc(lo_ready, 2)
            dve.sem_inc(u_added, 2)
            dve.memset(zero16[:, :], 0.0).then_inc(table_read, 1)
            n = rounds_of(dve)
            dve.wait_ge(u_landed, 16)

            def slots(a, col, slot):
                dve.wait_ge(sums_done, a + 1)
                for c in range(CAP):
                    dve.tensor_scalar(oh[slot][:, c, :], k["iota16"][:, 0:TT], k["slot_dst"][:, bass.ds(col + c, 1)],
                                      None, ALU.is_equal)
                dve.tensor_scalar(src[slot][:, :], k["slot_src"][:, bass.ds(col, CAP)], 0.0, None, ALU.add
                                  ).then_inc(slots_ready, 1)

            def low(a, slot):
                dve.wait_ge(hi_ready, a + 1)
                dve.scalar_tensor_tensor(sT_lo[slot][:, :].rearrange("p (b x) -> p b x", b=2),
                                         ps_a[slot][:, :, 0:4 * TT], 1 / XS,
                                         sT_hi[slot][:, :].bitcast(F32).rearrange("p (b x) -> p b x", b=2),
                                         ALU.mult, ALU.subtract).then_inc(lo_ready, 1)

            with dve.Fori(0, n) as rd:
                for a in range(2):
                    slots(NW * rd + a, CAP * a, a)
                low(NW * rd, 0)
                with dve.Fori(0, R) as r:
                    for w in range(NT):
                        slots(NW * rd + NT * r + (w + 2), CAP * NT * r + CAP * (w + 2), w % 2)
                        if w == 0:
                            for h in range(2):
                                for c in range(4):
                                    dve.wait_ge(w_hi, 64 * rd + 8 * r + (4 * h + c + 1))
                                    dve.tensor_tensor(wlo[h][:, 2 * c:2 * c + 2, :], raw[h][:, 2 * c:2 * c + 2, :],
                                                      whi[h][:, 2 * c:2 * c + 2, :].bitcast(F32), ALU.subtract
                                                      ).then_inc(w_lo, 1)
                        low(NW * rd + NT * r + (w + 1), (w + 1) % 2)
                        dve.wait_ge(gemm_done, NB * rd + NT * r + (w + 3))
                        b = 2 * (w % 2)
                        dve.scalar_tensor_tensor(u[:, w, :].rearrange("p (b x) -> p b x", b=2), ring[0:TT, b:b + 2, :],
                                                 k["rc"][:, bass.ds(NT * r + w, 1)],
                                                 u[:, w, :].rearrange("p (b x) -> p b x", b=2), ALU.mult, ALU.add
                                                 ).then_inc(u_added, 1)
                low(NW * rd + (NB + 1), 1)
                with dve.If(rd < n - 1):
                    ch = Chain(dve, dve_step, base=(4 + CAP - 2) * rd)
                    dve.wait_ge(sums_done, NW * rd + (NW + 2))
                    dve.wait_ge(lo_ready, NW * rd + (NW + 2))
                    ch.link(dve.tensor_scalar(k["rank"][:, :], k["rank"][:, :], float(-CAP * P), None, ALU.add))
                    slot_of_rank(dve, ch, k, tmp)
                    assert ch.n == 4 + CAP - 2
                    dve.sem_inc(waited, 1)
                    with dve.Fori(0, EJ // 2) as j:
                        for s in range(2):
                            dve.wait_ge(job_used, EJ * rd + 2 * j + (s + 1))
                            one_hots(dve, k, job[s][:, :], 2 * j + s).then_inc(job_ready, 1)
                    dve.wait_ge(table_done, rd + 1)
                    read_table(dve, k, ps_a[0][:, 0, :], ps_a[0][:, 1, :]).then_inc(table_read, 1)
                    dve.wait_ge(table_read, rd + 2)
                    dve.sem_inc(waited, 1)

        @block.tensor
        def _(pe):
            pe.sem_inc(gemm_done, 2)
            pe.sem_inc(job_used, 2)
            n = rounds_of(pe)
            pe.wait_ge(table_read, 1)

            def sums(a, landed, slot):
                pe.wait_ge(rows_landed[slot], landed)
                pe.wait_ge(slots_ready, a + 1)
                pe.wait_ge(lo_ready, a + 1)
                for kb in range(KB):
                    for c in range(CAP):
                        for part in range(2):
                            o = nc.tensor.matmul(ps_a[slot][:, kb // 4, (kb % 4) * TT:(kb % 4 + 1) * TT],
                                                 rows[slot][:, c, part * D + kb * P:part * D + (kb + 1) * P],
                                                 oh[slot][:, c, :], start=(c == 0 and part == 0),
                                                 stop=(c == CAP - 1 and part == 1))
                o.then_inc(sums_done, 1)

            LAND = 16 * CAP
            with pe.Fori(0, n) as rd:
                sums(NW * rd, LAND * (NW // 2) * rd + LAND, 0)
                with pe.Fori(0, R) as r:
                    for w in range(NT):
                        sums(NW * rd + NT * r + (w + 1),
                             LAND * (NW // 2) * rd + LAND * (NT // 2) * r + LAND * ((w + 1) // 2 + 1), (w + 1) % 2)
                        pe.wait_ge(lo_ready, NW * rd + NT * r + (w + 3))
                        pe.wait_ge(u_added, NB * rd + NT * r + (w + 1))
                        for h in range(2):
                            for kb in range(KB):
                                if w == 0 and kb % 2 == 0:
                                    pe.wait_ge(w_lo, 64 * rd + 8 * r + (4 * h + kb // 2 + 1))
                                tk = slice(kb * TT, (kb + 1) * TT)
                                o = mm3(nc, ring[0:TT, 2 * (w % 2) + h, :], (sT_hi[w % 2][:, tk], sT_lo[w % 2][:, tk]),
                                        (whi[h][:, kb, :], wlo[h][:, kb, :]), kb == 0, kb == KB - 1)
                        o.then_inc(gemm_done, 1)
                sums(NW * rd + (NB + 1), LAND * (NW // 2) * rd + LAND * (NW // 2), 1)
                with pe.If(rd < n - 1):
                    pe.wait_ge(lo_ready, NW * rd + (NW + 2))
                    banks = [ps_a[0][:, s, 0:NC] for s in range(2)]
                    for b in banks:
                        nc.tensor.matmul(b, zero16[:, 0:P], zero16[:, :], start=True, stop=False)
                    with pe.Fori(0, EJ // 2) as j:
                        for s in range(2):
                            pe.wait_ge(job_ready, EJ * rd + 2 * j + (s + 1))
                            table_products(nc, job[s][:, :], ps_a[0][:, 0, :], ps_a[0][:, 1, :], None
                                           ).then_inc(job_used, 1)
                    for b in banks:
                        o = nc.tensor.matmul(b, zero16[:, 0:P], zero16[:, :], start=False, stop=True)
                    o.then_inc(table_done, 1)
                    pe.wait_ge(table_read, rd + 2)
    return u


def phase_update(nc, mem, io, k):
    half = KB * HC * 4
    whi = [mem.at(f"g_whi{s}", [P, KB, HC], F32R, o) for s, o in enumerate((0, 4 * half))]
    wlo = [mem.at(f"g_wlo{s}", [P, KB, HC], F32R, o) for s, o in enumerate((half, 5 * half))]
    raw = [mem.at(f"g_raw{s}", [P, KB, HC], F32, o) for s, o in enumerate((2 * half, 3 * half))]
    u = k["u"]
    mem.cursor = 6 * half + 4 * NT * D
    aT_hi = [mem.next(f"g_aT_hi{s}", [P, KB * TT], F32R) for s in range(2)]
    aT_lo = [mem.next(f"g_aT_lo{s}", [P, KB * TT], F32R) for s in range(2)]
    attn = [mem.at(f"g_attn{s}", [P, KB, TT], F32, mem.cursor + s * 4 * D) for s in range(2)]
    row = [mem.next(f"g_row{s}", [TT, D], F32) for s in range(2)]
    th = [mem.next(f"g_th{s}", [TT, D], F32) for s in range(2)]
    assert mem.cursor <= k["start"]
    mem.cursor = k["start"] + k["bytes"]
    xn_t, z0_t, xx_t = ([mem.next(f"g_{n}{s}", [TT, D], F32) for s in range(2)] for n in ("xn", "z0", "xx"))
    stats = mem.at("g_stats", [TT, NT, 2, 6], F32, k["start"] + k["bytes"])
    std = mem.at("g_std", [TT, NT], F32, k["start"] + k["bytes"] + 512)
    eps = mem.at("g_eps", [TT, 1], F32, k["start"] + k["bytes"] + 576)
    mv, rstd = k["mv"], k["rstd"]

    with ExitStack() as ctx:
        def sem(name):
            return ctx.enter_context(nc.semaphore("g_" + name))

        ring = ctx.enter_context(nc.psum_tensor("g_ring", [P, 4, HC], F32))
        ps_t = [ctx.enter_context(nc.psum_tensor(f"g_ps_t{s}", [P, 2, HC], F32)) for s in range(2)]
        w_landed = [sem(f"w_landed{s}") for s in range(2)]
        t_landed = [[sem(f"t_landed{s}{j}") for j in range(3)] for s in range(2)]
        a_landed = [sem(f"a_landed{s}") for s in range(2)]
        w_hi, w_lo = sem("w_hi"), sem("w_lo")
        row_ready, turned, hi_ready, lo_ready = sem("row_ready"), sem("turned"), sem("hi_ready"), sem("lo_ready")
        gemm_done, ring_read, tanh_ready, tiles_used = (sem(n) for n in ("gemm_done", "ring_read", "tanh_ready", "tiles_used"))
        x2_ready, var_ready, std_ready = sem("x2_ready"), sem("var_ready"), sem("std_ready")
        x2_stored, dve_step = sem("x2_stored"), sem("dve_step")
        block = ctx.enter_context(nc.Block())

        @block.sync
        def _(sp):
            for h in range(2):
                sp.dma_start(raw[h][:, :, :], io["w"][STEP_GATE + h]).then_inc(w_landed[h], 16)
            for t in range(NT):
                if t >= 2:
                    sp.wait_ge(tiles_used, t - 1)
                rows = slice(t * TT, (t + 1) * TT)
                for j, (dst, src) in enumerate(((xn_t, io["xn"][rows, :]), (xx_t, io["xx"][rows, :]),
                                                (z0_t, io["tm"][2 * NPAD + t * TT:2 * NPAD + (t + 1) * TT, :]))):
                    sp.dma_start(dst[t % 2][:, :], src).then_inc(t_landed[t % 2][j], 16)
                if t == 0:
                    for h in range(2):
                        sp.wait_ge(w_lo, 4 * h + 4)
                        sp.dma_start(raw[h][:, :, :], io["w"][STEP_WO + h]).then_inc(w_landed[h], 16)

        @block.gpsimd
        def _(pool):
            for t in range(NT):
                if t >= 2:
                    pool.wait_ge(turned, t - 1)
                pool.tensor_copy(row[t % 2][:, :], u[:, t, :]).then_inc(row_ready, 1)
            for t in range(NT):
                if t < 2:
                    pool.wait_ge(turned, NT)
                    pool.wait_ge(tanh_ready, NT)
                    pool.wait_ge(tiles_used, NT)
                else:
                    pool.wait_ge(lo_ready, NT + t - 1)
                pool.dma_start(attn[t % 2][:, :, :], io["attnT"][:, t * TT:(t + 1) * TT]
                               .rearrange("(b p) t -> p b t", p=P)).then_inc(a_landed[t % 2], 16)
            for t in range(NT):
                pool.wait_ge(x2_ready, t + 1)
                pool.dma_start(io["x2"][t * TT:(t + 1) * TT, :], u[:, t, :]).then_inc(x2_stored, 16)
            pool.wait_ge(x2_stored, 16 * NT)

        def split_w_hi(act, m, h):
            act.wait_ge(w_landed[h], 16 * (m + 1))
            for c in range(4):
                act.activation(whi[h][:, 2 * c:2 * c + 2, :], raw[h][:, 2 * c:2 * c + 2, :], ACT.Copy).then_inc(w_hi, 1)

        def split_w_lo(dve, m, h):
            for c in range(4):
                dve.wait_ge(w_hi, 8 * m + 4 * h + c + 1)
                dve.tensor_tensor(wlo[h][:, 2 * c:2 * c + 2, :], raw[h][:, 2 * c:2 * c + 2, :],
                                  whi[h][:, 2 * c:2 * c + 2, :].bitcast(F32), ALU.subtract).then_inc(w_lo, 1)

        @block.scalar
        def _(act):
            for h in range(2):
                split_w_hi(act, 0, h)
            for t in range(NT):
                act.wait_ge(turned, t + 1)
                if t >= 2:
                    act.wait_ge(gemm_done, t - 1)
                act.activation(aT_hi[t % 2][:, :].rearrange("p (b x) -> p b x", b=2), ps_t[t % 2][:, :, 0:4 * TT],
                               ACT.Copy).then_inc(hi_ready, 1)
                if t >= 2:
                    act.wait_ge(tiles_used, t - 1)
                act.activation(th[t % 2][:, :], u[:, t, :], ACT.Tanh).then_inc(tanh_ready, 1)
            act.wait_ge(gemm_done, NT)
            for h in range(2):
                split_w_hi(act, 1, h)
            for t in range(NT):
                act.wait_ge(a_landed[t % 2], 16 * (t // 2 + 1))
                if t >= 2:
                    act.wait_ge(gemm_done, NT + t - 1)
                act.activation(aT_hi[t % 2][:, :], attn[t % 2][:, :, :].rearrange("p b t -> p (b t)"), ACT.Copy
                               ).then_inc(hi_ready, 1)
            act.wait_ge(var_ready, 1)
            act.activation(std[:, :], mv[:, :, 1], ACT.Sqrt, bias=eps[:, :]).then_inc(std_ready, 1)

        @block.vector
        def _(dve):
            ch = Chain(dve, dve_step)
            for h in range(2):
                split_w_lo(dve, 0, h)

            def low(t):
                dve.wait_ge(hi_ready, t + 1)
                dve.tensor_tensor(aT_lo[t % 2][:, :].rearrange("p (b x) -> p b x", b=2), ps_t[t % 2][:, :, 0:4 * TT],
                                  aT_hi[t % 2][:, :].bitcast(F32).rearrange("p (b x) -> p b x", b=2), ALU.subtract
                                  ).then_inc(lo_ready, 1)

            low(0)
            for t in range(NT):
                if t + 1 < NT:
                    low(t + 1)
                for j in range(3):
                    dve.wait_ge(t_landed[t % 2][j], 16 * (t // 2 + 1))
                dve.wait_ge(tanh_ready, t + 1)
                ch.add(dve.tensor_tensor(th[t % 2][:, :], th[t % 2][:, :], xn_t[t % 2][:, :], ALU.subtract))
                dve.wait_ge(gemm_done, t + 1)
                z = z0_t[t % 2][:, :].rearrange("p (b x) -> p b x", b=2)
                dve.tensor_tensor(z, ring[0:TT, 2 * (t % 2):2 * (t % 2) + 2, :], z, ALU.add).then_inc(ring_read, 1)
                dve.wait_ge(ring_read, t + 1)
                ch.link(dve.tensor_tensor(th[t % 2][:, :], th[t % 2][:, :], z0_t[t % 2][:, :], ALU.mult))
                dve.tensor_tensor(u[:, t, :], th[t % 2][:, :], xx_t[t % 2][:, :], ALU.add).then_inc(tiles_used, 1)
            for h in range(2):
                split_w_lo(dve, 1, h)

            def low_attn(t):
                dve.wait_ge(hi_ready, NT + t + 1)
                dve.tensor_tensor(aT_lo[t % 2][:, :], attn[t % 2][:, :, :].rearrange("p b t -> p (b t)"),
                                  aT_hi[t % 2][:, :].bitcast(F32), ALU.subtract).then_inc(lo_ready, 1)

            dve.wait_ge(tiles_used, NT)
            ch.link(dve.memset(eps[:, :], EPS))
            low_attn(0)
            for t in range(NT):
                if t + 1 < NT:
                    low_attn(t + 1)
                dve.wait_ge(gemm_done, NT + t + 1)
                ut = u[:, t, :].rearrange("p (b x) -> p b x", b=2)
                dve.tensor_tensor(ut, ring[0:TT, 2 * (t % 2):2 * (t % 2) + 2, :], ut, ALU.add).then_inc(x2_ready, 1)
                dve.wait_ge(x2_ready, t + 1)
                for h in range(2):
                    ch.add(dve.bn_stats(stats[:, t, h, :], u[:, t, h * HC:(h + 1) * HC]))
            ch.wait()
            for t in range(NT):
                o = dve.bn_aggr(mv[:, t, :], stats[:, t, :, :].rearrange("p a b -> p (a b)"))
            o.then_inc(var_ready, 1)
            dve.wait_ge(std_ready, 1)
            inverse_root(dve, ch, rstd, std, mv[:, :, 1], EPS)

        @block.tensor
        def _(pe):
            def turn(t):
                pe.wait_ge(row_ready, t + 1)
                if t >= 2:
                    pe.wait_ge(lo_ready, t - 1)
                for kb in range(KB):
                    o = nc.tensor.transpose(ps_t[t % 2][:, kb // 4, (kb % 4) * TT:(kb % 4 + 1) * TT],
                                            row[t % 2][:, kb * P:(kb + 1) * P], k["ident"][0:TT, 0:TT])
                o.then_inc(turned, 1)

            def gemm(t, m):
                pe.wait_ge(lo_ready, NT * m + t + 1)
                if NT * m + t >= 2:
                    if m == 0:
                        pe.wait_ge(ring_read, t - 1)
                    elif t < 2:
                        pe.wait_ge(ring_read, NT + t - 1)
                    else:
                        pe.wait_ge(x2_ready, t - 1)
                for h in range(2):
                    for kb in range(KB):
                        if t == 0 and kb % 2 == 0:
                            pe.wait_ge(w_lo, 8 * m + 4 * h + kb // 2 + 1)
                        tk = slice(kb * TT, (kb + 1) * TT)
                        o = mm3(nc, ring[0:TT, 2 * (t % 2) + h, :], (aT_hi[t % 2][:, tk], aT_lo[t % 2][:, tk]),
                                (whi[h][:, kb, :], wlo[h][:, kb, :]), kb == 0, kb == KB - 1)
                o.then_inc(gemm_done, 1)

            turn(0)
            for t in range(NT):
                if t + 1 < NT:
                    turn(t + 1)
                gemm(t, 0)
            for t in range(NT):
                gemm(t, 1)


def phase_ffn(nc, mem, io, k):
    half = KB * HC * 4
    whi = [mem.at(f"f_whi{s}", [P, KB, HC], F32R, o) for s, o in enumerate((0, 4 * half))]
    wlo = [mem.at(f"f_wlo{s}", [P, KB, HC], F32R, o) for s, o in enumerate((half, 5 * half))]
    raw = mem.at("f_raw", [P, KB, HC], F32, 2 * half)
    mem.cursor = 3 * half
    y = [mem.next(f"f_y{s}", [TT, D], F32) for s in range(2)]
    pre = [mem.next(f"f_pre{s}", [TT, HC], F32) for s in range(4)]
    mem.cursor = 6 * half
    yT_hi = mem.next("f_yT_hi", [P, KB, N], F32R)
    yT_lo = mem.next("f_yT_lo", [P, KB, N], F32R)
    mem.cursor = k["start"] + k["bytes"]
    cell = mem.next("f_cell", [TT, NT, HC], F32)
    x2h = [mem.next(f"f_x2h{s}", [TT, HC], F32) for s in range(2)]
    bias = [mem.at(f"f_bias{s}", [TT, HC], F32, k["edges_at"] + s * HC * 4) for s in range(2)]
    mv, rstd = k["mv"], k["rstd"]
    STEPS = 6

    with ExitStack() as ctx:
        def sem(name):
            return ctx.enter_context(nc.semaphore("f_" + name))

        ring = ctx.enter_context(nc.psum_tensor("f_ring", [P, 4, HC], F32))
        ps_t = [ctx.enter_context(nc.psum_tensor(f"f_ps_t{s}", [P, 2, HC], F32)) for s in range(2)]
        w_landed, bias_landed, x2_landed = sem("w_landed"), [sem(f"bias_landed{s}") for s in range(2)], [
            sem(f"x2_landed{s}") for s in range(2)]
        h_landed = [sem(f"h_landed{s}") for s in range(2)]
        w_hi, w_lo = sem("w_hi"), sem("w_lo")
        y_ready, turned, hi_ready, lo_ready = sem("y_ready"), sem("turned"), sem("hi_ready"), sem("lo_ready")
        gemm_done, pre_ready, gate_ready, cell_ready, out_ready = (
            sem(n) for n in ("gemm_done", "pre_ready", "gate_ready", "cell_ready", "out_ready"))
        act_step, dve_step = sem("act_step"), sem("dve_step")
        out_stored = [sem(f"out_stored{s}") for s in range(4)]
        block = ctx.enter_context(nc.Block())

        @block.sync
        def _(sp):
            def load(q):
                if q >= 1:
                    sp.wait_ge(w_lo, 4 * q)
                sp.dma_start(raw[:, :, :], io["w"][STEP_LSTM + q]).then_inc(w_landed, 16)
                if q >= 2:
                    sp.wait_ge(pre_ready, NT * (q - 1))
                sp.dma_start(bias[q % 2][:, :], io["bias_lstm"][q:q + 1, :].to_broadcast([TT, HC])
                             ).then_inc(bias_landed[q % 2], 16)

            load(0)
            for t in range(NT):
                if t == 2:
                    load(1)
                if t >= 2:
                    sp.wait_ge(turned, t - 1)
                sp.dma_start(y[t % 2][:, :], io["x2"][t * TT:(t + 1) * TT, :]).then_inc(x2_landed[t % 2], 16)
            for q in range(2, STEPS):
                load(q)

        def slot_of(v):
            return (NT * (3 * (v // NT) + 2) + v % NT) % 4

        def stores_before(v):
            return sum(1 for w in range(v) if slot_of(w) == slot_of(v))

        def store(pool, v):
            c, t = divmod(v, NT)
            pool.wait_ge(out_ready, v + 1)
            pool.dma_start(io["out"][t * TT:(t + 1) * TT, c * HC:(c + 1) * HC], pre[slot_of(v)][:, :]
                           ).then_inc(out_stored[slot_of(v)], 16)

        @block.gpsimd
        def _(pool):
            for c in range(2):
                for t in range(NT):
                    v = NT * c + t
                    if v >= 2:
                        pool.wait_ge(out_ready, v - 1)
                    pool.dma_start(x2h[t % 2][:, :], io["x2"][t * TT:(t + 1) * TT, c * HC:(c + 1) * HC]
                                   ).then_inc(h_landed[t % 2], 16)
                    if v >= 1:
                        store(pool, v - 1)
            store(pool, 2 * NT - 1)
            for s in range(4):
                pool.wait_ge(out_stored[s], 16 * sum(1 for v in range(2 * NT) if slot_of(v) == s))

        def split_w_hi(act, q):
            act.wait_ge(w_landed, 16 * (q + 1))
            if q >= 2:
                act.wait_ge(gemm_done, NT * (q - 1))
            for c in range(4):
                act.activation(whi[q % 2][:, 2 * c:2 * c + 2, :], raw[:, 2 * c:2 * c + 2, :], ACT.Copy).then_inc(w_hi, 1)

        def split_w_lo(dve, q):
            for c in range(4):
                dve.wait_ge(w_hi, 4 * q + c + 1)
                dve.tensor_tensor(wlo[q % 2][:, 2 * c:2 * c + 2, :], raw[:, 2 * c:2 * c + 2, :],
                                  whi[q % 2][:, 2 * c:2 * c + 2, :].bitcast(F32), ALU.subtract).then_inc(w_lo, 1)

        @block.scalar
        def _(act):
            split_w_hi(act, 0)

            def high(t):
                act.wait_ge(turned, t + 1)
                act.activation(yT_hi[:, :, t * TT:(t + 1) * TT].rearrange("p (b k) t -> p b k t", b=2),
                               ps_t[t % 2][:, :, 0:4 * TT].rearrange("p b (k t) -> p b k t", t=TT), ACT.Copy
                               ).then_inc(hi_ready, 1)

            high(0)
            for q in range(STEPS):
                c, gate = divmod(q, 3)
                for t in range(NT):
                    n = NT * q + t
                    if n + 1 < NT:
                        high(n + 1)
                    if n == 2:
                        split_w_hi(act, 1)
                    if gate == 2:
                        act.wait_ge(cell_ready, NT * c + t + 1)
                        act.activation(cell[:, t, :], cell[:, t, :], ACT.Tanh).then_inc(act_step, 1)
                    act.wait_ge(pre_ready, n + 1)
                    if gate == 0 and c == 1:
                        act.wait_ge(out_ready, t + 1)
                    act.activation(cell[:, t, :] if gate == 0 else pre[n % 4][:, :], pre[n % 4][:, :],
                                   ACT.Tanh if gate == 1 else ACT.Sigmoid).then_inc(gate_ready, 1)
                if q + 2 < STEPS:
                    split_w_hi(act, q + 2)

        @block.vector
        def _(dve):
            ch = Chain(dve, dve_step)
            split_w_lo(dve, 0)

            def normalise(t):
                dve.wait_ge(x2_landed[t % 2], 16 * (t // 2 + 1))
                dve.tensor_scalar(y[t % 2][:, :], y[t % 2][:, :], mv[:, t, 0:1], rstd[:, t:t + 1],
                                  ALU.subtract, ALU.mult).then_inc(y_ready, 1)

            def low(t):
                dve.wait_ge(hi_ready, t + 1)
                sl = slice(t * TT, (t + 1) * TT)
                dve.tensor_tensor(yT_lo[:, :, sl].rearrange("p (b k) t -> p b k t", b=2),
                                  ps_t[t % 2][:, :, 0:4 * TT].rearrange("p b (k t) -> p b k t", t=TT),
                                  yT_hi[:, :, sl].bitcast(F32).rearrange("p (b k) t -> p b k t", b=2), ALU.subtract
                                  ).then_inc(lo_ready, 1)

            def finish(n):
                q, t = divmod(n, NT)
                c, gate = divmod(q, 3)
                dve.wait_ge(gate_ready, n + 1)
                if gate == 1:
                    dve.tensor_tensor(cell[:, t, :], cell[:, t, :], pre[n % 4][:, :], ALU.mult).then_inc(cell_ready, 1)
                elif gate == 2:
                    ch.link(dve.tensor_tensor(pre[n % 4][:, :], pre[n % 4][:, :], cell[:, t, :], ALU.mult))
                    dve.wait_ge(h_landed[t % 2], 16 * (NT // 2 * c + t // 2 + 1))
                    dve.tensor_tensor(pre[n % 4][:, :], pre[n % 4][:, :], x2h[t % 2][:, :], ALU.add
                                      ).then_inc(out_ready, 1)

            def add_bias(n):
                q, t = divmod(n, NT)
                if t == 0:
                    dve.wait_ge(bias_landed[q % 2], 16 * (q // 2 + 1))
                dve.wait_ge(gemm_done, n + 1)
                if n >= 4:
                    before = n - 4
                    qb, tb = divmod(before, NT)
                    cb, gb = divmod(qb, 3)
                    if gb == 0:
                        dve.wait_ge(gate_ready, before + 1)
                    elif gb == 1:
                        dve.wait_ge(cell_ready, NT * cb + tb + 1)
                    else:
                        v = NT * cb + tb
                        dve.wait_ge(out_stored[slot_of(v)], 16 * (stores_before(v) + 1))
                dve.tensor_tensor(pre[n % 4][:, :], ring[0:TT, n % 4, :], bias[q % 2][:, :], ALU.add
                                  ).then_inc(pre_ready, 1)

            normalise(0)
            low(0)
            for n in range(NT * STEPS):
                if n + 1 < NT:
                    normalise(n + 1)
                    low(n + 1)
                if n == 2:
                    split_w_lo(dve, 1)
                add_bias(n)
                if n >= 1:
                    finish(n - 1)
                if n % NT == NT - 1 and n // NT + 2 < STEPS:
                    split_w_lo(dve, n // NT + 2)
            finish(NT * STEPS - 1)

        @block.tensor
        def _(pe):
            def turn(t):
                pe.wait_ge(y_ready, t + 1)
                if t >= 2:
                    pe.wait_ge(lo_ready, t - 1)
                for kb in range(KB):
                    o = nc.tensor.transpose(ps_t[t % 2][:, kb // 4, (kb % 4) * TT:(kb % 4 + 1) * TT],
                                            y[t % 2][:, kb * P:(kb + 1) * P], k["ident"][0:TT, 0:TT])
                o.then_inc(turned, 1)

            turn(0)
            for q in range(STEPS):
                for t in range(NT):
                    if q == 0 and t + 1 < NT:
                        turn(t + 1)
                    n = NT * q + t
                    if q == 0:
                        pe.wait_ge(lo_ready, t + 1)
                    if n >= 4:
                        pe.wait_ge(pre_ready, n - 3)
                    for kb in range(KB):
                        if t == 0 and kb % 2 == 0:
                            pe.wait_ge(w_lo, 4 * q + kb // 2 + 1)
                        tk = slice(t * TT, (t + 1) * TT)
                        o = mm3(nc, ring[0:TT, n % 4, :], (yT_hi[:, kb, tk], yT_lo[:, kb, tk]),
                                (whi[q % 2][:, kb, :], wlo[q % 2][:, kb, :]), kb == 0, kb == KB - 1)
                    o.then_inc(gemm_done, 1)


def inverse_root(dve, ch, out, root, var, eps):
    ch.link(dve.reciprocal(out[:, :], root[:, :]))
    ch.link(dve.tensor_tensor(root[:, :], out[:, :], out[:, :], ALU.mult))
    ch.link(dve.scalar_tensor_tensor(root[:, :], var, eps, root[:, :], ALU.add, ALU.mult))
    ch.link(dve.tensor_scalar(root[:, :], root[:, :], -0.5, 1.5, ALU.mult, ALU.add))
    ch.link(dve.tensor_tensor(out[:, :], out[:, :], root[:, :], ALU.mult))


def slot_of_rank(dve, ch, k, tmp):
    ch.link(dve.tensor_scalar(tmp[:, :], k["rank"][:, :], float(P), None, ALU.is_ge))
    for c in range(2, CAP):
        ch.link(dve.scalar_tensor_tensor(tmp[:, :], k["rank"][:, :], float(c * P), tmp[:, :], ALU.is_ge, ALU.add))
    ch.add(dve.scalar_tensor_tensor(k["lo"][:, :], tmp[:, :], float(-P), k["rank"][:, :], ALU.mult, ALU.add))
    ch.link(dve.scalar_tensor_tensor(k["hi"][:, :], k["bkt"][:, :], float(CAP), tmp[:, :], ALU.mult, ALU.add))


def one_hots(dve, k, out, j):
    i16 = k["iota16"]
    col = {n: k[n][:, bass.ds(j, 1)] for n in ("lo", "hi", "srcf", "dl1", "dl", "bkt")}
    dve.tensor_scalar(out[:, 0:128], i16[0:EP, 0:128], col["lo"], col["srcf"], ALU.is_equal, ALU.mult)
    dve.tensor_scalar(out[:, 128:256], i16[0:EP, 0:128], col["lo"], col["dl1"], ALU.is_equal, ALU.mult)
    dve.tensor_scalar(out[:, 256:256 + NC], i16[0:EP, 0:NC], col["hi"], None, ALU.is_equal)
    dve.tensor_scalar(out[:, 496:496 + TT], i16[0:EP, 0:TT], col["dl"], None, ALU.is_equal)
    return dve.tensor_scalar(out[:, 622:622 + NB], i16[0:EP, 0:NB], col["bkt"], None, ALU.is_equal)


def table_products(nc, j, ps_src, ps_dst, ps_cnt):
    hi = j[:, 256:256 + NC]
    nc.tensor.matmul(ps_src[0:P, 0:NC], j[:, 0:128], hi, start=False, stop=False)
    o = nc.tensor.matmul(ps_dst[0:P, 0:NC], j[:, 128:256], hi, start=False, stop=False)
    if ps_cnt is not None:
        o = nc.tensor.matmul(ps_cnt[0:TT, 0:NB], j[:, 496:496 + TT], j[:, 622:622 + NB], start=False, stop=False)
    return o


def read_table(dve, k, ps_src, ps_dst):
    dve.tensor_copy(k["slot_src"][:, 0:NC], ps_src[:, 0:NC])
    dve.memset(k["slot_src"][:, NC:NC + 2 * CAP], 0.0)
    dve.tensor_scalar(k["slot_dst"][:, 0:NC], ps_dst[:, 0:NC], 1.0, None, ALU.subtract)
    return dve.memset(k["slot_dst"][:, NC:NC + 2 * CAP], -1.0)


def kept_tensors(mem):
    half = KB * HC * 4
    mem.cursor = 6 * half + 2 * KB * N * 4
    start = mem.cursor
    k = {
        "ident": mem.next("ident", [P, P], F32),
        "iota16": mem.next("iota16", [P, 256], F16),
        "slot_src": mem.next("slot_src", [P, NC + 2 * CAP], F32),
        "slot_dst": mem.next("slot_dst", [P, NC + 2 * CAP], F32),
        "rc": mem.next("rc", [TT, NB], F32),
        "rounds": mem.next("rounds", [P, 1], I32),
    }
    k["mv"] = mem.next("mv", [TT, NT, 2], F32)
    k["rstd"] = mem.next("rstd", [TT, NT], F32)
    k["edges_at"] = mem.cursor
    for n in ("srcf", "dl", "dl1", "bkt", "lo", "hi", "rank"):
        k[n] = mem.next("e_" + n, [EP, EJ], F32)
    k["start"], k["bytes"] = start, mem.cursor - start
    return k


def build(nc, io):
    mem = Memory(nc)
    keep = kept_tensors(mem)
    phase_project(nc, mem, io, keep)
    phase_attend(nc, mem, io, keep)
    keep["u"] = phase_relate(nc, mem, io, keep)
    phase_update(nc, mem, io, keep)
    phase_ffn(nc, mem, io, keep)
    return keep


def kernel(**inputs):
    import numpy as _np
    import concourse.bacc as _bacc
    from concourse import mybir as _mybir
    from concourse.bass_utils import run_bass_kernel_spmd as _run

    a = {n: _np.asarray(v) for n, v in inputs.items()}

    def halves(w):
        return w.reshape(KB, P, 2, HC).transpose(2, 1, 0, 3)

    gnn, mix, ffn = "L0_gnn_", "L0_mix_", "L0_ffn_"
    gate = a[gnn + "w_gate"]
    mats = [a[mix + "Wq"], a[mix + "Wk"], a[mix + "Wv"], a[gnn + "root"], gate[D:]]
    mats += [a[gnn + "weight"][r] for r in range(R)] + [gate[:D], a[mix + "Wo"]]
    steps = [s for w in mats for s in halves(w)]
    lstm = [halves(a[ffn + n][:, D:].T) for n in ("W_i", "W_c", "W_o")]
    steps += [w[h] for h in range(2) for w in lstm]
    edges = _np.zeros((3, EP * EJ), _np.int32)
    edges[2] = -1
    for i, n in enumerate(("src", "dst", "edge_type_8")):
        edges[i, :a[n].shape[0]] = a[n]
    host = {
        "x": a["x"],
        "w": _np.ascontiguousarray(_np.stack(steps)),
        "edges": _np.ascontiguousarray(edges.reshape(3, EP, EJ).transpose(1, 0, 2)),
        "bias_qk": _np.ascontiguousarray(_np.stack([a[mix + "bq"], a[mix + "bk"]]).reshape(2, KB, P).transpose(2, 0, 1)),
        "bias_tm": _np.ascontiguousarray(
            _np.stack([a[mix + "bv"], a[gnn + "bias"], a[gnn + "b_gate"]]).reshape(6, HC)),
        "bo": a[mix + "bo"].reshape(1, D),
        "bias_lstm": _np.ascontiguousarray(_np.stack([a[ffn + n] for n in ("b_i", "b_c", "b_o")]).reshape(3, 2, HC)
                                           .transpose(1, 0, 2).reshape(6, HC)),
        "rfT": _np.ascontiguousarray(a[mix + "rf"].T),
    }
    nc = _bacc.Bacc("TRN2", target_bir_lowering=False, num_devices=1)
    io, arrays = {}, {}
    for n, v in host.items():
        arrays["in_" + n] = v
        io[n] = nc.dram_tensor("in_" + n, v.shape, _mybir.dt.from_np(v.dtype), kind="ExternalInput").ap()
    for n, shape, dt in (("qkT", (2 * D, NPAD), F32), ("tm", (3 * NPAD, D), F32), ("rows", (N, 2 * D), F16),
                         ("xn", (N, D), F32), ("xx", (N, D), F32), ("attnT", (D, NPAD), F32), ("x2", (N, D), F32)):
        io[n] = nc.dram_tensor("mid_" + n, shape, dt, kind=MID).ap()
    io["out"] = nc.dram_tensor("out_0_dram", (N, D), F32, kind="ExternalOutput").ap()
    build(nc, io)
    r = _run(nc, [arrays], core_ids=[0])
    return r.results[0]["out_0_dram"]
```

```python
from contextlib import ExitStack

import numpy as np
import concourse.bass as bass
from concourse import mybir

F32 = mybir.dt.float32
F32R = mybir.dt.float32r
F16 = mybir.dt.float16
I32 = mybir.dt.int32
U32 = mybir.dt.uint32
ALU = mybir.AluOpType
ACT = mybir.ActivationFunctionType
AX = mybir.AxisListType

P = 128
N = 1250
D = 1024
R = 8
TT = 125
NT = N // TT
KB = D // P
HC = 512
NPAD = 1280
EP, EJ = 125, 180
NB = R * NT
CAP = 3
NC = NB * CAP
NH, HD, M = 16, 64, 256
EPS = 1e-5
SIZE = {F32: 4, F32R: 4, I32: 4, U32: 4, F16: 2}
MID = "Internal"
XS = 1024.0
NEG = -1e30

STEP_QK, STEP_TM, STEP_REL, STEP_GATE, STEP_WO, STEP_LSTM = 0, 4, 10, 26, 28, 30


def mm3(nc, out, a, b, first, last):
    nc.tensor.matmul(out, a[0], b[0], start=first, stop=False)
    nc.tensor.matmul(out, a[0], b[1], start=False, stop=False)
    return nc.tensor.matmul(out, a[1], b[0], start=False, stop=last)


class Chain:

    def __init__(self, eng, sem, base=0):
        self.eng, self.sem, self.base, self.n = eng, sem, base, 0

    def add(self, ins):
        ins.then_inc(self.sem, 1)
        self.n += 1
        return ins

    def wait(self):
        self.eng.wait_ge(self.sem, self.base + self.n)

    def link(self, ins):
        self.add(ins)
        self.wait()


class Memory:

    def __init__(self, nc):
        self.nc = nc
        self.base = (nc.sbuf_base + 63) // 64 * 64
        self.end = nc.sbuf_usable_end
        self.cursor = 0

    def at(self, name, shape, dt, offset):
        size = int(np.prod(shape[1:])) * SIZE[dt]
        assert self.base + offset + size <= self.end, (name, offset, size, self.end - self.base)
        return self.nc.alloc_sbuf_tensor_at(name, shape, dt, offset=self.base + offset)

    def next(self, name, shape, dt):
        t = self.at(name, shape, dt, self.cursor)
        self.cursor += (int(np.prod(shape[1:])) * SIZE[dt] + 31) // 32 * 32
        return t


def phase_project(nc, mem, io, keep):
    half = KB * HC * 4
    whi = [mem.at(f"p_whi{s}", [P, KB, HC], F32R, o) for s, o in enumerate((0, 4 * half))]
    wlo = [mem.at(f"p_wlo{s}", [P, KB, HC], F32R, o) for s, o in enumerate((half, 5 * half))]
    raw = [mem.at(f"p_raw{s}", [P, KB, HC], F32, o) for s, o in enumerate((2 * half, 3 * half))]
    x_all = mem.at("p_x_all", [TT, NT, D], F32, 3 * half)
    hl = [mem.at(f"p_hl{s}", [TT, 2 * D], F16, 3 * half + NT * D * 4 + s * D * 4) for s in range(2)]
    mem.cursor = 6 * half
    xT_hi = mem.next("p_xT_hi", [P, KB, N], F32R)
    xT_lo = mem.next("p_xT_lo", [P, KB, N], F32R)
    at_small = mem.cursor
    mem.cursor = at_small + keep["bytes"]
    stage = [mem.next(f"p_stage{s}", [P, HC], F32) for s in range(4)]
    at_sort = mem.cursor
    CB = 5
    NCH = NB // CB
    oh_c = mem.next("p_oh_c", [EP, CB, EJ], F16)
    reset = mem.next("p_reset", [EP, CB, EJ], F16)
    scan_c = mem.next("p_scan_c", [EP, CB, EJ], F32)
    edges = mem.next("p_edges", [EP, 3, EJ], I32)
    tot = mem.next("p_tot", [EP, NB], F32)
    tot16 = mem.next("p_tot16", [EP, NB], F16)
    base1 = mem.next("p_base1", [EP, NB], F32)
    below = mem.next("p_below", [EP, EP], F16)
    ones16 = mem.next("p_ones16", [EP, P], F16)
    thr = mem.next("p_thr", [EP, 56], F32)
    after_sort = mem.cursor
    JU, JU0, JW = 4, 15, 704
    assert JU * (6 * NT - JU0) == EJ
    job = [mem.at(f"p_job{s}", [EP, JU, JW], F16, at_sort + s * JU * JW * 2) for s in range(2)]
    mem.cursor = max(after_sort, at_sort + 2 * JU * JW * 2)
    pads = mem.at("p_pads", [P, HC], F32, mem.cursor)
    bias_bc = [mem.next(f"p_bias_bc{s}", [TT, HC], F32) for s in range(2)]
    bias_qk = mem.next("p_bias_qk", [P, 2, KB], F32)
    k = keep
    at_stats = at_sort
    stats = mem.at("p_stats", [TT, NT, 2, 6], F32, at_stats)
    mv = mem.at("p_mv", [TT, NT, 2], F32, at_stats + 512)
    std = mem.at("p_std", [TT, NT], F32, at_stats + 640)
    rstd = mem.at("p_rstd", [TT, NT], F32, at_stats + 704)
    eps = mem.at("p_eps", [TT, 1], F32, at_stats + 768)
    tmp = mem.next("p_tmp", [EP, EJ], F32)
    zero16 = mem.next("p_zero16", [EP, NC], F16)
    mx = mem.next("p_mx", [EP, 2], F32)

    with ExitStack() as ctx:
        def sem(name):
            return ctx.enter_context(nc.semaphore("p_" + name))

        ring = ctx.enter_context(nc.psum_tensor("p_ring", [P, 4, HC], F32))
        ps_t = ctx.enter_context(nc.psum_tensor("p_ps_t", [P, 4, HC], F32))
        ps_src, ps_dst, ps_cnt, ps_base = (ps_t[:, i, :] for i in range(4))
        x_landed = [sem(f"x_landed{i}") for i in range(5)]
        w_landed = [sem(f"w_landed{s}") for s in range(2)]
        bias_landed = [sem(f"bias_landed{s}") for s in range(2)]
        bqk_landed, edges_landed = sem("bqk_landed"), sem("edges_landed")
        consts, pconst = sem("consts"), sem("pconst")
        w_hi, w_lo = sem("w_hi"), sem("w_lo")
        var_ready, std_ready = sem("var_ready"), sem("std_ready")
        xn_ready, h16_ready, l16_ready = sem("xn_ready"), sem("h16_ready"), sem("l16_ready")
        tr_done, xT_hi_ready, xT_lo_ready = sem("tr_done"), sem("xT_hi_ready"), sem("xT_lo_ready")
        xn_stored = sem("xn_stored")
        hl_stored = [sem(f"hl_stored{s}") for s in range(2)]
        gemm_done, qk_evac, tm_evac = sem("gemm_done"), sem("qk_evac"), sem("tm_evac")
        stored = [sem(f"stored{s}") for s in range(4)]
        pad_zero, pad_stored = sem("pad_zero"), sem("pad_stored")
        dve_step = sem("dve_step")
        tot_ready, base_ready, base_read = sem("tot_ready"), sem("base_ready"), sem("base_read")
        job_ready, job_used, table_done = sem("job_ready"), sem("job_used"), sem("table_done")
        block = ctx.enter_context(nc.Block())

        x_rows = io["x"].rearrange("(t p) d -> p t d", p=TT)
        xn_rows = io["xn"].rearrange("(t p) d -> p t d", p=TT)
        QK_CH = [(0, 4 * TT), (4 * TT, 4 * TT), (8 * TT, 2 * TT)]

        def turned(t):
            return ps_t[:, 2 * (t % 2):2 * (t % 2) + 2, 0:4 * TT].rearrange("p b (k t) -> p b k t", t=TT)

        @block.sync
        def _(sp):
            for i in range(NT // 2):
                sp.dma_start(x_all[:, 2 * i:2 * i + 2, :], x_rows[:, 2 * i:2 * i + 2, :]).then_inc(x_landed[i], 16)
                if i == 1:
                    sp.dma_start(raw[0][:, :, :], io["w"][0]).then_inc(w_landed[0], 16)
            for i in range(NT // 2):
                sp.wait_ge(xn_ready, 2 * i + 2)
                sp.dma_start(xn_rows[:, 2 * i:2 * i + 2, :], x_all[:, 2 * i:2 * i + 2, :]).then_inc(xn_stored, 16)
            sp.wait_ge(xn_stored, 16 * NT // 2)
            sp.wait_ge(xT_lo_ready, 4)
            sp.wait_ge(l16_ready, 4)
            for s in range(1, STEP_REL):
                if s >= 2:
                    sp.wait_ge(w_lo, 4 * (s - 1))
                sp.dma_start(raw[s % 2][:, :, :], io["w"][s]).then_inc(w_landed[s % 2], 16)
                if s >= STEP_TM:
                    m = s - STEP_TM
                    if m == 0:
                        sp.wait_ge(pad_stored, 48)
                    if m >= 2:
                        sp.wait_ge(tm_evac, 4 + NT * (m - 1))
                    sp.dma_start(bias_bc[m % 2][:, :], io["bias_tm"][m:m + 1, :].to_broadcast([TT, HC])
                                 ).then_inc(bias_landed[m % 2], 16)

        def split_hi(slot, sem_val):
            nc.scalar.wait_ge(w_landed[slot], sem_val)
            for c in range(4):
                nc.scalar.activation(whi[slot][:, 2 * c:2 * c + 2, :], raw[slot][:, 2 * c:2 * c + 2, :],
                                     ACT.Copy).then_inc(w_hi, 1)

        def split_lo_part(s, slot, c):
            nc.vector.wait_ge(w_hi, 4 * s + (c + 1))
            nc.vector.tensor_tensor(wlo[slot][:, 2 * c:2 * c + 2, :], raw[slot][:, 2 * c:2 * c + 2, :],
                                    whi[slot][:, 2 * c:2 * c + 2, :].bitcast(F32), ALU.subtract
                                    ).then_inc(w_lo, 1)

        def split_lo(s, slot):
            for c in range(4):
                split_lo_part(s, slot, c)

        @block.gpsimd
        def _(pool):
            pool.dma_start(bias_qk[:, :, :], io["bias_qk"]).then_inc(bqk_landed, 16)
            pool.iota(k["iota16"][:, :], [[1, 256]], base=0, channel_multiplier=0,
                      allow_small_or_imprecise_dtypes=True).then_inc(pconst, 1)
            pool.iota(thr[:, :], [[CAP * P, 56]], base=0, channel_multiplier=0,
                      allow_small_or_imprecise_dtypes=True).then_inc(pconst, 1)
            pool.memset(k["ident"][:, :], 0.0).then_inc(pconst, 1)
            pool.memset(below[:, :], 1.0).then_inc(pconst, 1)
            pool.memset(ones16[:, :], 1.0).then_inc(pconst, 1)
            pool.memset(zero16[:, :], 0.0).then_inc(pconst, 1)
            pool.memset(pads[:, :], 0.0).then_inc(pad_zero, 1)
            pool.wait_ge(pconst, 6)
            pool.affine_select(out=k["ident"][:, :], in_=k["ident"][:, :], compare_op=ALU.not_equal, fill=1.0, base=0,
                               pattern=[[-1, P]], channel_multiplier=1).then_inc(consts, 1)
            pool.affine_select(out=below[:, :], in_=below[:, :], compare_op=ALU.is_ge, fill=0.0, base=-1,
                               pattern=[[1, EP]], channel_multiplier=-1).then_inc(consts, 1)
            pool.wait_ge(pad_zero, 1)
            pad = NPAD - N
            pool.dma_start(io["qkT"].rearrange("(b p) t -> p b t", p=P)[:, :, N:NPAD],
                           pads[:, 0:2 * KB * pad].rearrange("p (b t) -> p b t", t=pad)).then_inc(pad_stored, 16)
            for c in range(2):
                pool.dma_start(io["tm"][N:NPAD, c * HC:(c + 1) * HC], pads[0:pad, :]).then_inc(pad_stored, 16)
            for t in range(NT):
                pool.wait_ge(l16_ready, t + 1)
                pool.dma_start(io["rows"][t * TT:(t + 1) * TT, :], hl[t % 2][:, :]).then_inc(hl_stored[t % 2], 16)
            with pool.Fori(0, 2) as m:
                for u in range(24):
                    h, c, dd = u // 12, u % 12 // 4, u % 4
                    c0, cn = QK_CH[c]
                    pool.wait_ge(qk_evac, 24 * m + (u + 5))
                    pool.dma_start(io["qkT"][bass.ds(m * D + (4 * h + dd) * P, P), c0:c0 + cn],
                                   stage[u % 4][:, 0:cn]).then_inc(stored[u % 4], 16)
            with pool.Fori(0, 3) as m:
                for u in range(2 * NT):
                    h, t = divmod(u, NT)
                    pool.wait_ge(tm_evac, 2 * NT * m + (u + 5))
                    pool.dma_start(io["tm"][bass.ds(m * NPAD + t * TT, TT), h * HC:(h + 1) * HC],
                                   stage[u % 4][0:TT, :]).then_inc(stored[u % 4], 16)
            for s in range(4):
                pool.wait_ge(stored[s], 16 * ((48 + 60) // 4))

        @block.scalar
        def _(act):
            act.dma_start(edges[:, :, :], io["edges"]).then_inc(edges_landed, 16)
            act.sem_inc(qk_evac, 4)

            def root(p):
                act.wait_ge(var_ready, p + 1)
                act.activation(std[:, 2 * p:2 * p + 2], mv[:, 2 * p:2 * p + 2, 1], ACT.Sqrt, bias=eps[:, :]
                               ).then_inc(std_ready, 1)

            def evacuate(m, u):
                c, dd = u % 12 // 4, u % 4
                cn = QK_CH[c][1]
                act.wait_ge(gemm_done, 24 * m + (u + 1))
                if 24 * m + u >= 4:
                    act.wait_ge(stored[u % 4], 16 * (6 * m + u // 4))
                act.activation(stage[u % 4][:, 0:cn], ring[:, u % 4, 0:cn], ACT.Identity,
                               bias=bias_qk[:, m, 4 * (u // 12) + dd:4 * (u // 12) + dd + 1]).then_inc(qk_evac, 1)

            root(0)
            for t in range(NT):
                if t % 2 == 0 and t + 2 < NT:
                    root(t // 2 + 1)
                act.wait_ge(xn_ready, t + 1)
                if t >= 2:
                    act.wait_ge(hl_stored[t % 2], 16 * (t // 2))
                act.activation(hl[t % 2][:, 0:D], x_all[:, t, :], ACT.Copy, scale=XS).then_inc(h16_ready, 1)
                act.wait_ge(tr_done, t + 1)
                act.activation(xT_hi[:, :, t * TT:(t + 1) * TT].rearrange("p (b k) t -> p b k t", b=2), turned(t),
                               ACT.Copy).then_inc(xT_hi_ready, 1)
                if t == 1:
                    split_hi(0, 16)
                if t == 4:
                    act.wait_ge(bqk_landed, 16)
                if t >= 5:
                    evacuate(0, t - 5)
            act.wait_ge(l16_ready, 8)
            act.wait_ge(xn_stored, 16 * NT // 2)
            split_hi(1, 16)
            for m in range(2):
                for h in range(2):
                    for v in range(12):
                        u = 12 * h + v
                        if 24 * m + u >= 5:
                            evacuate(m, u)
                    split_hi(h, 16 * m + 32)
            for s in range(STEP_TM + 2, STEP_REL):
                act.wait_ge(gemm_done, 48 + NT * (s - STEP_TM - 1))
                split_hi(s % 2, 16 * (s // 2 + 1))

        @block.vector
        def _(dve):
            ch = Chain(dve, dve_step)
            ch.add(dve.memset(eps[:, :], EPS))

            def statistics(p):
                dve.wait_ge(x_landed[p], 16)
                for t in (2 * p, 2 * p + 1):
                    for h in range(2):
                        ch.add(dve.bn_stats(stats[:, t, h, :], x_all[:, t, h * HC:(h + 1) * HC]))
                ch.wait()
                for t in (2 * p, 2 * p + 1):
                    last = dve.bn_aggr(mv[:, t, :], stats[:, t, :, :].rearrange("p a b -> p (a b)"))
                last.then_inc(var_ready, 1)
                dve.wait_ge(std_ready, p + 1)
                sl = slice(2 * p, 2 * p + 2)
                inverse_root(dve, ch, rstd[:, sl], std[:, sl], mv[:, sl, 1], EPS)

            def normalise(t):
                dve.tensor_scalar(x_all[:, t, :], x_all[:, t, :], mv[:, t, 0:1], rstd[:, t:t + 1],
                                  ALU.subtract, ALU.mult).then_inc(xn_ready, 1)

            statistics(0)
            normalise(0)
            for t in range(NT):
                if t % 2 == 0 and t + 2 < NT:
                    statistics(t // 2 + 1)
                if t + 1 < NT:
                    normalise(t + 1)
                dve.wait_ge(h16_ready, t + 1)
                dve.wait_ge(xn_ready, t + 1)
                dve.scalar_tensor_tensor(hl[t % 2][:, D:2 * D], x_all[:, t, :], XS, hl[t % 2][:, 0:D],
                                         ALU.mult, ALU.subtract).then_inc(l16_ready, 1)
                dve.wait_ge(xT_hi_ready, t + 1)
                sl = slice(t * TT, (t + 1) * TT)
                dve.tensor_tensor(xT_lo[:, :, sl].rearrange("p (b k) t -> p b k t", b=2), turned(t),
                                  xT_hi[:, :, sl].bitcast(F32).rearrange("p (b k) t -> p b k t", b=2),
                                  ALU.subtract).then_inc(xT_lo_ready, 1)
                if t == 1:
                    split_lo(0, 0)
            for s in range(2):
                dve.wait_ge(hl_stored[s], 16 * (NT // 2))
            split_lo(1, 1)

            dve.wait_ge(edges_landed, 16)
            dve.wait_ge(pconst, 2)
            srcf, dl, dl1, bkt, lo, hi, rank = (k[n] for n in ("srcf", "dl", "dl1", "bkt", "lo", "hi", "rank"))
            ch.link(dve.tensor_scalar(srcf[:, :], edges[:, 0, :], 0.0, float(N - 1), ALU.max, ALU.min))
            ch.add(dve.tensor_copy(dl[:, :], edges[:, 1, :]))
            ch.add(dve.tensor_copy(bkt[:, :], edges[:, 2, :]))
            ch.link(dve.memset(tmp[:, :], 0.0))
            for w in range(1, NT):
                ch.link(dve.scalar_tensor_tensor(tmp[:, :], dl[:, :], float(w * TT), tmp[:, :], ALU.is_ge, ALU.add))
            ch.add(dve.scalar_tensor_tensor(dl[:, :], tmp[:, :], float(-TT), dl[:, :], ALU.mult, ALU.add))
            ch.link(dve.scalar_tensor_tensor(bkt[:, :], bkt[:, :], float(NT), tmp[:, :], ALU.mult, ALU.add))
            ch.add(dve.tensor_scalar(dl1[:, :], dl[:, :], 1.0, None, ALU.add))
            dve.wait_ge(xn_ready, NT)
            ch.add(dve.memset(reset[:, :, :], 1.0))
            ch.add(dve.memset(rank[:, :], 0.0))
            ch.wait()
            ch.link(dve.memset(reset[:, :, 0:1], 0.0))

            def one_hot_chunk(c):
                return dve.tensor_tensor(oh_c[:, :, :], bkt[:, :].unsqueeze(1).to_broadcast([EP, CB, EJ]),
                                         k["iota16"][0:EP, bass.ds(c * CB, CB)].unsqueeze(2).to_broadcast([EP, CB, EJ]),
                                         ALU.is_equal)

            n0 = ch.n
            with dve.Fori(0, NCH) as c:
                lp = Chain(dve, dve_step, base=2 * c + n0)
                lp.link(one_hot_chunk(c))
                lp.link(dve.reduce_sum(tot[:, bass.ds(c * CB, CB)], oh_c[:, :, :], AX.X))
            ch.n += 2 * NCH
            dve.tensor_copy(tot16[:, :], tot[:, :]).then_inc(tot_ready, 1)
            split_lo(2, 0)
            dve.wait_ge(base_ready, 1)
            ch.add(dve.tensor_scalar(base1[:, :], ps_base[0:EP, 0:NB], 1.0, None, ALU.subtract))
            ch.link(dve.reduce_max(mx[:, 0:1], ps_cnt[0:EP, 0:NB], AX.X))
            ch.link(dve.tensor_scalar(thr[:, :], thr[:, :], mx[:, 0:1], None, ALU.is_lt))
            ch.link(dve.reduce_sum(mx[:, 1:2], thr[:, 1:56], AX.X))
            ch.link(dve.tensor_scalar(k["rounds"][0:EP, :], mx[:, 1:2], 1.0, None, ALU.add))

            def rank_chunks(c0, c1):
                n0 = ch.n
                with dve.Fori(c0, c1) as c:
                    lp = Chain(dve, dve_step, base=6 * c + (n0 - 6 * c0))
                    lp.link(one_hot_chunk(c))
                    lp.link(dve.tensor_tensor_scan(scan_c[:, :, :].rearrange("p b j -> p (b j)"),
                                                   reset[:, :, :].rearrange("p b j -> p (b j)"),
                                                   oh_c[:, :, :].rearrange("p b j -> p (b j)"), 0.0, ALU.mult, ALU.add))
                    lp.link(dve.tensor_tensor(scan_c[:, :, :], scan_c[:, :, :],
                                              base1[:, bass.ds(c * CB, CB)].unsqueeze(2).to_broadcast([EP, CB, EJ]),
                                              ALU.add))
                    lp.link(dve.tensor_tensor(scan_c[:, :, :], scan_c[:, :, :], oh_c[:, :, :], ALU.mult))
                    lp.link(dve.reduce_sum(tmp[:, :], scan_c[:, :, :].rearrange("p b j -> p j b"), AX.X))
                    lp.link(dve.tensor_tensor(rank[:, :], rank[:, :], tmp[:, :], ALU.add))
                ch.n += 6 * (c1 - c0)

            rank_chunks(0, NCH // 3)
            split_lo(3, 1)
            rank_chunks(NCH // 3, 2 * NCH // 3 + 1)
            split_lo(4, 0)
            rank_chunks(2 * NCH // 3 + 1, NCH)
            slot_of_rank(dve, ch, k, tmp)

            dve.sem_inc(tm_evac, 4)
            dve.sem_inc(job_used, 2)

            def token_major(m, first, last):
                for h in range(2):
                    dve.wait_ge(bias_landed[h], 16 * m + 16)
                    for t in range(NT):
                        u = NT * h + t
                        v = u - JU0
                        if not first or v >= 0:
                            dve.wait_ge(job_used, 20 * m + (v + 1))
                            for jj in range(JU):
                                o = one_hots(dve, k, job[v % 2][:, jj, :], 20 * JU * m + (JU * v + jj))
                            o.then_inc(job_ready, 1)
                        dve.wait_ge(gemm_done, 20 * m + (48 + u + 1))
                        dve.wait_ge(stored[u % 4], 80 * m + (16 * (u // 4) + 16 * 12))
                        dve.tensor_tensor(stage[u % 4][0:TT, :], ring[0:TT, u % 4, :], bias_bc[h][:, :], ALU.add
                                          ).then_inc(tm_evac, 1)
                        if t < 4 and not (last and h == 1):
                            split_lo_part(2 * m + (STEP_TM + 1 + h), 1 - h, t)

            token_major(0, True, False)
            with dve.Fori(1, 2) as m:
                token_major(m, False, False)
            token_major(2, False, True)
            dve.wait_ge(table_done, 1)
            read_table(dve, k, ps_src, ps_dst)
            dve.tensor_scalar(k["rc"][:, :], ps_cnt[0:TT, 0:NB], 1.0, None, ALU.max).then_inc(base_read, 1)
            dve.wait_ge(base_read, 1)
            dve.reciprocal(k["rc"][:, :], k["rc"][:, :])

        @block.tensor
        def _(pe):
            pe.wait_ge(consts, 2)

            def turn(t):
                pe.wait_ge(xn_ready, t + 1)
                if t >= 2:
                    pe.wait_ge(xT_lo_ready, t - 1)
                for kb in range(KB):
                    o = nc.tensor.transpose(ps_t[:, 2 * (t % 2) + kb // 4, (kb % 4) * TT:(kb % 4 + 1) * TT],
                                            x_all[:, t, kb * P:(kb + 1) * P], k["ident"][0:TT, 0:TT])
                o.then_inc(tr_done, 1)

            def feature_major(m, u):
                h, c, dd = u // 12, u % 12 // 4, u % 4
                c0, cn = QK_CH[c]
                if m == 0 and h == 0 and dd == 0:
                    pe.wait_ge(xT_lo_ready, (c0 + cn) // TT)
                pe.wait_ge(qk_evac, 24 * m + (u + 1))
                for kb in range(KB):
                    if u % 12 == 0 and kb % 2 == 0:
                        pe.wait_ge(w_lo, 8 * m + (4 * h + kb // 2 + 1))
                    w = slice(dd * P, (dd + 1) * P)
                    o = mm3(nc, ring[:, u % 4, 0:cn], (whi[h][:, kb, w], wlo[h][:, kb, w]),
                            (xT_hi[:, kb, c0:c0 + cn], xT_lo[:, kb, c0:c0 + cn]), kb == 0, kb == KB - 1)
                o.then_inc(gemm_done, 1)

            for t in range(5):
                turn(t)
            for t in range(5, NT):
                feature_major(0, t - 5)
                turn(t)
            for m in range(2):
                for u in range(24):
                    if 24 * m + u >= 5:
                        feature_major(m, u)
                if m == 0:
                    pe.wait_ge(tot_ready, 1)
                    nc.tensor.matmul(ps_cnt[0:EP, 0:NB], ones16[:, 0:EP], tot16[:, :], start=True, stop=True)
                    nc.tensor.matmul(ps_base[0:EP, 0:NB], below[:, :], tot16[:, :], start=True, stop=True
                                     ).then_inc(base_ready, 1)
            pe.wait_ge(qk_evac, 48 + 4)

            def table(out, a, b, start=False, stop=False):
                return nc.tensor.matmul(out, a, b, start=start, stop=stop)

            tables = ((ps_src[0:P, 0:NC], P), (ps_dst[0:P, 0:NC], P), (ps_cnt[0:TT, 0:NB], TT))
            pe.wait_ge(w_lo, 16 + 4)
            for o_, n_ in tables:
                table(o_, zero16[:, 0:n_], zero16[:, 0:o_.shape[1]], start=True)

            def token_major(m, first):
                for h in range(2):
                    for t in range(NT):
                        u = NT * h + t
                        pe.wait_ge(tm_evac, 20 * m + (u + 1))
                        for kb in range(KB):
                            if t == 0 and kb % 2 == 0:
                                pe.wait_ge(w_lo, 8 * m + (16 + 4 * h + kb // 2 + 1))
                            tk = slice(t * TT, (t + 1) * TT)
                            o = mm3(nc, ring[0:TT, u % 4, :], (xT_hi[:, kb, tk], xT_lo[:, kb, tk]),
                                    (whi[h][:, kb, :], wlo[h][:, kb, :]), kb == 0, kb == KB - 1)
                        o.then_inc(gemm_done, 1)
                        v = u - JU0
                        if not first or v >= 0:
                            pe.wait_ge(job_ready, 20 * m + (v + 1))
                            for jj in range(JU):
                                o = table_products(nc, job[v % 2][:, jj, :], ps_src, ps_dst, ps_cnt)
                            o.then_inc(job_used, 1)

            token_major(0, True)
            with pe.Fori(1, 3) as m:
                token_major(m, False)
            for o_, n_ in tables:
                o = table(o_, zero16[:, 0:n_], zero16[:, 0:o_.shape[1]], stop=True)
            o.then_inc(table_done, 1)


def phase_attend(nc, mem, io, k):
    mem.cursor = 0
    CH, G, NCK = P, 16, NPAD // P
    feat = [[mem.next(f"a_feat{s}{j}", [P, 2, CH, NH], F32) for j in range(2)] for s in range(2)]
    qk = [[mem.next(f"a_qk{s}{j}", [P, KB, CH], F32) for j in range(2)] for s in range(2)]
    qk_hi = [[mem.next(f"a_qk_hi{s}{j}", [P, KB, CH], F32R) for j in range(2)] for s in range(2)]
    qk_lo = [[mem.next(f"a_qk_lo{s}{j}", [P, KB, CH], F32R) for j in range(2)] for s in range(2)]
    v2 = [mem.next(f"a_v{s}", [P, G, 2, HD], F32) for s in range(2)]
    msk = [mem.next(f"a_msk{s}", [P, 4, P], F32) for s in range(4)]
    prob = [mem.next(f"a_prob{s}", [P, 4, P], F32) for s in range(4)]
    probT = [mem.next(f"a_probT{s}", [P, 4 * P], F32) for s in range(2)]
    att = [mem.next(f"a_att{s}", [P, KB, CH], F32) for s in range(2)]
    mask = mem.next("a_mask", [P, P], F32)
    rfT = mem.next("a_rfT", [P, M], F32)
    rf_hi, rf_lo = mem.next("a_rf_hi", [P, M], F32R), mem.next("a_rf_lo", [P, M], F32R)
    mx = [mem.next(f"a_mx{s}", [P, 4], F32) for s in range(2)]
    sm = [mem.next(f"a_sm{s}", [P, 4], F32) for s in range(2)]
    assert mem.cursor <= 6 * KB * HC * 4 + 2 * KB * N * 4

    with ExitStack() as ctx:
        def sem(name):
            return ctx.enter_context(nc.semaphore("a_" + name))

        ps_f = ctx.enter_context(nc.psum_tensor("a_ps_f", [P, 2, HC], F32))
        ps_s = ctx.enter_context(nc.psum_tensor("a_ps_s", [P, 2, HC], F32))
        ps_t = ctx.enter_context(nc.psum_tensor("a_ps_t", [P, 2, HC], F32))
        ps_o = ctx.enter_context(nc.psum_tensor("a_ps_o", [P, 2, HC], F32))
        landed = [[sem(f"landed{s}{j}") for j in range(4)] for s in range(2)]
        rf_landed, mask_step = sem("rf_landed"), sem("mask_step")
        rf_hi_ready, rf_lo_ready = sem("rf_hi_ready"), sem("rf_lo_ready")
        qk_hi_ready, qk_lo_ready = sem("qk_hi_ready"), sem("qk_lo_ready")
        feat_done, feat_evac = sem("feat_done"), sem("feat_evac")
        s_done, s_read, msk_ready, exp_done, p_ready = (sem(n) for n in
                                                        ("s_done", "s_read", "msk_ready", "exp_done", "p_ready"))
        t_done, t_evac, o_done, o_evac = (sem(n) for n in ("t_done", "t_evac", "o_done", "o_evac"))
        att_stored = [sem(f"att_stored{s}") for s in range(2)]
        att_free = sem("att_free")
        dve_step = sem("dve_step")
        block = ctx.enter_context(nc.Block())

        qk_rows = [io["qkT"][j * D:(j + 1) * D, :].rearrange("(b p) t -> p b t", p=P) for j in range(2)]
        v_rows = io["tm"][0:NPAD, :].rearrange("t (h d) -> (t h) d", d=HD)
        att_rows = io["attnT"].rearrange("(b p) t -> p b t", p=P)

        def load_qk(sp, s, c):
            for j in range(2):
                sp.dma_start(qk[s][j][:, :, :], qk_rows[j][:, :, bass.ds(c * CH, CH)]).then_inc(landed[s][j], 16)

        def load_v(sp, s, c):
            for j in range(2):
                sp.dma_start(v2[s][:, :, j, :], v_rows[bass.ds(c * CH * NH, CH * NH), :]
                             .rearrange("(g p) d -> p g d", p=P)).then_inc(landed[s][2 + j], 16)

        @block.sync
        def _(sp):
            for j in range(2):
                sp.dma_start(rfT[j * HD:(j + 1) * HD, :], io["rfT"]).then_inc(rf_landed, 16)
            for s in range(2):
                load_qk(sp, s, s)
                load_v(sp, s, s)

            def chunk(i, s, last):
                if not last:
                    sp.wait_ge(qk_lo_ready, 4 * i + (2 * s + 2))
                    load_qk(sp, s, 2 * i + (s + 2))
                    sp.wait_ge(o_done, 8 * i + (4 * s + 4 + 2))
                    load_v(sp, s, 2 * i + (s + 2))
                sp.wait_ge(o_evac, 8 * i + (4 * s + 4 + 2))
                sp.dma_start(att_rows[:, :, bass.ds((2 * i + s) * CH, CH)], att[s][:, :, :]
                             ).then_inc(att_stored[s], 16)
                sp.wait_ge(att_stored[s], 16 * i + 16)
                sp.sem_inc(att_free, 1)

            with sp.Fori(0, NCK // 2 - 1) as i:
                for s in range(2):
                    chunk(i, s, False)
            for s in range(2):
                chunk(NCK // 2 - 1, s, True)

        @block.gpsimd
        def _(pool):
            pool.memset(mask[:, :], 0.0).then_inc(mask_step, 1)
            pool.wait_ge(mask_step, 1)
            mv_ = mask[:, :].rearrange("p (b h) -> p b h", h=NH)
            pool.affine_select(out=mv_, in_=mv_, compare_op=ALU.is_ge, fill=NEG, base=0,
                               pattern=[[-NH, 8], [0, NH]], channel_multiplier=1).then_inc(mask_step, 1)
            pool.wait_ge(mask_step, 2)
            pool.affine_select(out=mv_, in_=mv_, compare_op=ALU.is_ge, fill=NEG, base=NH - 1,
                               pattern=[[NH, 8], [0, NH]], channel_multiplier=-1).then_inc(mask_step, 1)

        UNITS = [(j, mh, kg, par) for j in range(2) for mh in range(2) for kg in range(2) for par in range(2)]

        @block.scalar
        def _(act):
            act.sem_inc(feat_evac, 2)
            act.sem_inc(t_evac, 2)
            act.sem_inc(exp_done, 4)

            act.wait_ge(rf_landed, 32)
            act.activation(rf_hi[:, :], rfT[:, :], ACT.Copy).then_inc(rf_hi_ready, 1)

            def split_high(i, s):
                for j in range(2):
                    act.wait_ge(landed[s][j], 16 * i + 16)
                    act.activation(qk_hi[s][j][:, :, :], qk[s][j][:, :, :], ACT.Copy).then_inc(qk_hi_ready, 1)

            def features(i, s, f0, f1):
                for f in range(f0, f1):
                    j, mh, kg, par = UNITS[f]
                    act.wait_ge(feat_done, 32 * i + (16 * s + f + 1))
                    out = feat[s][j][:, :, :, :].rearrange("p m t (g i r) -> p m g r i t", g=2, r=2)[:, mh, kg, par, :, :]
                    act.activation(out, ps_f[:, f % 2, :].rearrange("p (i t) -> p i t", i=4), ACT.Relu
                                   ).then_inc(feat_evac, 1)

            def chunk(i, s, last, peeled=False):
                def exponential(b):
                    act.wait_ge(msk_ready, 8 * i + (4 * s + b + 1))
                    act.wait_ge(t_done, 8 * i + (4 * s + b + 1))
                    act.activation(prob[b][:, :, :], msk[b][:, :, :], ACT.Exp, scale=HD ** -0.5
                                   ).then_inc(exp_done, 1)

                def transposed(b):
                    act.wait_ge(t_done, 8 * i + (4 * s + b + 1 + 4))
                    act.wait_ge(o_done, 8 * i + (4 * s + b + 1))
                    act.activation(probT[b % 2][:, :], ps_t[:, b % 2, :], ACT.Copy).then_inc(t_evac, 1)

                def next_features(f0, f1):
                    if not last:
                        features(i + s, 1 - s, f0, f1)

                exponential(0)
                exponential(1)
                next_features(0, 2)
                exponential(2)
                next_features(2, 4)
                exponential(3)
                next_features(4, 10)
                transposed(0)
                next_features(10, 14)
                transposed(1)
                next_features(14, 16)
                if not peeled:
                    split_high(i + 1, s)
                transposed(2)
                transposed(3)

            split_high(0, 0)
            split_high(0, 1)
            features(0, 0, 0, 16)
            with act.Fori(0, NCK // 2 - 1) as i:
                for s in range(2):
                    chunk(i, s, False)
            for s in range(2):
                chunk(NCK // 2 - 1, s, s == 1, True)

        @block.vector
        def _(dve):
            dve.sem_inc(s_read, 2)
            dve.sem_inc(o_evac, 2)
            dve.wait_ge(mask_step, 3)

            dve.wait_ge(rf_hi_ready, 1)
            dve.tensor_tensor(rf_lo[:, :], rfT[:, :], rf_hi[:, :].bitcast(F32), ALU.subtract).then_inc(rf_lo_ready, 1)

            def split_low(i, s):
                for j in range(2):
                    dve.wait_ge(qk_hi_ready, 4 * i + (2 * s + j + 1))
                    dve.tensor_tensor(qk_lo[s][j][:, :, :], qk[s][j][:, :, :], qk_hi[s][j][:, :, :].bitcast(F32),
                                      ALU.subtract).then_inc(qk_lo_ready, 1)

            def chunk(i, s, last):
                ch = Chain(dve, dve_step, base=(i * 2 + s) * 12)

                def shift(b):
                    dve.wait_ge(s_done, 8 * i + (4 * s + b + 1))
                    dve.wait_ge(exp_done, 8 * i + (4 * s + b + 1))
                    dve.tensor_tensor(msk[b][:, :, :], ps_s[:, b % 2, :].rearrange("p (g c) -> p g c", g=4),
                                      mask[:, :].unsqueeze(1).to_broadcast([P, 4, P]), ALU.add).then_inc(s_read, 1)
                    dve.wait_ge(s_read, 8 * i + (4 * s + b + 3))
                    ch.link(dve.reduce_max(mx[b % 2][:, :], msk[b][:, :, :], AX.X))
                    dve.tensor_tensor(msk[b][:, :, :], msk[b][:, :, :],
                                      mx[b % 2][:, :].unsqueeze(2).to_broadcast([P, 4, P]), ALU.subtract
                                      ).then_inc(msk_ready, 1)

                def normalise(b):
                    dve.wait_ge(exp_done, 8 * i + (4 * s + b + 1 + 4))
                    ch.link(dve.reduce_sum(sm[b % 2][:, :], prob[b][:, :, :], AX.X))
                    ch.link(dve.reciprocal(sm[b % 2][:, :], sm[b % 2][:, :]))
                    dve.tensor_tensor(prob[b][:, :, :], prob[b][:, :, :],
                                      sm[b % 2][:, :].unsqueeze(2).to_broadcast([P, 4, P]), ALU.mult
                                      ).then_inc(p_ready, 1)

                shift(0)
                shift(1)
                normalise(0)
                shift(2)
                normalise(1)
                shift(3)
                normalise(2)
                normalise(3)
                assert ch.n == 12
                dve.wait_ge(att_free, 2 * i + (s + 1))
                if not last:
                    split_low(i + 1, s)
                for b in range(4):
                    dve.wait_ge(o_done, 8 * i + (4 * s + b + 3))
                    for r in range(2):
                        src = ps_o[:, b % 2, :].rearrange("p (x a r) -> p r x a", r=2, a=KB)
                        rows = slice(r * HD, (r + 1) * HD)
                        o = dve.tensor_copy(att[s][rows, :, b * 32:(b + 1) * 32].rearrange("p a x -> p x a"),
                                            src[rows, r, :, :])
                    o.then_inc(o_evac, 1)

            dve.sem_inc(att_free, 2)
            for s in range(2):
                split_low(0, s)
            with dve.Fori(0, NCK // 2 - 1) as i:
                for s in range(2):
                    chunk(i, s, False)
            for s in range(2):
                chunk(NCK // 2 - 1, s, True)

        @block.tensor
        def _(pe):
            pe.sem_inc(t_done, 4)
            pe.sem_inc(o_done, 2)
            pe.wait_ge(rf_lo_ready, 1)

            def features(i, s, f0, f1):
                for f in range(f0, f1):
                    j, mh, kg, par = UNITS[f]
                    if f % 8 == 0:
                        pe.wait_ge(qk_lo_ready, 4 * i + (2 * s + f // 8 + 1))
                    pe.wait_ge(feat_evac, 32 * i + (16 * s + f + 1))
                    rows, cols, heads = slice(par * HD, (par + 1) * HD), slice(mh * P, (mh + 1) * P), slice(4 * kg, 4 * kg + 4)
                    mm3(nc, ps_f[:, f % 2, :], (rf_hi[rows, cols], rf_lo[rows, cols]),
                        tuple(part[s][j][rows, heads, :].rearrange("p a t -> p (a t)") for part in (qk_hi, qk_lo)),
                        True, True).then_inc(feat_done, 1)

            def chunk(i, s, last):
                pe.wait_ge(feat_evac, 32 * i + (16 * s + 16 + 2))
                for b in range(4):
                    pe.wait_ge(s_read, 8 * i + (4 * s + b + 1))
                    for n in range(4):
                        t0 = (4 * b + n) * 8
                        for mh in range(2):
                            o = nc.tensor.matmul(ps_s[:, b % 2, n * P:(n + 1) * P],
                                                 feat[s][0][:, mh, t0:t0 + 8, :].rearrange("p t h -> p (t h)"),
                                                 feat[s][1][:, mh, t0:t0 + 8, :].rearrange("p t h -> p (t h)"),
                                                 start=(mh == 0), stop=(mh == 1))
                    o.then_inc(s_done, 1)
                def turn(b):
                    pe.wait_ge(p_ready, 8 * i + (4 * s + b + 1))
                    pe.wait_ge(t_evac, 8 * i + (4 * s + b + 1))
                    for n in range(4):
                        o = nc.tensor.transpose(ps_t[:, b % 2, n * P:(n + 1) * P], prob[b][:, n, :],
                                                k["ident"][:, :])
                    o.then_inc(t_done, 1)

                def weigh(b):
                    if b == 0:
                        for j in range(2):
                            pe.wait_ge(landed[s][2 + j], 16 * i + 16)
                    pe.wait_ge(t_evac, 8 * i + (4 * s + b + 3))
                    pe.wait_ge(o_evac, 8 * i + (4 * s + b + 1))
                    for n in range(4):
                        o = nc.tensor.matmul(ps_o[:, b % 2, n * P:(n + 1) * P],
                                             v2[s][:, 4 * b + n, :, :].rearrange("p a d -> p (a d)"),
                                             probT[b % 2][:, n * P:(n + 1) * P], start=True, stop=True)
                    o.then_inc(o_done, 1)

                def next_features(f0, f1):
                    if not last:
                        features(i + s, 1 - s, f0, f1)

                next_features(0, 8)
                turn(0)
                next_features(8, 12)
                turn(1)
                next_features(12, 16)
                weigh(0)
                turn(2)
                weigh(1)
                turn(3)
                weigh(2)
                weigh(3)

            features(0, 0, 0, 16)
            with pe.Fori(0, NCK // 2 - 1) as i:
                for s in range(2):
                    chunk(i, s, False)
            for s in range(2):
                chunk(NCK // 2 - 1, s, s == 1)

def phase_relate(nc, mem, io, k):
    half = KB * HC * 4
    whi = [mem.at(f"r_whi{s}", [P, KB, HC], F32R, o) for s, o in enumerate((0, 4 * half))]
    wlo = [mem.at(f"r_wlo{s}", [P, KB, HC], F32R, o) for s, o in enumerate((half, 5 * half))]
    raw = [mem.at(f"r_raw{s}", [P, KB, HC], F32, o) for s, o in enumerate((2 * half, 3 * half))]
    mem.cursor = 6 * half
    u = mem.next("r_u", [TT, NT, D], F32)
    sT_hi = [mem.next(f"r_sT_hi{s}", [P, KB * TT], F32R) for s in range(2)]
    sT_lo = [mem.next(f"r_sT_lo{s}", [P, KB * TT], F32R) for s in range(2)]
    rows = [mem.next("r_rows0", [P, CAP, 2 * D], F16)]
    oh = [mem.next(f"r_oh{s}", [P, CAP, TT], F16) for s in range(2)]
    src = [mem.next(f"r_src{s}", [P, CAP], U32) for s in range(2)]
    job = [mem.next(f"r_job{s}", [EP, 704], F16) for s in range(2)]
    zero16 = mem.next("r_zero16", [EP, NC], F16)
    tmp = mem.next("r_tmp", [EP, EJ], F32)
    assert mem.cursor <= k["start"]
    mem.cursor = k["start"] + k["bytes"]
    rows.append(mem.next("r_rows1", [P, CAP, 2 * D], F16))
    NW = NB + 2
    MAXR = -(-EP * EJ // (CAP * P))

    with ExitStack() as ctx:
        def sem(name):
            return ctx.enter_context(nc.semaphore("r_" + name))

        ring = ctx.enter_context(nc.psum_tensor("r_ring", [P, 4, HC], F32))
        ps_a = [ctx.enter_context(nc.psum_tensor(f"r_ps_a{s}", [P, 2, HC], F32)) for s in range(2)]
        w_landed = [sem(f"w_landed{s}") for s in range(2)]
        rows_landed = [sem(f"rows_landed{s}") for s in range(2)]
        u_landed = sem("u_landed")
        w_hi, w_lo = sem("w_hi"), sem("w_lo")
        slots_ready, sums_done, hi_ready, lo_ready = sem("slots_ready"), sem("sums_done"), sem("hi_ready"), sem("lo_ready")
        gemm_done, u_added = sem("gemm_done"), sem("u_added")
        dve_step, job_ready, job_used, table_done, table_read = (
            sem(n) for n in ("dve_step", "job_ready", "job_used", "table_done", "table_read"))
        waited = sem("waited")
        block = ctx.enter_context(nc.Block())
        w_rows = io["w"].rearrange("s p b n -> (s p) (b n)")

        def rounds_of(eng):
            return eng.value_load(k["rounds"][0:1, 0:1], min_val=1, max_val=MAXR)

        @block.sync
        def _(sp):
            sp.dma_start(u[:, :, :], io["tm"][NPAD:NPAD + N, :].rearrange("(t p) d -> p t d", p=TT)
                         ).then_inc(u_landed, 16)

            def load(r, h):
                sp.dma_start(raw[h][:, :, :].rearrange("p b n -> p (b n)"),
                             w_rows[bass.ds((STEP_REL + h) * P + r * 2 * P, P), :]).then_inc(w_landed[h], 16)

            for h in range(2):
                load(0, h)
            n = rounds_of(sp)
            with sp.Fori(0, n) as rd:
                with sp.Fori(0, R - 1) as r:
                    for h in range(2):
                        sp.wait_ge(w_lo, 64 * rd + 8 * r + (4 * h + 4))
                        load(r + 1, h)
                for h in range(2):
                    sp.wait_ge(w_lo, 64 * rd + (8 * (R - 1) + 4 * h + 4))
                    load(0, h)
            for h in range(2):
                sp.wait_ge(w_landed[h], 16 * R * n + 16)
                sp.sem_inc(waited, 1)

        @block.gpsimd
        def _(pool):
            n = rounds_of(pool)

            def gather(a, slot):
                pool.wait_ge(slots_ready, a + 1)
                pool.sem_inc(waited, 1)
                for c in range(CAP):
                    pool.indirect_dma_start(out=rows[slot][:, c, :], out_offset=None, in_=io["rows"],
                                            in_offset=bass.IndirectOffsetOnAxis(src[slot][:, c:c + 1], 0)
                                            ).then_inc(rows_landed[slot], 16)

            with pool.Fori(0, n) as rd:
                with pool.Fori(0, NW // 2) as i:
                    for s in range(2):
                        gather(NW * rd + 2 * i + s, s)

        @block.scalar
        def _(act):
            act.sem_inc(sums_done, 2)
            n = rounds_of(act)

            def high(a, g, slot):
                act.wait_ge(sums_done, a + 3)
                act.wait_ge(lo_ready, a + 1)
                act.wait_ge(gemm_done, g + 1)
                act.activation(sT_hi[slot][:, :].rearrange("p (b x) -> p b x", b=2), ps_a[slot][:, :, 0:4 * TT],
                               ACT.Copy, scale=1 / XS).then_inc(hi_ready, 1)

            with act.Fori(0, n) as rd:
                high(NW * rd, NB * rd, 0)
                with act.Fori(0, R) as r:
                    act.wait_ge(gemm_done, NB * rd + NT * r + 2)
                    for h in range(2):
                        act.wait_ge(w_landed[h], 128 * rd + 16 * r + 16)
                        for c in range(4):
                            act.activation(whi[h][:, 2 * c:2 * c + 2, :], raw[h][:, 2 * c:2 * c + 2, :], ACT.Copy
                                           ).then_inc(w_hi, 1)
                    for w in range(NT):
                        high(NW * rd + NT * r + (w + 1), NB * rd + NT * r + (w + 1), (w + 1) % 2)
                high(NW * rd + (NB + 1), NB * rd + (NB + 1), 1)

        @block.vector
        def _(dve):
            dve.sem_inc(lo_ready, 2)
            dve.sem_inc(u_added, 2)
            dve.memset(zero16[:, :], 0.0).then_inc(table_read, 1)
            n = rounds_of(dve)
            dve.wait_ge(u_landed, 16)

            def slots(a, col, slot):
                dve.wait_ge(sums_done, a + 1)
                for c in range(CAP):
                    dve.tensor_scalar(oh[slot][:, c, :], k["iota16"][:, 0:TT], k["slot_dst"][:, bass.ds(col + c, 1)],
                                      None, ALU.is_equal)
                dve.tensor_scalar(src[slot][:, :], k["slot_src"][:, bass.ds(col, CAP)], 0.0, None, ALU.add
                                  ).then_inc(slots_ready, 1)

            def low(a, slot):
                dve.wait_ge(hi_ready, a + 1)
                dve.scalar_tensor_tensor(sT_lo[slot][:, :].rearrange("p (b x) -> p b x", b=2),
                                         ps_a[slot][:, :, 0:4 * TT], 1 / XS,
                                         sT_hi[slot][:, :].bitcast(F32).rearrange("p (b x) -> p b x", b=2),
                                         ALU.mult, ALU.subtract).then_inc(lo_ready, 1)

            with dve.Fori(0, n) as rd:
                for a in range(2):
                    slots(NW * rd + a, CAP * a, a)
                low(NW * rd, 0)
                with dve.Fori(0, R) as r:
                    for w in range(NT):
                        slots(NW * rd + NT * r + (w + 2), CAP * NT * r + CAP * (w + 2), w % 2)
                        if w == 0:
                            for h in range(2):
                                for c in range(4):
                                    dve.wait_ge(w_hi, 64 * rd + 8 * r + (4 * h + c + 1))
                                    dve.tensor_tensor(wlo[h][:, 2 * c:2 * c + 2, :], raw[h][:, 2 * c:2 * c + 2, :],
                                                      whi[h][:, 2 * c:2 * c + 2, :].bitcast(F32), ALU.subtract
                                                      ).then_inc(w_lo, 1)
                        low(NW * rd + NT * r + (w + 1), (w + 1) % 2)
                        dve.wait_ge(gemm_done, NB * rd + NT * r + (w + 3))
                        b = 2 * (w % 2)
                        dve.scalar_tensor_tensor(u[:, w, :].rearrange("p (b x) -> p b x", b=2), ring[0:TT, b:b + 2, :],
                                                 k["rc"][:, bass.ds(NT * r + w, 1)],
                                                 u[:, w, :].rearrange("p (b x) -> p b x", b=2), ALU.mult, ALU.add
                                                 ).then_inc(u_added, 1)
                low(NW * rd + (NB + 1), 1)
                with dve.If(rd < n - 1):
                    ch = Chain(dve, dve_step, base=(4 + CAP - 2) * rd)
                    dve.wait_ge(sums_done, NW * rd + (NW + 2))
                    dve.wait_ge(lo_ready, NW * rd + (NW + 2))
                    ch.link(dve.tensor_scalar(k["rank"][:, :], k["rank"][:, :], float(-CAP * P), None, ALU.add))
                    slot_of_rank(dve, ch, k, tmp)
                    assert ch.n == 4 + CAP - 2
                    dve.sem_inc(waited, 1)
                    with dve.Fori(0, EJ // 2) as j:
                        for s in range(2):
                            dve.wait_ge(job_used, EJ * rd + 2 * j + (s + 1))
                            one_hots(dve, k, job[s][:, :], 2 * j + s).then_inc(job_ready, 1)
                    dve.wait_ge(table_done, rd + 1)
                    read_table(dve, k, ps_a[0][:, 0, :], ps_a[0][:, 1, :]).then_inc(table_read, 1)
                    dve.wait_ge(table_read, rd + 2)
                    dve.sem_inc(waited, 1)

        @block.tensor
        def _(pe):
            pe.sem_inc(gemm_done, 2)
            pe.sem_inc(job_used, 2)
            n = rounds_of(pe)
            pe.wait_ge(table_read, 1)

            def sums(a, landed, slot):
                pe.wait_ge(rows_landed[slot], landed)
                pe.wait_ge(slots_ready, a + 1)
                pe.wait_ge(lo_ready, a + 1)
                for kb in range(KB):
                    for c in range(CAP):
                        for part in range(2):
                            o = nc.tensor.matmul(ps_a[slot][:, kb // 4, (kb % 4) * TT:(kb % 4 + 1) * TT],
                                                 rows[slot][:, c, part * D + kb * P:part * D + (kb + 1) * P],
                                                 oh[slot][:, c, :], start=(c == 0 and part == 0),
                                                 stop=(c == CAP - 1 and part == 1))
                o.then_inc(sums_done, 1)

            LAND = 16 * CAP
            with pe.Fori(0, n) as rd:
                sums(NW * rd, LAND * (NW // 2) * rd + LAND, 0)
                with pe.Fori(0, R) as r:
                    for w in range(NT):
                        sums(NW * rd + NT * r + (w + 1),
                             LAND * (NW // 2) * rd + LAND * (NT // 2) * r + LAND * ((w + 1) // 2 + 1), (w + 1) % 2)
                        pe.wait_ge(lo_ready, NW * rd + NT * r + (w + 3))
                        pe.wait_ge(u_added, NB * rd + NT * r + (w + 1))
                        for h in range(2):
                            for kb in range(KB):
                                if w == 0 and kb % 2 == 0:
                                    pe.wait_ge(w_lo, 64 * rd + 8 * r + (4 * h + kb // 2 + 1))
                                tk = slice(kb * TT, (kb + 1) * TT)
                                o = mm3(nc, ring[0:TT, 2 * (w % 2) + h, :], (sT_hi[w % 2][:, tk], sT_lo[w % 2][:, tk]),
                                        (whi[h][:, kb, :], wlo[h][:, kb, :]), kb == 0, kb == KB - 1)
                        o.then_inc(gemm_done, 1)
                sums(NW * rd + (NB + 1), LAND * (NW // 2) * rd + LAND * (NW // 2), 1)
                with pe.If(rd < n - 1):
                    pe.wait_ge(lo_ready, NW * rd + (NW + 2))
                    banks = [ps_a[0][:, s, 0:NC] for s in range(2)]
                    for b in banks:
                        nc.tensor.matmul(b, zero16[:, 0:P], zero16[:, :], start=True, stop=False)
                    with pe.Fori(0, EJ // 2) as j:
                        for s in range(2):
                            pe.wait_ge(job_ready, EJ * rd + 2 * j + (s + 1))
                            table_products(nc, job[s][:, :], ps_a[0][:, 0, :], ps_a[0][:, 1, :], None
                                           ).then_inc(job_used, 1)
                    for b in banks:
                        o = nc.tensor.matmul(b, zero16[:, 0:P], zero16[:, :], start=False, stop=True)
                    o.then_inc(table_done, 1)
                    pe.wait_ge(table_read, rd + 2)
    return u


def phase_update(nc, mem, io, k):
    half = KB * HC * 4
    whi = [mem.at(f"g_whi{s}", [P, KB, HC], F32R, o) for s, o in enumerate((0, 4 * half))]
    wlo = [mem.at(f"g_wlo{s}", [P, KB, HC], F32R, o) for s, o in enumerate((half, 5 * half))]
    raw = [mem.at(f"g_raw{s}", [P, KB, HC], F32, o) for s, o in enumerate((2 * half, 3 * half))]
    u = k["u"]
    mem.cursor = 6 * half + 4 * NT * D
    aT_hi = [mem.next(f"g_aT_hi{s}", [P, KB * TT], F32R) for s in range(2)]
    aT_lo = [mem.next(f"g_aT_lo{s}", [P, KB * TT], F32R) for s in range(2)]
    attn = [mem.at(f"g_attn{s}", [P, KB, TT], F32, mem.cursor + s * 4 * D) for s in range(2)]
    row = [mem.next(f"g_row{s}", [TT, D], F32) for s in range(2)]
    th = [mem.next(f"g_th{s}", [TT, D], F32) for s in range(2)]
    bo_bc = mem.next("g_bo_bc", [TT, D], F32)
    assert mem.cursor <= k["start"]
    mem.cursor = k["start"] + k["bytes"]
    xn_t, z0_t, xx_t = ([mem.next(f"g_{n}{s}", [TT, D], F32) for s in range(2)] for n in ("xn", "z0", "xx"))
    stats = mem.at("g_stats", [TT, NT, 2, 6], F32, k["start"] + k["bytes"])
    std = mem.at("g_std", [TT, NT], F32, k["start"] + k["bytes"] + 512)
    eps = mem.at("g_eps", [TT, 1], F32, k["start"] + k["bytes"] + 576)
    mv, rstd = k["mv"], k["rstd"]

    with ExitStack() as ctx:
        def sem(name):
            return ctx.enter_context(nc.semaphore("g_" + name))

        ring = ctx.enter_context(nc.psum_tensor("g_ring", [P, 4, HC], F32))
        ps_t = [ctx.enter_context(nc.psum_tensor(f"g_ps_t{s}", [P, 2, HC], F32)) for s in range(2)]
        w_landed = [sem(f"w_landed{s}") for s in range(2)]
        t_landed = [[sem(f"t_landed{s}{j}") for j in range(3)] for s in range(2)]
        a_landed = [sem(f"a_landed{s}") for s in range(2)]
        w_hi, w_lo = sem("w_hi"), sem("w_lo")
        row_ready, turned, hi_ready, lo_ready = sem("row_ready"), sem("turned"), sem("hi_ready"), sem("lo_ready")
        gemm_done, ring_read, tanh_ready, tiles_used = (sem(n) for n in ("gemm_done", "ring_read", "tanh_ready", "tiles_used"))
        x2_ready, var_ready, std_ready = sem("x2_ready"), sem("var_ready"), sem("std_ready")
        x2_stored, dve_step = sem("x2_stored"), sem("dve_step")
        bo_landed, xx_step = sem("bo_landed"), sem("xx_step")
        block = ctx.enter_context(nc.Block())

        @block.sync
        def _(sp):
            for h in range(2):
                sp.dma_start(raw[h][:, :, :], io["w"][STEP_GATE + h]).then_inc(w_landed[h], 16)
            for t in range(NT):
                if t >= 2:
                    sp.wait_ge(tiles_used, t - 1)
                rows = slice(t * TT, (t + 1) * TT)
                for j, (dst, src) in enumerate(((xn_t, io["xn"][rows, :]), (xx_t, io["x"][rows, :]),
                                                (z0_t, io["tm"][2 * NPAD + t * TT:2 * NPAD + (t + 1) * TT, :]))):
                    sp.dma_start(dst[t % 2][:, :], src).then_inc(t_landed[t % 2][j], 16)
                if t == 0:
                    for h in range(2):
                        sp.wait_ge(w_lo, 4 * h + 4)
                        sp.dma_start(raw[h][:, :, :], io["w"][STEP_WO + h]).then_inc(w_landed[h], 16)

        @block.gpsimd
        def _(pool):
            pool.dma_start(bo_bc[:, :], io["bo"].to_broadcast([TT, D])).then_inc(bo_landed, 16)

            def fetch(t):
                if t >= 2:
                    pool.wait_ge(turned, t - 1)
                pool.tensor_copy(row[t % 2][:, :], u[:, t, :]).then_inc(row_ready, 1)

            fetch(0)
            fetch(1)
            pool.wait_ge(bo_landed, 16)
            for t in range(NT):
                xx = xx_t[t % 2][:, :]
                for j in range(2):
                    pool.wait_ge(t_landed[t % 2][j], 16 * (t // 2 + 1))
                pool.tensor_tensor(xx, xx, xn_t[t % 2][:, :], ALU.add).then_inc(xx_step, 1)
                pool.wait_ge(xx_step, 2 * t + 1)
                pool.tensor_tensor(xx, xx, bo_bc[:, :], ALU.add).then_inc(xx_step, 1)
                if t + 2 < NT:
                    fetch(t + 2)
            for t in range(NT):
                if t < 2:
                    pool.wait_ge(turned, NT)
                    pool.wait_ge(tanh_ready, NT)
                    pool.wait_ge(tiles_used, NT)
                else:
                    pool.wait_ge(lo_ready, NT + t - 1)
                pool.dma_start(attn[t % 2][:, :, :], io["attnT"][:, t * TT:(t + 1) * TT]
                               .rearrange("(b p) t -> p b t", p=P)).then_inc(a_landed[t % 2], 16)
            for t in range(NT):
                pool.wait_ge(x2_ready, t + 1)
                pool.dma_start(io["x2"][t * TT:(t + 1) * TT, :], u[:, t, :]).then_inc(x2_stored, 16)
            pool.wait_ge(x2_stored, 16 * NT)

        def split_w_hi(act, m, h):
            act.wait_ge(w_landed[h], 16 * (m + 1))
            for c in range(4):
                act.activation(whi[h][:, 2 * c:2 * c + 2, :], raw[h][:, 2 * c:2 * c + 2, :], ACT.Copy).then_inc(w_hi, 1)

        def split_w_lo(dve, m, h):
            for c in range(4):
                dve.wait_ge(w_hi, 8 * m + 4 * h + c + 1)
                dve.tensor_tensor(wlo[h][:, 2 * c:2 * c + 2, :], raw[h][:, 2 * c:2 * c + 2, :],
                                  whi[h][:, 2 * c:2 * c + 2, :].bitcast(F32), ALU.subtract).then_inc(w_lo, 1)

        @block.scalar
        def _(act):
            for h in range(2):
                split_w_hi(act, 0, h)
            for t in range(NT):
                act.wait_ge(turned, t + 1)
                if t >= 2:
                    act.wait_ge(gemm_done, t - 1)
                act.activation(aT_hi[t % 2][:, :].rearrange("p (b x) -> p b x", b=2), ps_t[t % 2][:, :, 0:4 * TT],
                               ACT.Copy).then_inc(hi_ready, 1)
                if t >= 2:
                    act.wait_ge(tiles_used, t - 1)
                act.activation(th[t % 2][:, :], u[:, t, :], ACT.Tanh).then_inc(tanh_ready, 1)
            act.wait_ge(gemm_done, NT)
            for h in range(2):
                split_w_hi(act, 1, h)
            for t in range(NT):
                act.wait_ge(a_landed[t % 2], 16 * (t // 2 + 1))
                if t >= 2:
                    act.wait_ge(gemm_done, NT + t - 1)
                act.activation(aT_hi[t % 2][:, :], attn[t % 2][:, :, :].rearrange("p b t -> p (b t)"), ACT.Copy
                               ).then_inc(hi_ready, 1)
            act.wait_ge(var_ready, 1)
            act.activation(std[:, :], mv[:, :, 1], ACT.Sqrt, bias=eps[:, :]).then_inc(std_ready, 1)

        @block.vector
        def _(dve):
            ch = Chain(dve, dve_step)
            for h in range(2):
                split_w_lo(dve, 0, h)

            def low(t):
                dve.wait_ge(hi_ready, t + 1)
                dve.tensor_tensor(aT_lo[t % 2][:, :].rearrange("p (b x) -> p b x", b=2), ps_t[t % 2][:, :, 0:4 * TT],
                                  aT_hi[t % 2][:, :].bitcast(F32).rearrange("p (b x) -> p b x", b=2), ALU.subtract
                                  ).then_inc(lo_ready, 1)

            low(0)
            for t in range(NT):
                if t + 1 < NT:
                    low(t + 1)
                for j in range(3):
                    dve.wait_ge(t_landed[t % 2][j], 16 * (t // 2 + 1))
                dve.wait_ge(tanh_ready, t + 1)
                ch.add(dve.tensor_tensor(th[t % 2][:, :], th[t % 2][:, :], xn_t[t % 2][:, :], ALU.subtract))
                dve.wait_ge(gemm_done, t + 1)
                z = z0_t[t % 2][:, :].rearrange("p (b x) -> p b x", b=2)
                dve.tensor_tensor(z, ring[0:TT, 2 * (t % 2):2 * (t % 2) + 2, :], z, ALU.add).then_inc(ring_read, 1)
                dve.wait_ge(ring_read, t + 1)
                ch.link(dve.tensor_tensor(th[t % 2][:, :], th[t % 2][:, :], z0_t[t % 2][:, :], ALU.mult))
                dve.wait_ge(xx_step, 2 * t + 2)
                dve.tensor_tensor(u[:, t, :], th[t % 2][:, :], xx_t[t % 2][:, :], ALU.add).then_inc(tiles_used, 1)
            for h in range(2):
                split_w_lo(dve, 1, h)

            def low_attn(t):
                dve.wait_ge(hi_ready, NT + t + 1)
                dve.tensor_tensor(aT_lo[t % 2][:, :], attn[t % 2][:, :, :].rearrange("p b t -> p (b t)"),
                                  aT_hi[t % 2][:, :].bitcast(F32), ALU.subtract).then_inc(lo_ready, 1)

            dve.wait_ge(tiles_used, NT)
            ch.link(dve.memset(eps[:, :], EPS))
            low_attn(0)
            for t in range(NT):
                if t + 1 < NT:
                    low_attn(t + 1)
                dve.wait_ge(gemm_done, NT + t + 1)
                ut = u[:, t, :].rearrange("p (b x) -> p b x", b=2)
                dve.tensor_tensor(ut, ring[0:TT, 2 * (t % 2):2 * (t % 2) + 2, :], ut, ALU.add).then_inc(x2_ready, 1)
                dve.wait_ge(x2_ready, t + 1)
                for h in range(2):
                    ch.add(dve.bn_stats(stats[:, t, h, :], u[:, t, h * HC:(h + 1) * HC]))
            ch.wait()
            for t in range(NT):
                o = dve.bn_aggr(mv[:, t, :], stats[:, t, :, :].rearrange("p a b -> p (a b)"))
            o.then_inc(var_ready, 1)
            dve.wait_ge(std_ready, 1)
            inverse_root(dve, ch, rstd, std, mv[:, :, 1], EPS)

        @block.tensor
        def _(pe):
            def turn(t):
                pe.wait_ge(row_ready, t + 1)
                if t >= 2:
                    pe.wait_ge(lo_ready, t - 1)
                for kb in range(KB):
                    o = nc.tensor.transpose(ps_t[t % 2][:, kb // 4, (kb % 4) * TT:(kb % 4 + 1) * TT],
                                            row[t % 2][:, kb * P:(kb + 1) * P], k["ident"][0:TT, 0:TT])
                o.then_inc(turned, 1)

            def gemm(t, m):
                pe.wait_ge(lo_ready, NT * m + t + 1)
                if NT * m + t >= 2:
                    if m == 0:
                        pe.wait_ge(ring_read, t - 1)
                    elif t < 2:
                        pe.wait_ge(ring_read, NT + t - 1)
                    else:
                        pe.wait_ge(x2_ready, t - 1)
                for h in range(2):
                    for kb in range(KB):
                        if t == 0 and kb % 2 == 0:
                            pe.wait_ge(w_lo, 8 * m + 4 * h + kb // 2 + 1)
                        tk = slice(kb * TT, (kb + 1) * TT)
                        o = mm3(nc, ring[0:TT, 2 * (t % 2) + h, :], (aT_hi[t % 2][:, tk], aT_lo[t % 2][:, tk]),
                                (whi[h][:, kb, :], wlo[h][:, kb, :]), kb == 0, kb == KB - 1)
                o.then_inc(gemm_done, 1)

            turn(0)
            for t in range(NT):
                if t + 1 < NT:
                    turn(t + 1)
                gemm(t, 0)
            for t in range(NT):
                gemm(t, 1)


def phase_ffn(nc, mem, io, k):
    half = KB * HC * 4
    whi = [mem.at(f"f_whi{s}", [P, KB, HC], F32R, o) for s, o in enumerate((0, 4 * half))]
    wlo = [mem.at(f"f_wlo{s}", [P, KB, HC], F32R, o) for s, o in enumerate((half, 5 * half))]
    raw = mem.at("f_raw", [P, KB, HC], F32, 2 * half)
    mem.cursor = 3 * half
    y = [mem.next(f"f_y{s}", [TT, D], F32) for s in range(2)]
    pre = [mem.next(f"f_pre{s}", [TT, HC], F32) for s in range(4)]
    mem.cursor = 6 * half
    yT_hi = mem.next("f_yT_hi", [P, KB, N], F32R)
    yT_lo = mem.next("f_yT_lo", [P, KB, N], F32R)
    mem.cursor = k["start"] + k["bytes"]
    cell = mem.next("f_cell", [TT, NT, HC], F32)
    x2h = [mem.next(f"f_x2h{s}", [TT, HC], F32) for s in range(2)]
    bias = [mem.at(f"f_bias{s}", [TT, HC], F32, k["edges_at"] + s * HC * 4) for s in range(2)]
    mv, rstd = k["mv"], k["rstd"]
    STEPS = 6

    with ExitStack() as ctx:
        def sem(name):
            return ctx.enter_context(nc.semaphore("f_" + name))

        ring = ctx.enter_context(nc.psum_tensor("f_ring", [P, 4, HC], F32))
        ps_t = [ctx.enter_context(nc.psum_tensor(f"f_ps_t{s}", [P, 2, HC], F32)) for s in range(2)]
        w_landed, bias_landed, x2_landed = sem("w_landed"), [sem(f"bias_landed{s}") for s in range(2)], [
            sem(f"x2_landed{s}") for s in range(2)]
        h_landed = [sem(f"h_landed{s}") for s in range(2)]
        w_hi, w_lo = sem("w_hi"), sem("w_lo")
        y_ready, turned, hi_ready, lo_ready = sem("y_ready"), sem("turned"), sem("hi_ready"), sem("lo_ready")
        gemm_done, pre_ready, gate_ready, cell_ready, out_ready = (
            sem(n) for n in ("gemm_done", "pre_ready", "gate_ready", "cell_ready", "out_ready"))
        act_step, dve_step = sem("act_step"), sem("dve_step")
        out_stored = [sem(f"out_stored{s}") for s in range(4)]
        block = ctx.enter_context(nc.Block())

        @block.sync
        def _(sp):
            def load(q):
                if q >= 1:
                    sp.wait_ge(w_lo, 4 * q)
                sp.dma_start(raw[:, :, :], io["w"][STEP_LSTM + q]).then_inc(w_landed, 16)
                if q >= 2:
                    sp.wait_ge(pre_ready, NT * (q - 1))
                sp.dma_start(bias[q % 2][:, :], io["bias_lstm"][q:q + 1, :].to_broadcast([TT, HC])
                             ).then_inc(bias_landed[q % 2], 16)

            load(0)
            for t in range(NT):
                if t == 2:
                    load(1)
                if t >= 2:
                    sp.wait_ge(turned, t - 1)
                sp.dma_start(y[t % 2][:, :], io["x2"][t * TT:(t + 1) * TT, :]).then_inc(x2_landed[t % 2], 16)
            for q in range(2, STEPS):
                load(q)

        def slot_of(v):
            return (NT * (3 * (v // NT) + 2) + v % NT) % 4

        def stores_before(v):
            return sum(1 for w in range(v) if slot_of(w) == slot_of(v))

        def store(pool, v):
            c, t = divmod(v, NT)
            pool.wait_ge(out_ready, v + 1)
            pool.dma_start(io["out"][t * TT:(t + 1) * TT, c * HC:(c + 1) * HC], pre[slot_of(v)][:, :]
                           ).then_inc(out_stored[slot_of(v)], 16)

        @block.gpsimd
        def _(pool):
            for c in range(2):
                for t in range(NT):
                    v = NT * c + t
                    if v >= 2:
                        pool.wait_ge(out_ready, v - 1)
                    pool.dma_start(x2h[t % 2][:, :], io["x2"][t * TT:(t + 1) * TT, c * HC:(c + 1) * HC]
                                   ).then_inc(h_landed[t % 2], 16)
                    if v >= 1:
                        store(pool, v - 1)
            store(pool, 2 * NT - 1)
            for s in range(4):
                pool.wait_ge(out_stored[s], 16 * sum(1 for v in range(2 * NT) if slot_of(v) == s))

        def split_w_hi(act, q):
            act.wait_ge(w_landed, 16 * (q + 1))
            if q >= 2:
                act.wait_ge(gemm_done, NT * (q - 1))
            for c in range(4):
                act.activation(whi[q % 2][:, 2 * c:2 * c + 2, :], raw[:, 2 * c:2 * c + 2, :], ACT.Copy).then_inc(w_hi, 1)

        def split_w_lo(dve, q):
            for c in range(4):
                dve.wait_ge(w_hi, 4 * q + c + 1)
                dve.tensor_tensor(wlo[q % 2][:, 2 * c:2 * c + 2, :], raw[:, 2 * c:2 * c + 2, :],
                                  whi[q % 2][:, 2 * c:2 * c + 2, :].bitcast(F32), ALU.subtract).then_inc(w_lo, 1)

        @block.scalar
        def _(act):
            split_w_hi(act, 0)

            def high(t):
                act.wait_ge(turned, t + 1)
                act.activation(yT_hi[:, :, t * TT:(t + 1) * TT].rearrange("p (b k) t -> p b k t", b=2),
                               ps_t[t % 2][:, :, 0:4 * TT].rearrange("p b (k t) -> p b k t", t=TT), ACT.Copy
                               ).then_inc(hi_ready, 1)

            high(0)
            for q in range(STEPS):
                c, gate = divmod(q, 3)
                for t in range(NT):
                    n = NT * q + t
                    if n + 1 < NT:
                        high(n + 1)
                    if n == 2:
                        split_w_hi(act, 1)
                    if gate == 2:
                        act.wait_ge(cell_ready, NT * c + t + 1)
                        act.activation(cell[:, t, :], cell[:, t, :], ACT.Tanh).then_inc(act_step, 1)
                    act.wait_ge(pre_ready, n + 1)
                    if gate == 0 and c == 1:
                        act.wait_ge(out_ready, t + 1)
                    act.activation(cell[:, t, :] if gate == 0 else pre[n % 4][:, :], pre[n % 4][:, :],
                                   ACT.Tanh if gate == 1 else ACT.Sigmoid).then_inc(gate_ready, 1)
                if q + 2 < STEPS:
                    split_w_hi(act, q + 2)

        @block.vector
        def _(dve):
            ch = Chain(dve, dve_step)
            split_w_lo(dve, 0)

            def normalise(t):
                dve.wait_ge(x2_landed[t % 2], 16 * (t // 2 + 1))
                dve.tensor_scalar(y[t % 2][:, :], y[t % 2][:, :], mv[:, t, 0:1], rstd[:, t:t + 1],
                                  ALU.subtract, ALU.mult).then_inc(y_ready, 1)

            def low(t):
                dve.wait_ge(hi_ready, t + 1)
                sl = slice(t * TT, (t + 1) * TT)
                dve.tensor_tensor(yT_lo[:, :, sl].rearrange("p (b k) t -> p b k t", b=2),
                                  ps_t[t % 2][:, :, 0:4 * TT].rearrange("p b (k t) -> p b k t", t=TT),
                                  yT_hi[:, :, sl].bitcast(F32).rearrange("p (b k) t -> p b k t", b=2), ALU.subtract
                                  ).then_inc(lo_ready, 1)

            def finish(n):
                q, t = divmod(n, NT)
                c, gate = divmod(q, 3)
                dve.wait_ge(gate_ready, n + 1)
                if gate == 1:
                    dve.tensor_tensor(cell[:, t, :], cell[:, t, :], pre[n % 4][:, :], ALU.mult).then_inc(cell_ready, 1)
                elif gate == 2:
                    ch.link(dve.tensor_tensor(pre[n % 4][:, :], pre[n % 4][:, :], cell[:, t, :], ALU.mult))
                    dve.wait_ge(h_landed[t % 2], 16 * (NT // 2 * c + t // 2 + 1))
                    dve.tensor_tensor(pre[n % 4][:, :], pre[n % 4][:, :], x2h[t % 2][:, :], ALU.add
                                      ).then_inc(out_ready, 1)

            def add_bias(n):
                q, t = divmod(n, NT)
                if t == 0:
                    dve.wait_ge(bias_landed[q % 2], 16 * (q // 2 + 1))
                dve.wait_ge(gemm_done, n + 1)
                if n >= 4:
                    before = n - 4
                    qb, tb = divmod(before, NT)
                    cb, gb = divmod(qb, 3)
                    if gb == 0:
                        dve.wait_ge(gate_ready, before + 1)
                    elif gb == 1:
                        dve.wait_ge(cell_ready, NT * cb + tb + 1)
                    else:
                        v = NT * cb + tb
                        dve.wait_ge(out_stored[slot_of(v)], 16 * (stores_before(v) + 1))
                dve.tensor_tensor(pre[n % 4][:, :], ring[0:TT, n % 4, :], bias[q % 2][:, :], ALU.add
                                  ).then_inc(pre_ready, 1)

            normalise(0)
            low(0)
            for n in range(NT * STEPS):
                if n + 1 < NT:
                    normalise(n + 1)
                    low(n + 1)
                if n == 2:
                    split_w_lo(dve, 1)
                add_bias(n)
                if n >= 1:
                    finish(n - 1)
                if n % NT == NT - 1 and n // NT + 2 < STEPS:
                    split_w_lo(dve, n // NT + 2)
            finish(NT * STEPS - 1)

        @block.tensor
        def _(pe):
            def turn(t):
                pe.wait_ge(y_ready, t + 1)
                if t >= 2:
                    pe.wait_ge(lo_ready, t - 1)
                for kb in range(KB):
                    o = nc.tensor.transpose(ps_t[t % 2][:, kb // 4, (kb % 4) * TT:(kb % 4 + 1) * TT],
                                            y[t % 2][:, kb * P:(kb + 1) * P], k["ident"][0:TT, 0:TT])
                o.then_inc(turned, 1)

            turn(0)
            for q in range(STEPS):
                for t in range(NT):
                    if q == 0 and t + 1 < NT:
                        turn(t + 1)
                    n = NT * q + t
                    if q == 0:
                        pe.wait_ge(lo_ready, t + 1)
                    if n >= 4:
                        pe.wait_ge(pre_ready, n - 3)
                    for kb in range(KB):
                        if t == 0 and kb % 2 == 0:
                            pe.wait_ge(w_lo, 4 * q + kb // 2 + 1)
                        tk = slice(t * TT, (t + 1) * TT)
                        o = mm3(nc, ring[0:TT, n % 4, :], (yT_hi[:, kb, tk], yT_lo[:, kb, tk]),
                                (whi[q % 2][:, kb, :], wlo[q % 2][:, kb, :]), kb == 0, kb == KB - 1)
                    o.then_inc(gemm_done, 1)


def inverse_root(dve, ch, out, root, var, eps):
    ch.link(dve.reciprocal(out[:, :], root[:, :]))
    ch.link(dve.tensor_tensor(root[:, :], out[:, :], out[:, :], ALU.mult))
    ch.link(dve.scalar_tensor_tensor(root[:, :], var, eps, root[:, :], ALU.add, ALU.mult))
    ch.link(dve.tensor_scalar(root[:, :], root[:, :], -0.5, 1.5, ALU.mult, ALU.add))
    ch.link(dve.tensor_tensor(out[:, :], out[:, :], root[:, :], ALU.mult))


def slot_of_rank(dve, ch, k, tmp):
    ch.link(dve.tensor_scalar(tmp[:, :], k["rank"][:, :], float(P), None, ALU.is_ge))
    for c in range(2, CAP):
        ch.link(dve.scalar_tensor_tensor(tmp[:, :], k["rank"][:, :], float(c * P), tmp[:, :], ALU.is_ge, ALU.add))
    ch.add(dve.scalar_tensor_tensor(k["lo"][:, :], tmp[:, :], float(-P), k["rank"][:, :], ALU.mult, ALU.add))
    ch.link(dve.scalar_tensor_tensor(k["hi"][:, :], k["bkt"][:, :], float(CAP), tmp[:, :], ALU.mult, ALU.add))


def one_hots(dve, k, out, j):
    i16 = k["iota16"]
    col = {n: k[n][:, bass.ds(j, 1)] for n in ("lo", "hi", "srcf", "dl1", "dl", "bkt")}
    dve.tensor_scalar(out[:, 0:128], i16[0:EP, 0:128], col["lo"], col["srcf"], ALU.is_equal, ALU.mult)
    dve.tensor_scalar(out[:, 128:256], i16[0:EP, 0:128], col["lo"], col["dl1"], ALU.is_equal, ALU.mult)
    dve.tensor_scalar(out[:, 256:256 + NC], i16[0:EP, 0:NC], col["hi"], None, ALU.is_equal)
    dve.tensor_scalar(out[:, 496:496 + TT], i16[0:EP, 0:TT], col["dl"], None, ALU.is_equal)
    return dve.tensor_scalar(out[:, 622:622 + NB], i16[0:EP, 0:NB], col["bkt"], None, ALU.is_equal)


def table_products(nc, j, ps_src, ps_dst, ps_cnt):
    hi = j[:, 256:256 + NC]
    nc.tensor.matmul(ps_src[0:P, 0:NC], j[:, 0:128], hi, start=False, stop=False)
    o = nc.tensor.matmul(ps_dst[0:P, 0:NC], j[:, 128:256], hi, start=False, stop=False)
    if ps_cnt is not None:
        o = nc.tensor.matmul(ps_cnt[0:TT, 0:NB], j[:, 496:496 + TT], j[:, 622:622 + NB], start=False, stop=False)
    return o


def read_table(dve, k, ps_src, ps_dst):
    dve.tensor_copy(k["slot_src"][:, 0:NC], ps_src[:, 0:NC])
    dve.memset(k["slot_src"][:, NC:NC + 2 * CAP], 0.0)
    dve.tensor_scalar(k["slot_dst"][:, 0:NC], ps_dst[:, 0:NC], 1.0, None, ALU.subtract)
    return dve.memset(k["slot_dst"][:, NC:NC + 2 * CAP], -1.0)


def kept_tensors(mem):
    half = KB * HC * 4
    mem.cursor = 6 * half + 2 * KB * N * 4
    start = mem.cursor
    k = {
        "ident": mem.next("ident", [P, P], F32),
        "iota16": mem.next("iota16", [P, 256], F16),
        "slot_src": mem.next("slot_src", [P, NC + 2 * CAP], F32),
        "slot_dst": mem.next("slot_dst", [P, NC + 2 * CAP], F32),
        "rc": mem.next("rc", [TT, NB], F32),
        "rounds": mem.next("rounds", [P, 1], I32),
    }
    k["mv"] = mem.next("mv", [TT, NT, 2], F32)
    k["rstd"] = mem.next("rstd", [TT, NT], F32)
    k["edges_at"] = mem.cursor
    for n in ("srcf", "dl", "dl1", "bkt", "lo", "hi", "rank"):
        k[n] = mem.next("e_" + n, [EP, EJ], F32)
    k["start"], k["bytes"] = start, mem.cursor - start
    return k


def build(nc, io):
    mem = Memory(nc)
    keep = kept_tensors(mem)
    phase_project(nc, mem, io, keep)
    phase_attend(nc, mem, io, keep)
    keep["u"] = phase_relate(nc, mem, io, keep)
    phase_update(nc, mem, io, keep)
    phase_ffn(nc, mem, io, keep)
    return keep


def kernel(**inputs):
    import numpy as _np
    import concourse.bacc as _bacc
    from concourse import mybir as _mybir
    from concourse.bass_utils import run_bass_kernel_spmd as _run

    a = {n: _np.asarray(v) for n, v in inputs.items()}

    def halves(w):
        return w.reshape(KB, P, 2, HC).transpose(2, 1, 0, 3)

    gnn, mix, ffn = "L0_gnn_", "L0_mix_", "L0_ffn_"
    gate = a[gnn + "w_gate"]
    mats = [a[mix + "Wq"], a[mix + "Wk"], a[mix + "Wv"], a[gnn + "root"], gate[D:]]
    mats += [a[gnn + "weight"][r] for r in range(R)] + [gate[:D], a[mix + "Wo"]]
    steps = [s for w in mats for s in halves(w)]
    lstm = [halves(a[ffn + n][:, D:].T) for n in ("W_i", "W_c", "W_o")]
    steps += [w[h] for h in range(2) for w in lstm]
    edges = _np.zeros((3, EP * EJ), _np.int32)
    edges[2] = -1
    for i, n in enumerate(("src", "dst", "edge_type_8")):
        edges[i, :a[n].shape[0]] = a[n]
    host = {
        "x": a["x"],
        "w": _np.ascontiguousarray(_np.stack(steps)),
        "edges": _np.ascontiguousarray(edges.reshape(3, EP, EJ).transpose(1, 0, 2)),
        "bias_qk": _np.ascontiguousarray(_np.stack([a[mix + "bq"], a[mix + "bk"]]).reshape(2, KB, P).transpose(2, 0, 1)),
        "bias_tm": _np.ascontiguousarray(
            _np.stack([a[mix + "bv"], a[gnn + "bias"], a[gnn + "b_gate"]]).reshape(6, HC)),
        "bo": a[mix + "bo"].reshape(1, D),
        "bias_lstm": _np.ascontiguousarray(_np.stack([a[ffn + n] for n in ("b_i", "b_c", "b_o")]).reshape(3, 2, HC)
                                           .transpose(1, 0, 2).reshape(6, HC)),
        "rfT": _np.ascontiguousarray(a[mix + "rf"].T),
    }
    nc = _bacc.Bacc("TRN2", target_bir_lowering=False, num_devices=1)
    io, arrays = {}, {}
    for n, v in host.items():
        arrays["in_" + n] = v
        io[n] = nc.dram_tensor("in_" + n, v.shape, _mybir.dt.from_np(v.dtype), kind="ExternalInput").ap()
    for n, shape, dt in (("qkT", (2 * D, NPAD), F32), ("tm", (3 * NPAD, D), F32), ("rows", (N, 2 * D), F16),
                         ("xn", (N, D), F32), ("attnT", (D, NPAD), F32), ("x2", (N, D), F32)):
        io[n] = nc.dram_tensor("mid_" + n, shape, dt, kind=MID).ap()
    io["out"] = nc.dram_tensor("out_0_dram", (N, D), F32, kind="ExternalOutput").ap()
    build(nc, io)
    r = _run(nc, [arrays], core_ids=[0])
    return r.results[0]["out_0_dram"]
```

```python
from contextlib import ExitStack

import numpy as np
import concourse.bass as bass
from concourse import mybir

F32 = mybir.dt.float32
F32R = mybir.dt.float32r
F16 = mybir.dt.float16
I32 = mybir.dt.int32
U32 = mybir.dt.uint32
ALU = mybir.AluOpType
ACT = mybir.ActivationFunctionType
AX = mybir.AxisListType

P = 128
N = 1250
D = 1024
R = 8
TT = 125
NT = N // TT
KB = D // P
HC = 512
NPAD = 1280
EP, EJ = 125, 180
NB = R * NT
CAP = 3
NC = NB * CAP
NH, HD, M = 16, 64, 256
EPS = 1e-5
SIZE = {F32: 4, F32R: 4, I32: 4, U32: 4, F16: 2}
MID = "Internal"
XS = 1024.0
NEG = -1e30

STEP_QK, STEP_TM, STEP_REL, STEP_GATE, STEP_WO, STEP_LSTM = 0, 4, 10, 26, 28, 30


def mm3(nc, out, a, b, first, last):
    nc.tensor.matmul(out, a[0], b[0], start=first, stop=False)
    nc.tensor.matmul(out, a[0], b[1], start=False, stop=False)
    return nc.tensor.matmul(out, a[1], b[0], start=False, stop=last)


class Chain:

    def __init__(self, eng, sem, base=0):
        self.eng, self.sem, self.base, self.n = eng, sem, base, 0

    def add(self, ins):
        ins.then_inc(self.sem, 1)
        self.n += 1
        return ins

    def wait(self):
        self.eng.wait_ge(self.sem, self.base + self.n)

    def link(self, ins):
        self.add(ins)
        self.wait()


class Memory:

    def __init__(self, nc):
        self.nc = nc
        self.base = (nc.sbuf_base + 63) // 64 * 64
        self.end = nc.sbuf_usable_end
        self.cursor = 0

    def at(self, name, shape, dt, offset):
        size = int(np.prod(shape[1:])) * SIZE[dt]
        assert self.base + offset + size <= self.end, (name, offset, size, self.end - self.base)
        return self.nc.alloc_sbuf_tensor_at(name, shape, dt, offset=self.base + offset)

    def next(self, name, shape, dt):
        t = self.at(name, shape, dt, self.cursor)
        self.cursor += (int(np.prod(shape[1:])) * SIZE[dt] + 31) // 32 * 32
        return t


def phase_project(nc, mem, io, keep):
    half = KB * HC * 4
    whi = [mem.at(f"p_whi{s}", [P, KB, HC], F32R, o) for s, o in enumerate((0, 4 * half))]
    wlo = [mem.at(f"p_wlo{s}", [P, KB, HC], F32R, o) for s, o in enumerate((half, 5 * half))]
    raw = keep["raw"]
    x_all = mem.at("p_x_all", [TT, NT, D], F32, 3 * half)
    hl = [mem.at(f"p_hl{s}", [TT, 2 * D], F16, 3 * half + NT * D * 4 + s * D * 4) for s in range(2)]
    mem.cursor = 6 * half
    xT_hi = mem.next("p_xT_hi", [P, KB, N], F32R)
    xT_lo = mem.next("p_xT_lo", [P, KB, N], F32R)
    mem.cursor += keep["bytes"]
    stage = [mem.next(f"p_stage{s}", [P, HC], F32) for s in range(4)]
    at_sort = mem.cursor
    CB = 5
    NCH = NB // CB
    oh_c = mem.next("p_oh_c", [EP, CB, EJ], F16)
    reset = mem.next("p_reset", [EP, CB, EJ], F16)
    scan_c = mem.next("p_scan_c", [EP, CB, EJ], F32)
    edges = mem.next("p_edges", [EP, 3, EJ], I32)
    tot = mem.next("p_tot", [EP, NB], F32)
    tot16 = mem.next("p_tot16", [EP, NB], F16)
    base1 = mem.next("p_base1", [EP, NB], F32)
    below = mem.next("p_below", [EP, EP], F16)
    ones16 = mem.next("p_ones16", [EP, P], F16)
    thr = mem.next("p_thr", [EP, 56], F32)
    after_sort = mem.cursor
    JU, JU0, JW = 4, 15, 704
    assert JU * (6 * NT - JU0) == EJ
    job = [mem.at(f"p_job{s}", [EP, JU, JW], F16, at_sort + s * JU * JW * 2) for s in range(2)]
    mem.cursor = max(after_sort, at_sort + 2 * JU * JW * 2)
    pads = mem.at("p_pads", [P, HC], F32, mem.cursor)
    bias_bc = [mem.next(f"p_bias_bc{s}", [TT, HC], F32) for s in range(2)]
    bias_qk = mem.next("p_bias_qk", [P, 2, KB], F32)
    k = keep
    at_stats = at_sort
    stats = mem.at("p_stats", [TT, NT, 2, 6], F32, at_stats)
    mv = mem.at("p_mv", [TT, NT, 2], F32, at_stats + 512)
    std = mem.at("p_std", [TT, NT], F32, at_stats + 640)
    rstd = mem.at("p_rstd", [TT, NT], F32, at_stats + 704)
    eps = mem.at("p_eps", [TT, 1], F32, at_stats + 768)
    tmp = mem.next("p_tmp", [EP, EJ], F32)
    zero16 = mem.next("p_zero16", [EP, NC], F16)
    mx = mem.next("p_mx", [EP, 2], F32)

    with ExitStack() as ctx:
        def sem(name):
            return ctx.enter_context(nc.semaphore("p_" + name))

        ring = ctx.enter_context(nc.psum_tensor("p_ring", [P, 4, HC], F32))
        ps_t = ctx.enter_context(nc.psum_tensor("p_ps_t", [P, 4, HC], F32))
        ps_src, ps_dst, ps_cnt, ps_base = (ps_t[:, i, :] for i in range(4))
        x_landed = [sem(f"x_landed{i}") for i in range(5)]
        w_landed = [sem(f"w_landed{s}") for s in range(2)]
        bias_landed = [sem(f"bias_landed{s}") for s in range(2)]
        bqk_landed, edges_landed = sem("bqk_landed"), sem("edges_landed")
        consts, pconst = sem("consts"), sem("pconst")
        w_hi, w_lo = sem("w_hi"), sem("w_lo")
        var_ready, std_ready = sem("var_ready"), sem("std_ready")
        xn_ready, h16_ready, l16_ready = sem("xn_ready"), sem("h16_ready"), sem("l16_ready")
        tr_done, xT_hi_ready, xT_lo_ready = sem("tr_done"), sem("xT_hi_ready"), sem("xT_lo_ready")
        xn_stored = sem("xn_stored")
        hl_stored = [sem(f"hl_stored{s}") for s in range(2)]
        gemm_done, qk_evac, tm_evac = sem("gemm_done"), sem("qk_evac"), sem("tm_evac")
        stored = [sem(f"stored{s}") for s in range(4)]
        pad_zero, pad_stored = sem("pad_zero"), sem("pad_stored")
        dve_step = sem("dve_step")
        tot_ready, base_ready, base_read = sem("tot_ready"), sem("base_ready"), sem("base_read")
        job_ready, job_used, table_done = sem("job_ready"), sem("job_used"), sem("table_done")
        block = ctx.enter_context(nc.Block())

        x_rows = io["x"].rearrange("(t p) d -> p t d", p=TT)
        xn_rows = io["xn"].rearrange("(t p) d -> p t d", p=TT)
        QK_CH = [(0, 4 * TT), (4 * TT, 4 * TT), (8 * TT, 2 * TT)]

        ROOT_BEFORE = {1: 1, 4: 2, 5: 3, 7: 4}

        def turned(t):
            return ps_t[:, 2 * (t % 2):2 * (t % 2) + 2, 0:4 * TT].rearrange("p b (k t) -> p b k t", t=TT)

        @block.sync
        def _(sp):
            for i in range(NT // 2):
                sp.dma_start(x_all[:, 2 * i:2 * i + 2, :], x_rows[:, 2 * i:2 * i + 2, :]).then_inc(x_landed[i], 16)
                if i == 1:
                    sp.dma_start(raw[0][:, :, :], io["w"][0]).then_inc(w_landed[0], 16)
            def store_xn(i):
                sp.wait_ge(xn_ready, 2 * i + 2)
                sp.dma_start(xn_rows[:, 2 * i:2 * i + 2, :], x_all[:, 2 * i:2 * i + 2, :]).then_inc(xn_stored, 16)

            def store_rows(t):
                sp.wait_ge(l16_ready, t + 1)
                sp.dma_start(io["rows"][t * TT:(t + 1) * TT, :], hl[t % 2][:, :]).then_inc(hl_stored[t % 2], 16)

            for i in range(3):
                store_xn(i)
            store_rows(0)
            store_xn(3)
            for t in range(1, 4):
                store_rows(t)
            store_xn(4)
            sp.wait_ge(xn_stored, 16 * NT // 2)
            sp.wait_ge(xT_lo_ready, 4)
            sp.wait_ge(l16_ready, 4)
            for s in range(1, STEP_REL):
                if s >= 2:
                    sp.wait_ge(w_lo, 4 * (s - 1))
                sp.dma_start(raw[s % 2][:, :, :], io["w"][s]).then_inc(w_landed[s % 2], 16)
                if s == 1:
                    for t in range(4, NT):
                        store_rows(t)
                if s >= STEP_TM:
                    m = s - STEP_TM
                    if m == 0:
                        sp.wait_ge(pad_stored, 48)
                    if m >= 2:
                        sp.wait_ge(tm_evac, 4 + NT * (m - 1))
                    sp.dma_start(bias_bc[m % 2][:, :], io["bias_tm"][m:m + 1, :].to_broadcast([TT, HC])
                                 ).then_inc(bias_landed[m % 2], 16)

        def split_hi(slot, sem_val):
            nc.scalar.wait_ge(w_landed[slot], sem_val)
            for c in range(4):
                nc.scalar.activation(whi[slot][:, 2 * c:2 * c + 2, :], raw[slot][:, 2 * c:2 * c + 2, :],
                                     ACT.Copy).then_inc(w_hi, 1)

        def split_lo_part(s, slot, c):
            nc.vector.wait_ge(w_hi, 4 * s + (c + 1))
            nc.vector.tensor_tensor(wlo[slot][:, 2 * c:2 * c + 2, :], raw[slot][:, 2 * c:2 * c + 2, :],
                                    whi[slot][:, 2 * c:2 * c + 2, :].bitcast(F32), ALU.subtract
                                    ).then_inc(w_lo, 1)

        def split_lo(s, slot):
            for c in range(4):
                split_lo_part(s, slot, c)

        @block.gpsimd
        def _(pool):
            pool.dma_start(bias_qk[:, :, :], io["bias_qk"]).then_inc(bqk_landed, 16)
            pool.iota(k["iota16"][:, :], [[1, 256]], base=0, channel_multiplier=0,
                      allow_small_or_imprecise_dtypes=True).then_inc(pconst, 1)
            pool.iota(thr[:, :], [[CAP * P, 56]], base=0, channel_multiplier=0,
                      allow_small_or_imprecise_dtypes=True).then_inc(pconst, 1)
            pool.memset(k["ident"][:, :], 0.0).then_inc(pconst, 1)
            pool.memset(below[:, :], 1.0).then_inc(pconst, 1)
            pool.memset(ones16[:, :], 1.0).then_inc(pconst, 1)
            pool.memset(zero16[:, :], 0.0).then_inc(pconst, 1)
            pool.memset(pads[:, :], 0.0).then_inc(pad_zero, 1)
            pool.wait_ge(pconst, 6)
            pool.affine_select(out=k["ident"][:, :], in_=k["ident"][:, :], compare_op=ALU.not_equal, fill=1.0, base=0,
                               pattern=[[-1, P]], channel_multiplier=1).then_inc(consts, 1)
            pool.affine_select(out=below[:, :], in_=below[:, :], compare_op=ALU.is_ge, fill=0.0, base=-1,
                               pattern=[[1, EP]], channel_multiplier=-1).then_inc(consts, 1)
            pool.wait_ge(pad_zero, 1)
            pad = NPAD - N
            pool.dma_start(io["qkT"].rearrange("(b p) t -> p b t", p=P)[:, :, N:NPAD],
                           pads[:, 0:2 * KB * pad].rearrange("p (b t) -> p b t", t=pad)).then_inc(pad_stored, 16)
            for c in range(2):
                pool.dma_start(io["tm"][N:NPAD, c * HC:(c + 1) * HC], pads[0:pad, :]).then_inc(pad_stored, 16)
            with pool.Fori(0, 2) as m:
                for u in range(24):
                    h, c, dd = u // 12, u % 12 // 4, u % 4
                    c0, cn = QK_CH[c]
                    pool.wait_ge(qk_evac, 24 * m + (u + 5))
                    pool.dma_start(io["qkT"][bass.ds(m * D + (4 * h + dd) * P, P), c0:c0 + cn],
                                   stage[u % 4][:, 0:cn]).then_inc(stored[u % 4], 16)
            with pool.Fori(0, 3) as m:
                for u in range(2 * NT):
                    h, t = divmod(u, NT)
                    pool.wait_ge(tm_evac, 2 * NT * m + (u + 5))
                    pool.dma_start(io["tm"][bass.ds(m * NPAD + t * TT, TT), h * HC:(h + 1) * HC],
                                   stage[u % 4][0:TT, :]).then_inc(stored[u % 4], 16)
            for s in range(4):
                pool.wait_ge(stored[s], 16 * ((48 + 60) // 4))

        @block.scalar
        def _(act):
            act.dma_start(edges[:, :, :], io["edges"]).then_inc(edges_landed, 16)
            act.sem_inc(qk_evac, 4)

            def root(p):
                act.wait_ge(var_ready, p + 1)
                act.activation(std[:, 2 * p:2 * p + 2], mv[:, 2 * p:2 * p + 2, 1], ACT.Sqrt, bias=eps[:, :]
                               ).then_inc(std_ready, 1)

            def evacuate(m, u):
                c, dd = u % 12 // 4, u % 4
                cn = QK_CH[c][1]
                act.wait_ge(gemm_done, 24 * m + (u + 1))
                if 24 * m + u >= 4:
                    act.wait_ge(stored[u % 4], 16 * (6 * m + u // 4))
                act.activation(stage[u % 4][:, 0:cn], ring[:, u % 4, 0:cn], ACT.Identity,
                               bias=bias_qk[:, m, 4 * (u // 12) + dd:4 * (u // 12) + dd + 1]).then_inc(qk_evac, 1)

            def rows_high(t):
                act.wait_ge(xn_ready, t + 1)
                if t >= 2:
                    act.wait_ge(hl_stored[t % 2], 16 * (t // 2))
                act.activation(hl[t % 2][:, 0:D], x_all[:, t, :], ACT.Copy, scale=XS).then_inc(h16_ready, 1)

            root(0)
            for t in range(NT):
                if t in ROOT_BEFORE:
                    root(ROOT_BEFORE[t])
                act.wait_ge(tr_done, t + 1)
                act.activation(xT_hi[:, :, t * TT:(t + 1) * TT].rearrange("p (b k) t -> p b k t", b=2), turned(t),
                               ACT.Copy).then_inc(xT_hi_ready, 1)
                if t == 3:
                    split_hi(0, 16)
                if t == 4:
                    act.wait_ge(bqk_landed, 16)
                if t >= 5:
                    evacuate(0, t - 5)
                if t >= 4:
                    rows_high(t - 4)
            for t in range(NT - 4, NT):
                rows_high(t)
                evacuate(0, t - 1)
            act.wait_ge(l16_ready, 8)
            act.wait_ge(xn_stored, 16 * NT // 2)
            split_hi(1, 16)
            for m in range(2):
                for h in range(2):
                    for v in range(12):
                        u = 12 * h + v
                        if 24 * m + u >= NT - 1:
                            evacuate(m, u)
                    split_hi(h, 16 * m + 32)
            for s in range(STEP_TM + 2, STEP_REL):
                act.wait_ge(gemm_done, 48 + NT * (s - STEP_TM - 1))
                split_hi(s % 2, 16 * (s // 2 + 1))

        @block.vector
        def _(dve):
            dve.sem_inc(tm_evac, 4)
            ch = Chain(dve, dve_step)
            ch.add(dve.memset(eps[:, :], EPS))

            def statistics(p):
                dve.wait_ge(x_landed[p], 16)
                for t in (2 * p, 2 * p + 1):
                    for h in range(2):
                        ch.add(dve.bn_stats(stats[:, t, h, :], x_all[:, t, h * HC:(h + 1) * HC]))
                ch.wait()
                for t in (2 * p, 2 * p + 1):
                    last = dve.bn_aggr(mv[:, t, :], stats[:, t, :, :].rearrange("p a b -> p (a b)"))
                last.then_inc(var_ready, 1)
                dve.wait_ge(std_ready, p + 1)
                sl = slice(2 * p, 2 * p + 2)
                inverse_root(dve, ch, rstd[:, sl], std[:, sl], mv[:, sl, 1], EPS)

            def normalise(t):
                dve.tensor_scalar(x_all[:, t, :], x_all[:, t, :], mv[:, t, 0:1], rstd[:, t:t + 1],
                                  ALU.subtract, ALU.mult).then_inc(xn_ready, 1)

            def rows_low(t):
                dve.wait_ge(h16_ready, t + 1)
                dve.scalar_tensor_tensor(hl[t % 2][:, D:2 * D], x_all[:, t, :], XS, hl[t % 2][:, 0:D],
                                         ALU.mult, ALU.subtract).then_inc(l16_ready, 1)

            def low(t):
                dve.wait_ge(xT_hi_ready, t + 1)
                sl = slice(t * TT, (t + 1) * TT)
                dve.tensor_tensor(xT_lo[:, :, sl].rearrange("p (b k) t -> p b k t", b=2), turned(t),
                                  xT_hi[:, :, sl].bitcast(F32).rearrange("p (b k) t -> p b k t", b=2),
                                  ALU.subtract).then_inc(xT_lo_ready, 1)
                if t >= 4:
                    rows_low(t - 4)

            statistics(0)
            normalise(0)
            normalise(1)
            low(0)
            for t in (1, 5, 7):
                if t == 5:
                    low(3)
                    split_lo(0, 0)
                    statistics(2)
                    normalise(4)
                    normalise(5)
                    low(4)
                statistics((t + 1) // 2)
                normalise(t + 1)
                low(t)
                normalise(t + 2)
                low(t + 1)
            low(9)
            for t in range(NT - 4, NT):
                rows_low(t)
            for s in range(2):
                dve.wait_ge(hl_stored[s], 16 * (NT // 2))
            split_lo(1, 1)

            dve.wait_ge(edges_landed, 16)
            dve.wait_ge(pconst, 2)
            srcf, dl, dl1, bkt, lo, hi, rank = (k[n] for n in ("srcf", "dl", "dl1", "bkt", "lo", "hi", "rank"))
            ch.link(dve.tensor_scalar(srcf[:, :], edges[:, 0, :], 0.0, float(N - 1), ALU.max, ALU.min))
            ch.add(dve.tensor_copy(dl[:, :], edges[:, 1, :]))
            ch.add(dve.tensor_copy(bkt[:, :], edges[:, 2, :]))
            ch.link(dve.memset(tmp[:, :], 0.0))
            for w in range(1, NT):
                ch.link(dve.scalar_tensor_tensor(tmp[:, :], dl[:, :], float(w * TT), tmp[:, :], ALU.is_ge, ALU.add))
            ch.add(dve.scalar_tensor_tensor(dl[:, :], tmp[:, :], float(-TT), dl[:, :], ALU.mult, ALU.add))
            ch.link(dve.scalar_tensor_tensor(bkt[:, :], bkt[:, :], float(NT), tmp[:, :], ALU.mult, ALU.add))
            ch.add(dve.tensor_scalar(dl1[:, :], dl[:, :], 1.0, None, ALU.add))
            dve.wait_ge(xn_ready, NT)
            ch.add(dve.memset(reset[:, :, :], 1.0))
            ch.add(dve.memset(rank[:, :], 0.0))
            ch.wait()
            ch.link(dve.memset(reset[:, :, 0:1], 0.0))

            def one_hot_chunk(c):
                return dve.tensor_tensor(oh_c[:, :, :], bkt[:, :].unsqueeze(1).to_broadcast([EP, CB, EJ]),
                                         k["iota16"][0:EP, bass.ds(c * CB, CB)].unsqueeze(2).to_broadcast([EP, CB, EJ]),
                                         ALU.is_equal)

            def count_chunks(c0, c1):
                n0 = ch.n
                with dve.Fori(c0, c1) as c:
                    lp = Chain(dve, dve_step, base=2 * c + (n0 - 2 * c0))
                    lp.link(one_hot_chunk(c))
                    lp.link(dve.reduce_sum(tot[:, bass.ds(c * CB, CB)], oh_c[:, :, :], AX.X))
                ch.n += 2 * (c1 - c0)

            count_chunks(0, 3 * NCH // 4)
            split_lo(2, 0)
            count_chunks(3 * NCH // 4, NCH)
            dve.tensor_copy(tot16[:, :], tot[:, :]).then_inc(tot_ready, 1)
            dve.wait_ge(base_ready, 1)
            ch.add(dve.tensor_scalar(base1[:, :], ps_base[0:EP, 0:NB], 1.0, None, ALU.subtract))
            ch.link(dve.reduce_max(mx[:, 0:1], ps_cnt[0:EP, 0:NB], AX.X))
            ch.link(dve.tensor_scalar(thr[:, :], thr[:, :], mx[:, 0:1], None, ALU.is_lt))
            ch.link(dve.reduce_sum(mx[:, 1:2], thr[:, 1:56], AX.X))
            ch.link(dve.tensor_scalar(k["rounds"][0:EP, :], mx[:, 1:2], 1.0, None, ALU.add))

            def rank_chunks(c0, c1):
                n0 = ch.n
                with dve.Fori(c0, c1) as c:
                    lp = Chain(dve, dve_step, base=6 * c + (n0 - 6 * c0))
                    lp.link(one_hot_chunk(c))
                    lp.link(dve.tensor_tensor_scan(scan_c[:, :, :].rearrange("p b j -> p (b j)"),
                                                   reset[:, :, :].rearrange("p b j -> p (b j)"),
                                                   oh_c[:, :, :].rearrange("p b j -> p (b j)"), 0.0, ALU.mult, ALU.add))
                    lp.link(dve.tensor_tensor(scan_c[:, :, :], scan_c[:, :, :],
                                              base1[:, bass.ds(c * CB, CB)].unsqueeze(2).to_broadcast([EP, CB, EJ]),
                                              ALU.add))
                    lp.link(dve.tensor_tensor(scan_c[:, :, :], scan_c[:, :, :], oh_c[:, :, :], ALU.mult))
                    lp.link(dve.reduce_sum(tmp[:, :], scan_c[:, :, :].rearrange("p b j -> p j b"), AX.X))
                    lp.link(dve.tensor_tensor(rank[:, :], rank[:, :], tmp[:, :], ALU.add))
                ch.n += 6 * (c1 - c0)

            rank_chunks(0, NCH // 3)
            split_lo(3, 1)
            rank_chunks(NCH // 3, 2 * NCH // 3 + 1)
            split_lo(4, 0)
            rank_chunks(2 * NCH // 3 + 1, NCH)
            slot_of_rank(dve, ch, k, tmp)

            dve.sem_inc(job_used, 2)

            def token_major(m, first, last):
                for h in range(2):
                    dve.wait_ge(bias_landed[h], 16 * m + 16)
                    for t in range(NT):
                        u = NT * h + t
                        v = u - JU0
                        if not first or v >= 0:
                            dve.wait_ge(job_used, 20 * m + (v + 1))
                            for jj in range(JU):
                                o = one_hots(dve, k, job[v % 2][:, jj, :], 20 * JU * m + (JU * v + jj))
                            o.then_inc(job_ready, 1)
                        dve.wait_ge(gemm_done, 20 * m + (48 + u + 1))
                        dve.wait_ge(stored[u % 4], 80 * m + (16 * (u // 4) + 16 * 12))
                        dve.tensor_tensor(stage[u % 4][0:TT, :], ring[0:TT, u % 4, :], bias_bc[h][:, :], ALU.add
                                          ).then_inc(tm_evac, 1)
                        if t < 4 and not (last and h == 1):
                            split_lo_part(2 * m + (STEP_TM + 1 + h), 1 - h, t)

            token_major(0, True, False)
            with dve.Fori(1, 2) as m:
                token_major(m, False, False)
            token_major(2, False, True)
            dve.wait_ge(table_done, 1)
            read_table(dve, k, ps_src, ps_dst)
            dve.tensor_scalar(k["rc"][:, :], ps_cnt[0:TT, 0:NB], 1.0, None, ALU.max).then_inc(base_read, 1)
            dve.wait_ge(base_read, 1)
            dve.reciprocal(k["rc"][:, :], k["rc"][:, :])

        @block.tensor
        def _(pe):
            pe.wait_ge(consts, 2)

            def turn(t):
                pe.wait_ge(xn_ready, t + 1)
                if t >= 2:
                    pe.wait_ge(xT_lo_ready, t - 1)
                for kb in range(KB):
                    o = nc.tensor.transpose(ps_t[:, 2 * (t % 2) + kb // 4, (kb % 4) * TT:(kb % 4 + 1) * TT],
                                            x_all[:, t, kb * P:(kb + 1) * P], k["ident"][0:TT, 0:TT])
                o.then_inc(tr_done, 1)

            def feature_major(m, u):
                h, c, dd = u // 12, u % 12 // 4, u % 4
                c0, cn = QK_CH[c]
                if m == 0 and h == 0 and dd == 0:
                    pe.wait_ge(xT_lo_ready, (c0 + cn) // TT)
                pe.wait_ge(qk_evac, 24 * m + (u + 1))
                for kb in range(KB):
                    if u % 12 == 0 and kb % 2 == 0:
                        pe.wait_ge(w_lo, 8 * m + (4 * h + kb // 2 + 1))
                    w = slice(dd * P, (dd + 1) * P)
                    o = mm3(nc, ring[:, u % 4, 0:cn], (whi[h][:, kb, w], wlo[h][:, kb, w]),
                            (xT_hi[:, kb, c0:c0 + cn], xT_lo[:, kb, c0:c0 + cn]), kb == 0, kb == KB - 1)
                o.then_inc(gemm_done, 1)

            for t in range(4):
                turn(t)
            for t in range(4, NT):
                feature_major(0, t - 4)
                turn(t)
            for m in range(2):
                for u in range(24):
                    if 24 * m + u >= NT - 4:
                        feature_major(m, u)
                    if (m, u) == (1, 1):
                        pe.wait_ge(tot_ready, 1)
                        nc.tensor.matmul(ps_cnt[0:EP, 0:NB], ones16[:, 0:EP], tot16[:, :], start=True, stop=True)
                        nc.tensor.matmul(ps_base[0:EP, 0:NB], below[:, :], tot16[:, :], start=True, stop=True
                                         ).then_inc(base_ready, 1)
            pe.wait_ge(qk_evac, 48 + 4)

            def table(out, a, b, start=False, stop=False):
                return nc.tensor.matmul(out, a, b, start=start, stop=stop)

            tables = ((ps_src[0:P, 0:NC], P), (ps_dst[0:P, 0:NC], P), (ps_cnt[0:TT, 0:NB], TT))
            pe.wait_ge(w_lo, 16 + 4)
            for o_, n_ in tables:
                table(o_, zero16[:, 0:n_], zero16[:, 0:o_.shape[1]], start=True)

            def token_major(m, first):
                for h in range(2):
                    for t in range(NT):
                        u = NT * h + t
                        pe.wait_ge(tm_evac, 20 * m + (u + 1))
                        for kb in range(KB):
                            if t == 0 and kb % 2 == 0:
                                pe.wait_ge(w_lo, 8 * m + (16 + 4 * h + kb // 2 + 1))
                            tk = slice(t * TT, (t + 1) * TT)
                            o = mm3(nc, ring[0:TT, u % 4, :], (xT_hi[:, kb, tk], xT_lo[:, kb, tk]),
                                    (whi[h][:, kb, :], wlo[h][:, kb, :]), kb == 0, kb == KB - 1)
                        o.then_inc(gemm_done, 1)
                        v = u - JU0
                        if not first or v >= 0:
                            pe.wait_ge(job_ready, 20 * m + (v + 1))
                            for jj in range(JU):
                                o = table_products(nc, job[v % 2][:, jj, :], ps_src, ps_dst, ps_cnt)
                            o.then_inc(job_used, 1)

            token_major(0, True)
            with pe.Fori(1, 3) as m:
                token_major(m, False)
            for o_, n_ in tables:
                o = table(o_, zero16[:, 0:n_], zero16[:, 0:o_.shape[1]], stop=True)
            o.then_inc(table_done, 1)


def phase_attend(nc, mem, io, k):
    CH, G, NCK = P, 16, NPAD // P
    TG = CH // G
    half = KB * HC * 4
    feat = [[mem.at(f"a_feat{s}{j}", [P, 2, NH, CH], F32, (4 * s + j) * half) for j in range(2)] for s in range(2)]
    mem.cursor = 6 * half
    qk = [[mem.next(f"a_qk{s}{j}", [P, KB, CH], F32) for j in range(2)] for s in range(2)]
    qk_hi = [[mem.next(f"a_qk_hi{s}{j}", [P, KB, CH], F32R) for j in range(2)] for s in range(2)]
    qk_lo = [[mem.next(f"a_qk_lo{s}{j}", [P, KB, CH], F32R) for j in range(2)] for s in range(2)]
    v2 = [mem.next(f"a_v{s}", [P, G, 2, HD], F32) for s in range(2)]
    msk = [mem.next(f"a_msk{s}", [P, 4, P], F32) for s in range(4)]
    mask = mem.next("a_mask", [P, P], F32)
    rfT = mem.next("a_rfT", [P, M], F32)
    rf_hi, rf_lo = mem.next("a_rf_hi", [P, M], F32R), mem.next("a_rf_lo", [P, M], F32R)
    mx = [mem.next(f"a_mx{s}", [P, 4], F32) for s in range(2)]
    sm = [mem.next(f"a_sm{s}", [P, 4], F32) for s in range(2)]
    assert mem.cursor <= k["start"]
    mem.cursor = k["start"] + k["bytes"]
    prob = [mem.next(f"a_prob{s}", [P, 4, P], F32) for s in range(4)]
    probT = [mem.next(f"a_probT{s}", [P, 4 * P], F32) for s in range(2)]
    att = [mem.next(f"a_att{s}", [P, KB, CH], F32) for s in range(2)]

    with ExitStack() as ctx:
        def sem(name):
            return ctx.enter_context(nc.semaphore("a_" + name))

        ps_f = ctx.enter_context(nc.psum_tensor("a_ps_f", [P, 2, HC], F32))
        ps_s = ctx.enter_context(nc.psum_tensor("a_ps_s", [P, 2, HC], F32))
        ps_t = ctx.enter_context(nc.psum_tensor("a_ps_t", [P, 2, HC], F32))
        ps_o = ctx.enter_context(nc.psum_tensor("a_ps_o", [P, 2, HC], F32))
        landed = [[sem(f"landed{s}{j}") for j in range(4)] for s in range(2)]
        rf_landed, mask_step = sem("rf_landed"), sem("mask_step")
        rf_hi_ready, rf_lo_ready = sem("rf_hi_ready"), sem("rf_lo_ready")
        qk_hi_ready, qk_lo_ready = sem("qk_hi_ready"), sem("qk_lo_ready")
        feat_done, feat_evac = sem("feat_done"), sem("feat_evac")
        s_done, s_read, msk_ready, exp_done, p_ready = (sem(n) for n in
                                                        ("s_done", "s_read", "msk_ready", "exp_done", "p_ready"))
        inv_ready = sem("inv_ready")
        t_done, t_evac, o_done, o_evac = (sem(n) for n in ("t_done", "t_evac", "o_done", "o_evac"))
        att_stored = [sem(f"att_stored{s}") for s in range(2)]
        att_free = sem("att_free")
        dve_step = sem("dve_step")
        block = ctx.enter_context(nc.Block())

        qk_rows = [io["qkT"][j * D:(j + 1) * D, :].rearrange("(b p) t -> p b t", p=P) for j in range(2)]
        v_rows = io["tm"][0:NPAD, :].rearrange("t (h d) -> h t d", d=HD)
        att_rows = io["attnT"].rearrange("(b p) t -> p b t", p=P)

        def load_qk(sp, s, c):
            for j in range(2):
                sp.dma_start(qk[s][j][:, :, :], qk_rows[j][:, :, bass.ds(c * CH, CH)]).then_inc(landed[s][j], 16)

        def load_v(sp, s, c):
            for j in range(2):
                for t in range(TG):
                    sp.dma_start(v2[s][t::TG, :, j, :], v_rows[:, bass.ds(c * CH + t * G, G), :]).then_inc(landed[s][2 + j], 16)

        @block.sync
        def _(sp):
            for j in range(2):
                sp.dma_start(rfT[j * HD:(j + 1) * HD, :], io["rfT"]).then_inc(rf_landed, 16)
            for s in range(2):
                load_qk(sp, s, s)
            for s in range(2):
                load_v(sp, s, s)

            def chunk(i, s, last):
                if not last:
                    sp.wait_ge(qk_lo_ready, 4 * i + (2 * s + 2))
                    load_qk(sp, s, 2 * i + (s + 2))
                    sp.wait_ge(o_done, 8 * i + (4 * s + 4 + 2))
                    load_v(sp, s, 2 * i + (s + 2))
                sp.wait_ge(o_evac, 8 * i + (4 * s + 4 + 2))
                sp.dma_start(att_rows[:, :, bass.ds((2 * i + s) * CH, CH)], att[s][:, :, :]
                             ).then_inc(att_stored[s], 16)
                sp.wait_ge(att_stored[s], 16 * i + 16)
                sp.sem_inc(att_free, 1)

            with sp.Fori(0, NCK // 2 - 1) as i:
                for s in range(2):
                    chunk(i, s, False)
            for h in range(2):
                sp.dma_start(k["raw"][h][:, :, :], io["w"][STEP_REL + h]).then_inc(k["rel_landed"][h], 16)
            for s in range(2):
                chunk(NCK // 2 - 1, s, True)

        @block.gpsimd
        def _(pool):
            def split_low(i, s):
                for j in range(2):
                    pool.wait_ge(qk_hi_ready, 4 * i + (2 * s + j + 1))
                    pool.tensor_tensor(qk_lo[s][j][:, :, :], qk[s][j][:, :, :], qk_hi[s][j][:, :, :].bitcast(F32),
                                       ALU.subtract).then_inc(qk_lo_ready, 1)

            pool.memset(mask[:, :], NEG).then_inc(mask_step, 1)
            for h in range(NH):
                pool.wait_ge(mask_step, h + 1)
                pool.affine_select(out=mask[:, :].rearrange("p (h t) -> p h t", h=NH),
                                   in_=mask[:, :].rearrange("p (h t) -> p h t", h=NH),
                                   compare_op=ALU.not_equal, fill=0.0, base=-h * TG,
                                   pattern=[[0, NH], [-1, TG]], channel_multiplier=1).then_inc(mask_step, 1)

            def chunk(i, s, last):
                for b in range(4):
                    pool.wait_ge(inv_ready, 8 * i + (4 * s + b + 1))
                    pool.tensor_tensor(prob[b][:, :, :], prob[b][:, :, :],
                                       sm[b % 2][:, :].unsqueeze(2).to_broadcast([P, 4, P]), ALU.mult
                                       ).then_inc(p_ready, 1)
                if not last:
                    split_low(i + 1, s)

            pool.wait_ge(qk_lo_ready, 2)
            split_low(0, 1)
            with pool.Fori(0, NCK // 2 - 1) as i:
                for s in range(2):
                    chunk(i, s, False)
            for s in range(2):
                chunk(NCK // 2 - 1, s, True)

        UNITS = [(j, mh, kg, par) for j in range(2) for mh in range(2) for kg in range(2) for par in range(2)]

        @block.scalar
        def _(act):
            act.sem_inc(feat_evac, 2)
            act.sem_inc(t_evac, 2)
            act.sem_inc(exp_done, 4)

            act.wait_ge(rf_landed, 32)
            act.activation(rf_hi[:, :], rfT[:, :], ACT.Copy).then_inc(rf_hi_ready, 1)

            def split_high(i, s):
                for j in range(2):
                    act.wait_ge(landed[s][j], 16 * i + 16)
                    act.activation(qk_hi[s][j][:, :, :], qk[s][j][:, :, :], ACT.Copy).then_inc(qk_hi_ready, 1)

            def features(i, s, f0, f1):
                for f in range(f0, f1):
                    j, mh, kg, par = UNITS[f]
                    act.wait_ge(feat_done, 32 * i + (16 * s + f + 1))
                    out = feat[s][j][:, mh, :, :].rearrange("p (g i r) t -> p g r i t", g=2, r=2)[:, kg, par, :, :]
                    act.activation(out, ps_f[:, f % 2, :].rearrange("p (i t) -> p i t", i=4), ACT.Relu
                                   ).then_inc(feat_evac, 1)

            def chunk(i, s, last, peeled=False):
                def exponential(b):
                    act.wait_ge(msk_ready, 8 * i + (4 * s + b + 1))
                    act.wait_ge(t_done, 8 * i + (4 * s + b + 1))
                    act.activation(prob[b][:, :, :], msk[b][:, :, :], ACT.Exp, scale=HD ** -0.5
                                   ).then_inc(exp_done, 1)

                def transposed(b):
                    act.wait_ge(t_done, 8 * i + (4 * s + b + 1 + 4))
                    act.wait_ge(o_done, 8 * i + (4 * s + b + 1))
                    act.activation(probT[b % 2][:, :], ps_t[:, b % 2, :], ACT.Copy).then_inc(t_evac, 1)

                def next_features(f0, f1):
                    if not last:
                        features(i + s, 1 - s, f0, f1)

                for b in range(4):
                    next_features(2 * b, 2 * b + 2)
                    exponential(b)
                next_features(8, 11)
                transposed(0)
                next_features(11, 14)
                transposed(1)
                next_features(14, 16)
                if not peeled:
                    split_high(i + 1, s)
                transposed(2)
                transposed(3)

            split_high(0, 0)
            split_high(0, 1)
            features(0, 0, 0, 16)
            with act.Fori(0, NCK // 2 - 1) as i:
                for s in range(2):
                    chunk(i, s, False)
            for s in range(2):
                chunk(NCK // 2 - 1, s, s == 1, True)

        @block.vector
        def _(dve):
            dve.sem_inc(s_read, 2)
            dve.sem_inc(o_evac, 2)

            dve.wait_ge(rf_hi_ready, 1)
            dve.tensor_tensor(rf_lo[:, :], rfT[:, :], rf_hi[:, :].bitcast(F32), ALU.subtract).then_inc(rf_lo_ready, 1)
            for j in range(2):
                dve.wait_ge(qk_hi_ready, j + 1)
                dve.tensor_tensor(qk_lo[0][j][:, :, :], qk[0][j][:, :, :], qk_hi[0][j][:, :, :].bitcast(F32),
                                  ALU.subtract).then_inc(qk_lo_ready, 1)
            dve.wait_ge(mask_step, NH + 1)

            def chunk(i, s):
                ch = Chain(dve, dve_step, base=(i * 2 + s) * 8)

                def shift(b):
                    dve.wait_ge(s_done, 8 * i + (4 * s + b + 1))
                    dve.wait_ge(exp_done, 8 * i + (4 * s + b + 1))
                    dve.tensor_tensor(msk[b][:, :, :], ps_s[:, b % 2, :].rearrange("p (g c) -> p g c", g=4),
                                      mask[:, :].unsqueeze(1).to_broadcast([P, 4, P]), ALU.add).then_inc(s_read, 1)
                    dve.wait_ge(s_read, 8 * i + (4 * s + b + 3))
                    ch.link(dve.reduce_max(mx[b % 2][:, :], msk[b][:, :, :], AX.X))
                    dve.tensor_tensor(msk[b][:, :, :], msk[b][:, :, :],
                                      mx[b % 2][:, :].unsqueeze(2).to_broadcast([P, 4, P]), ALU.subtract
                                      ).then_inc(msk_ready, 1)

                def total(b):
                    dve.wait_ge(exp_done, 8 * i + (4 * s + b + 1 + 4))
                    dve.wait_ge(p_ready, 8 * i + (4 * s + b + 1))
                    ch.link(dve.reduce_sum(sm[b % 2][:, :], prob[b][:, :, :], AX.X))
                    dve.reciprocal(sm[b % 2][:, :], sm[b % 2][:, :]).then_inc(inv_ready, 1)

                shift(0)
                shift(1)
                total(0)
                shift(2)
                total(1)
                shift(3)
                total(2)
                total(3)
                assert ch.n == 8
                dve.wait_ge(att_free, 2 * i + (s + 1))
                for b in range(4):
                    dve.wait_ge(o_done, 8 * i + (4 * s + b + 3))
                    for r in range(2):
                        src = ps_o[:, b % 2, :].rearrange("p (n a r t) -> p r a t n", n=4, a=KB, r=2)
                        rows = slice(r * HD, (r + 1) * HD)
                        o = dve.tensor_copy(att[s][rows, :, :].rearrange("p a (t g) -> p a t g", g=G)[:, :, :, 4 * b:4 * b + 4],
                                            src[rows, r, :, :, :])
                    o.then_inc(o_evac, 1)

            dve.sem_inc(att_free, 2)
            dve.sem_inc(p_ready, 2)
            with dve.Fori(0, NCK // 2) as i:
                for s in range(2):
                    chunk(i, s)

        @block.tensor
        def _(pe):
            pe.sem_inc(t_done, 4)
            pe.sem_inc(o_done, 2)
            pe.wait_ge(rf_lo_ready, 1)

            def features(i, s, f0, f1):
                for f in range(f0, f1):
                    j, mh, kg, par = UNITS[f]
                    if f % 8 == 0:
                        pe.wait_ge(qk_lo_ready, 4 * i + (2 * s + f // 8 + 1))
                    pe.wait_ge(feat_evac, 32 * i + (16 * s + f + 1))
                    rows, cols, heads = slice(par * HD, (par + 1) * HD), slice(mh * P, (mh + 1) * P), slice(4 * kg, 4 * kg + 4)
                    mm3(nc, ps_f[:, f % 2, :], (rf_hi[rows, cols], rf_lo[rows, cols]),
                        tuple(part[s][j][rows, heads, :].rearrange("p a t -> p (a t)") for part in (qk_hi, qk_lo)),
                        True, True).then_inc(feat_done, 1)

            def chunk(i, s, last):
                pe.wait_ge(feat_evac, 32 * i + (16 * s + 16 + 2))
                def score(b):
                    pe.wait_ge(s_read, 8 * i + (4 * s + b + 1))
                    for n in range(4):
                        for mh in range(2):
                            qf, kf = (feat[s][j][:, mh, :, :].rearrange("p h t -> p (h t)")[:, 4 * b + n::G] for j in range(2))
                            o = nc.tensor.matmul(ps_s[:, b % 2, n * P:(n + 1) * P], qf, kf, start=(mh == 0), stop=(mh == 1))
                    o.then_inc(s_done, 1)

                def turn(b):
                    pe.wait_ge(p_ready, 8 * i + (4 * s + b + 3))
                    pe.wait_ge(t_evac, 8 * i + (4 * s + b + 1))
                    for n in range(4):
                        o = nc.tensor.transpose(ps_t[:, b % 2, n * P:(n + 1) * P], prob[b][:, n, :],
                                                k["ident"][:, :])
                    o.then_inc(t_done, 1)

                def weigh(b):
                    if b == 0:
                        for j in range(2):
                            pe.wait_ge(landed[s][2 + j], 16 * TG * i + 16 * TG)
                    pe.wait_ge(t_evac, 8 * i + (4 * s + b + 3))
                    pe.wait_ge(o_evac, 8 * i + (4 * s + b + 1))
                    for n in range(4):
                        o = nc.tensor.matmul(ps_o[:, b % 2, n * P:(n + 1) * P],
                                             v2[s][:, 4 * b + n, :, :].rearrange("p a d -> p (a d)"),
                                             probT[b % 2][:, n * P:(n + 1) * P], start=True, stop=True)
                    o.then_inc(o_done, 1)

                def next_features(f0, f1):
                    if not last:
                        features(i + s, 1 - s, f0, f1)

                score(0)
                score(1)
                next_features(0, 4)
                score(2)
                next_features(4, 6)
                score(3)
                next_features(6, 10)
                turn(0)
                next_features(10, 13)
                turn(1)
                next_features(13, 16)
                weigh(0)
                turn(2)
                weigh(1)
                turn(3)
                weigh(2)
                weigh(3)

            features(0, 0, 0, 16)
            with pe.Fori(0, NCK // 2 - 1) as i:
                for s in range(2):
                    chunk(i, s, False)
            for s in range(2):
                chunk(NCK // 2 - 1, s, s == 1)

def phase_relate(nc, mem, io, k):
    half = KB * HC * 4
    whi = [mem.at(f"r_whi{s}", [P, KB, HC], F32R, o) for s, o in enumerate((0, 4 * half))]
    wlo = [mem.at(f"r_wlo{s}", [P, KB, HC], F32R, o) for s, o in enumerate((half, 5 * half))]
    raw = k["raw"]
    mem.cursor = 6 * half
    u = mem.next("r_u", [TT, NT, D], F32)
    sT_hi = [mem.next(f"r_sT_hi{s}", [P, KB * TT], F32R) for s in range(2)]
    sT_lo = [mem.next(f"r_sT_lo{s}", [P, KB * TT], F32R) for s in range(2)]
    rows = [mem.next("r_rows0", [P, CAP, 2 * D], F16)]
    oh = [mem.next(f"r_oh{s}", [P, CAP, TT], F16) for s in range(2)]
    src = [mem.next(f"r_src{s}", [P, CAP], U32) for s in range(2)]
    job = [mem.next(f"r_job{s}", [EP, 704], F16) for s in range(2)]
    zero16 = mem.next("r_zero16", [EP, NC], F16)
    tmp = mem.next("r_tmp", [EP, EJ], F32)
    assert mem.cursor <= k["start"]
    mem.cursor = k["start"] + k["bytes"]
    rows.append(mem.next("r_rows1", [P, CAP, 2 * D], F16))
    NW = NB + 2
    MAXR = -(-EP * EJ // (CAP * P))

    with ExitStack() as ctx:
        def sem(name):
            return ctx.enter_context(nc.semaphore("r_" + name))

        ring = ctx.enter_context(nc.psum_tensor("r_ring", [P, 4, HC], F32))
        ps_a = [ctx.enter_context(nc.psum_tensor(f"r_ps_a{s}", [P, 2, HC], F32)) for s in range(2)]
        w_landed = k["rel_landed"]
        rows_landed = [sem(f"rows_landed{s}") for s in range(2)]
        u_landed = [sem(f"u_landed{g}") for g in range(NT // 2)]
        w_hi, w_lo = sem("w_hi"), sem("w_lo")
        slots_ready, sums_done, hi_ready, lo_ready = sem("slots_ready"), sem("sums_done"), sem("hi_ready"), sem("lo_ready")
        gemm_done, u_added = sem("gemm_done"), sem("u_added")
        dve_step, job_ready, job_used, table_done, table_read = (
            sem(n) for n in ("dve_step", "job_ready", "job_used", "table_done", "table_read"))
        waited = sem("waited")
        block = ctx.enter_context(nc.Block())
        w_rows = io["w"].rearrange("s p b n -> (s p) (b n)")

        def rounds_of(eng):
            return eng.value_load(k["rounds"][0:1, 0:1], min_val=1, max_val=MAXR)

        @block.sync
        def _(sp):
            u_rows = io["tm"][NPAD:NPAD + N, :].rearrange("(t p) d -> p t d", p=TT)
            for g in range(NT // 2):
                sp.wait_ge(hi_ready, g + 1)
                sp.dma_start(u[:, 2 * g:2 * g + 2, :], u_rows[:, 2 * g:2 * g + 2, :]).then_inc(u_landed[g], 16)

            def load(r, h):
                sp.dma_start(raw[h][:, :, :].rearrange("p b n -> p (b n)"),
                             w_rows[bass.ds((STEP_REL + h) * P + r * 2 * P, P), :]).then_inc(w_landed[h], 16)

            n = rounds_of(sp)
            with sp.Fori(0, n) as rd:
                with sp.Fori(0, R - 1) as r:
                    for h in range(2):
                        sp.wait_ge(w_lo, 64 * rd + 8 * r + (4 * h + 4))
                        load(r + 1, h)
                sp.wait_ge(w_lo, 64 * rd + 64)
                sp.sem_inc(waited, 1)
                with sp.If(rd < n - 1):
                    for h in range(2):
                        load(0, h)
            for h in range(2):
                sp.dma_start(raw[h][:, :, :], io["w"][STEP_GATE + h]).then_inc(k["gate_landed"][h], 16)

        @block.gpsimd
        def _(pool):
            n = rounds_of(pool)

            def gather(a, slot):
                pool.wait_ge(slots_ready, a + 1)
                pool.sem_inc(waited, 1)
                for c in range(CAP):
                    pool.indirect_dma_start(out=rows[slot][:, c, :], out_offset=None, in_=io["rows"],
                                            in_offset=bass.IndirectOffsetOnAxis(src[slot][:, c:c + 1], 0)
                                            ).then_inc(rows_landed[slot], 16)

            with pool.Fori(0, n) as rd:
                with pool.Fori(0, NW // 2) as i:
                    for s in range(2):
                        gather(NW * rd + 2 * i + s, s)

        @block.scalar
        def _(act):
            act.sem_inc(sums_done, 2)
            n = rounds_of(act)

            def high(a, g, slot):
                act.wait_ge(sums_done, a + 3)
                act.wait_ge(lo_ready, a + 1)
                act.wait_ge(gemm_done, g + 1)
                act.activation(sT_hi[slot][:, :].rearrange("p (b x) -> p b x", b=2), ps_a[slot][:, :, 0:4 * TT],
                               ACT.Copy, scale=1 / XS).then_inc(hi_ready, 1)

            with act.Fori(0, n) as rd:
                high(NW * rd, NB * rd, 0)
                with act.Fori(0, R) as r:
                    act.wait_ge(gemm_done, NB * rd + NT * r + 2)
                    for h in range(2):
                        act.wait_ge(w_landed[h], 128 * rd + 16 * r + 16)
                        for c in range(4):
                            act.activation(whi[h][:, 2 * c:2 * c + 2, :], raw[h][:, 2 * c:2 * c + 2, :], ACT.Copy
                                           ).then_inc(w_hi, 1)
                    for w in range(NT):
                        high(NW * rd + NT * r + (w + 1), NB * rd + NT * r + (w + 1), (w + 1) % 2)
                high(NW * rd + (NB + 1), NB * rd + (NB + 1), 1)

        @block.vector
        def _(dve):
            dve.sem_inc(lo_ready, 2)
            dve.sem_inc(u_added, 2)
            dve.memset(zero16[:, :], 0.0).then_inc(table_read, 1)
            n = rounds_of(dve)

            def slots(a, col, slot):
                dve.wait_ge(sums_done, a + 1)
                for c in range(CAP):
                    dve.tensor_scalar(oh[slot][:, c, :], k["iota16"][:, 0:TT], k["slot_dst"][:, bass.ds(col + c, 1)],
                                      None, ALU.is_equal)
                dve.tensor_scalar(src[slot][:, :], k["slot_src"][:, bass.ds(col, CAP)], 0.0, None, ALU.add
                                  ).then_inc(slots_ready, 1)

            def low(a, slot):
                dve.wait_ge(hi_ready, a + 1)
                dve.scalar_tensor_tensor(sT_lo[slot][:, :].rearrange("p (b x) -> p b x", b=2),
                                         ps_a[slot][:, :, 0:4 * TT], 1 / XS,
                                         sT_hi[slot][:, :].bitcast(F32).rearrange("p (b x) -> p b x", b=2),
                                         ALU.mult, ALU.subtract).then_inc(lo_ready, 1)

            with dve.Fori(0, n) as rd:
                for a in range(2):
                    slots(NW * rd + a, CAP * a, a)
                low(NW * rd, 0)
                with dve.Fori(0, R) as r:
                    for w in range(NT):
                        slots(NW * rd + NT * r + (w + 2), CAP * NT * r + CAP * (w + 2), w % 2)
                        if w == 0:
                            for h in range(2):
                                for c in range(4):
                                    dve.wait_ge(w_hi, 64 * rd + 8 * r + (4 * h + c + 1))
                                    dve.tensor_tensor(wlo[h][:, 2 * c:2 * c + 2, :], raw[h][:, 2 * c:2 * c + 2, :],
                                                      whi[h][:, 2 * c:2 * c + 2, :].bitcast(F32), ALU.subtract
                                                      ).then_inc(w_lo, 1)
                        low(NW * rd + NT * r + (w + 1), (w + 1) % 2)
                        dve.wait_ge(gemm_done, NB * rd + NT * r + (w + 3))
                        dve.wait_ge(u_landed[w // 2], 16)
                        b = 2 * (w % 2)
                        dve.scalar_tensor_tensor(u[:, w, :].rearrange("p (b x) -> p b x", b=2), ring[0:TT, b:b + 2, :],
                                                 k["rc"][:, bass.ds(NT * r + w, 1)],
                                                 u[:, w, :].rearrange("p (b x) -> p b x", b=2), ALU.mult, ALU.add
                                                 ).then_inc(u_added, 1)
                low(NW * rd + (NB + 1), 1)
                with dve.If(rd < n - 1):
                    ch = Chain(dve, dve_step, base=(4 + CAP - 2) * rd)
                    dve.wait_ge(sums_done, NW * rd + (NW + 2))
                    dve.wait_ge(lo_ready, NW * rd + (NW + 2))
                    ch.link(dve.tensor_scalar(k["rank"][:, :], k["rank"][:, :], float(-CAP * P), None, ALU.add))
                    slot_of_rank(dve, ch, k, tmp)
                    assert ch.n == 4 + CAP - 2
                    dve.sem_inc(waited, 1)
                    with dve.Fori(0, EJ // 2) as j:
                        for s in range(2):
                            dve.wait_ge(job_used, EJ * rd + 2 * j + (s + 1))
                            one_hots(dve, k, job[s][:, :], 2 * j + s).then_inc(job_ready, 1)
                    dve.wait_ge(table_done, rd + 1)
                    read_table(dve, k, ps_a[0][:, 0, :], ps_a[0][:, 1, :]).then_inc(table_read, 1)
                    dve.wait_ge(table_read, rd + 2)
                    dve.sem_inc(waited, 1)

        @block.tensor
        def _(pe):
            pe.sem_inc(gemm_done, 2)
            pe.sem_inc(job_used, 2)
            n = rounds_of(pe)
            pe.wait_ge(table_read, 1)

            def sums(a, landed, slot):
                pe.wait_ge(rows_landed[slot], landed)
                pe.wait_ge(slots_ready, a + 1)
                pe.wait_ge(lo_ready, a + 1)
                for kb in range(KB):
                    for c in range(CAP):
                        for part in range(2):
                            o = nc.tensor.matmul(ps_a[slot][:, kb // 4, (kb % 4) * TT:(kb % 4 + 1) * TT],
                                                 rows[slot][:, c, part * D + kb * P:part * D + (kb + 1) * P],
                                                 oh[slot][:, c, :], start=(c == 0 and part == 0),
                                                 stop=(c == CAP - 1 and part == 1))
                o.then_inc(sums_done, 1)

            LAND = 16 * CAP
            with pe.Fori(0, n) as rd:
                sums(NW * rd, LAND * (NW // 2) * rd + LAND, 0)
                with pe.Fori(0, R) as r:
                    for w in range(NT):
                        sums(NW * rd + NT * r + (w + 1),
                             LAND * (NW // 2) * rd + LAND * (NT // 2) * r + LAND * ((w + 1) // 2 + 1), (w + 1) % 2)
                        pe.wait_ge(lo_ready, NW * rd + NT * r + (w + 3))
                        pe.wait_ge(u_added, NB * rd + NT * r + (w + 1))
                        for h in range(2):
                            for kb in range(KB):
                                if w == 0 and kb % 2 == 0:
                                    pe.wait_ge(w_lo, 64 * rd + 8 * r + (4 * h + kb // 2 + 1))
                                tk = slice(kb * TT, (kb + 1) * TT)
                                o = mm3(nc, ring[0:TT, 2 * (w % 2) + h, :], (sT_hi[w % 2][:, tk], sT_lo[w % 2][:, tk]),
                                        (whi[h][:, kb, :], wlo[h][:, kb, :]), kb == 0, kb == KB - 1)
                        o.then_inc(gemm_done, 1)
                sums(NW * rd + (NB + 1), LAND * (NW // 2) * rd + LAND * (NW // 2), 1)
                with pe.If(rd < n - 1):
                    pe.wait_ge(lo_ready, NW * rd + (NW + 2))
                    banks = [ps_a[0][:, s, 0:NC] for s in range(2)]
                    for b in banks:
                        nc.tensor.matmul(b, zero16[:, 0:P], zero16[:, :], start=True, stop=False)
                    with pe.Fori(0, EJ // 2) as j:
                        for s in range(2):
                            pe.wait_ge(job_ready, EJ * rd + 2 * j + (s + 1))
                            table_products(nc, job[s][:, :], ps_a[0][:, 0, :], ps_a[0][:, 1, :], None
                                           ).then_inc(job_used, 1)
                    for b in banks:
                        o = nc.tensor.matmul(b, zero16[:, 0:P], zero16[:, :], start=False, stop=True)
                    o.then_inc(table_done, 1)
                    pe.wait_ge(table_read, rd + 2)
    return u


def phase_update(nc, mem, io, k):
    half = KB * HC * 4
    whi = [mem.at(f"g_whi{s}", [P, KB, HC], F32R, o) for s, o in enumerate((0, 4 * half))]
    wlo = [mem.at(f"g_wlo{s}", [P, KB, HC], F32R, o) for s, o in enumerate((half, 5 * half))]
    raw = k["raw"]
    u = k["u"]
    mem.cursor = 6 * half + 4 * NT * D
    aT_hi = [mem.next(f"g_aT_hi{s}", [P, KB * TT], F32R) for s in range(2)]
    aT_lo = [mem.next(f"g_aT_lo{s}", [P, KB * TT], F32R) for s in range(2)]
    attn = [mem.next(f"g_attn{s}", [P, KB, TT], F32) for s in range(2)]
    th = [mem.next(f"g_th{s}", [TT, D], F32) for s in range(2)]
    bo_bc = mem.next("g_bo_bc", [TT, D], F32)
    assert mem.cursor <= k["start"]
    mem.cursor = k["start"] + k["bytes"]
    xn_t, z0_t, xx_t = ([mem.next(f"g_{n}{s}", [TT, D], F32) for s in range(2)] for n in ("xn", "z0", "xx"))
    stats = mem.at("g_stats", [TT, NT, 2, 6], F32, k["start"] + k["bytes"])
    std = mem.at("g_std", [TT, NT], F32, k["start"] + k["bytes"] + 512)
    eps = mem.at("g_eps", [TT, 1], F32, k["start"] + k["bytes"] + 576)
    mv, rstd = k["mv"], k["rstd"]

    with ExitStack() as ctx:
        def sem(name):
            return ctx.enter_context(nc.semaphore("g_" + name))

        ring = ctx.enter_context(nc.psum_tensor("g_ring", [P, 4, HC], F32))
        ps_t = [ctx.enter_context(nc.psum_tensor(f"g_ps_t{s}", [P, 2, HC], F32)) for s in range(2)]
        w_landed = k["gate_landed"]
        t_landed = [[sem(f"t_landed{s}{j}") for j in range(3)] for s in range(2)]
        a_landed = [sem(f"a_landed{s}") for s in range(2)]
        w_hi, w_lo = sem("w_hi"), sem("w_lo")
        turned, hi_ready, lo_ready = sem("turned"), sem("hi_ready"), sem("lo_ready")
        gemm_done, ring_read, tanh_ready, tiles_used = (sem(n) for n in ("gemm_done", "ring_read", "tanh_ready", "tiles_used"))
        x2_ready, var_ready, std_ready = sem("x2_ready"), sem("var_ready"), sem("std_ready")
        dve_step = sem("dve_step")
        bo_landed, xx_step, half_done = sem("bo_landed"), sem("xx_step"), sem("half_done")
        GRP = (slice(0, NT // 2), slice(NT // 2, NT))
        block = ctx.enter_context(nc.Block())

        @block.sync
        def _(sp):
            for t in range(NT):
                if t >= 2:
                    sp.wait_ge(tiles_used, t - 1)
                rows = slice(t * TT, (t + 1) * TT)
                for j, (dst, src) in enumerate(((xn_t, io["xn"][rows, :]), (xx_t, io["x"][rows, :]),
                                                (z0_t, io["tm"][2 * NPAD + t * TT:2 * NPAD + (t + 1) * TT, :]))):
                    sp.dma_start(dst[t % 2][:, :], src).then_inc(t_landed[t % 2][j], 16)
                if t == 0:
                    for h in range(2):
                        sp.wait_ge(w_lo, 4 * h + 4)
                        sp.dma_start(raw[h][:, :, :], io["w"][STEP_WO + h]).then_inc(w_landed[h], 16)
            sp.wait_ge(w_lo, 8 + 4)
            sp.dma_start(raw[0][:, :, :], io["w"][STEP_LSTM]).then_inc(k["lstm_landed"], 16)

        @block.gpsimd
        def _(pool):
            pool.dma_start(bo_bc[:, :], io["bo"].to_broadcast([TT, D])).then_inc(bo_landed, 16)

            def load_attn(t):
                if t >= 2:
                    pool.wait_ge(lo_ready, NT + t - 1)
                pool.dma_start(attn[t % 2][:, :, :], io["attnT"][:, t * TT:(t + 1) * TT]
                               .rearrange("(b p) t -> p b t", p=P)).then_inc(a_landed[t % 2], 16)

            load_attn(0)
            load_attn(1)
            pool.wait_ge(bo_landed, 16)
            for t in range(NT):
                xx = xx_t[t % 2][:, :]
                for j in range(2):
                    pool.wait_ge(t_landed[t % 2][j], 16 * (t // 2 + 1))
                pool.tensor_tensor(xx, xx, xn_t[t % 2][:, :], ALU.add).then_inc(xx_step, 1)
                pool.wait_ge(xx_step, 2 * t + 1)
                pool.tensor_tensor(xx, xx, bo_bc[:, :], ALU.add).then_inc(xx_step, 1)
            for t in range(2, NT):
                load_attn(t)
            for t in range(NT):
                pool.wait_ge(x2_ready, t + 1)
                pool.dma_start(io["x2"][t * TT:(t + 1) * TT, :], u[:, t, :]).then_inc(k["x2_stored"], 16)

        def split_w_hi(act, m, h):
            act.wait_ge(w_landed[h], 16 * (m + 1))
            for c in range(4):
                act.activation(whi[h][:, 2 * c:2 * c + 2, :], raw[h][:, 2 * c:2 * c + 2, :], ACT.Copy).then_inc(w_hi, 1)

        def split_w_lo(dve, m, h):
            for c in range(4):
                dve.wait_ge(w_hi, 8 * m + 4 * h + c + 1)
                dve.tensor_tensor(wlo[h][:, 2 * c:2 * c + 2, :], raw[h][:, 2 * c:2 * c + 2, :],
                                  whi[h][:, 2 * c:2 * c + 2, :].bitcast(F32), ALU.subtract).then_inc(w_lo, 1)

        @block.scalar
        def _(act):
            def high(t):
                act.wait_ge(turned, t + 1)
                if t >= 2:
                    act.wait_ge(gemm_done, t - 1)
                act.activation(aT_hi[t % 2][:, :].rearrange("p (b x) -> p b x", b=2), ps_t[t % 2][:, :, 0:4 * TT],
                               ACT.Copy).then_inc(hi_ready, 1)

            high(0)
            split_w_hi(act, 0, 0)
            high(1)
            split_w_hi(act, 0, 1)
            for t in range(NT):
                if t >= 2:
                    high(t)
                if t >= 2:
                    act.wait_ge(tiles_used, t - 1)
                act.activation(th[t % 2][:, :], u[:, t, :], ACT.Tanh).then_inc(tanh_ready, 1)

            def high_attn(t):
                act.wait_ge(a_landed[t % 2], 16 * (t // 2 + 1))
                act.wait_ge(gemm_done, NT + t - 1)
                act.activation(aT_hi[t % 2][:, :], attn[t % 2][:, :, :].rearrange("p b t -> p (b t)"), ACT.Copy
                               ).then_inc(hi_ready, 1)

            high_attn(0)
            act.wait_ge(half_done, 1)
            split_w_hi(act, 1, 0)
            high_attn(1)
            act.wait_ge(gemm_done, NT)
            split_w_hi(act, 1, 1)

            def root(g):
                act.wait_ge(var_ready, g + 1)
                act.activation(std[:, GRP[g]], mv[:, GRP[g], 1], ACT.Sqrt, bias=eps[:, :]).then_inc(std_ready, 1)

            for t in range(2, NT):
                high_attn(t)
                if t == NT - 2:
                    root(0)
            root(1)

        @block.vector
        def _(dve):
            ch = Chain(dve, dve_step)

            def low(t):
                dve.wait_ge(hi_ready, t + 1)
                dve.tensor_tensor(aT_lo[t % 2][:, :].rearrange("p (b x) -> p b x", b=2), ps_t[t % 2][:, :, 0:4 * TT],
                                  aT_hi[t % 2][:, :].bitcast(F32).rearrange("p (b x) -> p b x", b=2), ALU.subtract
                                  ).then_inc(lo_ready, 1)

            def low_attn(t):
                dve.wait_ge(hi_ready, NT + t + 1)
                dve.tensor_tensor(aT_lo[t % 2][:, :], attn[t % 2][:, :, :].rearrange("p b t -> p (b t)"),
                                  aT_hi[t % 2][:, :].bitcast(F32), ALU.subtract).then_inc(lo_ready, 1)

            low(0)
            split_w_lo(dve, 0, 0)
            low(1)
            split_w_lo(dve, 0, 1)
            for t in range(NT):
                if 1 <= t < NT - 1:
                    low(t + 1)
                for j in range(3):
                    dve.wait_ge(t_landed[t % 2][j], 16 * (t // 2 + 1))
                if t == NT - 1:
                    low_attn(0)
                    split_w_lo(dve, 1, 0)
                dve.wait_ge(tanh_ready, t + 1)
                ch.add(dve.tensor_tensor(th[t % 2][:, :], th[t % 2][:, :], xn_t[t % 2][:, :], ALU.subtract))
                dve.wait_ge(gemm_done, t + 1)
                z = z0_t[t % 2][:, :].rearrange("p (b x) -> p b x", b=2)
                dve.tensor_tensor(z, ring[0:TT, 2 * (t % 2):2 * (t % 2) + 2, :], z, ALU.add).then_inc(ring_read, 1)
                dve.wait_ge(ring_read, t + 1)
                ch.link(dve.tensor_tensor(th[t % 2][:, :], th[t % 2][:, :], z0_t[t % 2][:, :], ALU.mult))
                dve.wait_ge(xx_step, 2 * t + 2)
                dve.tensor_tensor(u[:, t, :], th[t % 2][:, :], xx_t[t % 2][:, :], ALU.add).then_inc(tiles_used, 1)

            def variances(g):
                ch.wait()
                for t in range(NT)[GRP[g]]:
                    o = dve.bn_aggr(mv[:, t, :], stats[:, t, :, :].rearrange("p a b -> p (a b)"))
                o.then_inc(var_ready, 1)

            def inverse_roots(g):
                dve.wait_ge(std_ready, g + 1)
                inverse_root(dve, ch, rstd[:, GRP[g]], std[:, GRP[g]], mv[:, GRP[g], 1], EPS)

            low_attn(1)
            split_w_lo(dve, 1, 1)
            dve.wait_ge(tiles_used, NT)
            ch.link(dve.memset(eps[:, :], EPS))
            for t in range(NT):
                if 1 <= t < NT - 1:
                    low_attn(t + 1)
                dve.wait_ge(gemm_done, NT + t + 1)
                ut = u[:, t, :].rearrange("p (b x) -> p b x", b=2)
                dve.tensor_tensor(ut, ring[0:TT, 2 * (t % 2):2 * (t % 2) + 2, :], ut, ALU.add).then_inc(x2_ready, 1)
                dve.wait_ge(x2_ready, t + 1)
                for h in range(2):
                    ch.add(dve.bn_stats(stats[:, t, h, :], u[:, t, h * HC:(h + 1) * HC]))
                if t == NT // 2 - 1:
                    variances(0)
                if t == NT - 2:
                    inverse_roots(0)
                    for s in range(2):
                        dve.tensor_scalar(k["y"][s][:, :], u[:, s, :], mv[:, s, 0:1], rstd[:, s:s + 1],
                                          ALU.subtract, ALU.mult)
            variances(1)
            inverse_roots(1)

        @block.tensor
        def _(pe):
            def turn(t):
                if t >= 2:
                    pe.wait_ge(lo_ready, t - 1)
                for kb in range(KB):
                    o = nc.tensor.transpose(ps_t[t % 2][:, kb // 4, (kb % 4) * TT:(kb % 4 + 1) * TT],
                                            u[:, t, kb * P:(kb + 1) * P], k["ident"][0:TT, 0:TT])
                o.then_inc(turned, 1)

            def gemm(t, m):
                pe.wait_ge(lo_ready, NT * m + t + 1)
                if NT * m + t >= 2:
                    if m == 0:
                        pe.wait_ge(ring_read, t - 1)
                    elif t < 2:
                        pe.wait_ge(ring_read, NT + t - 1)
                    else:
                        pe.wait_ge(x2_ready, t - 1)
                for h in range(2):
                    for kb in range(KB):
                        if t == 0 and kb % 2 == 0:
                            pe.wait_ge(w_lo, 8 * m + 4 * h + kb // 2 + 1)
                        tk = slice(kb * TT, (kb + 1) * TT)
                        o = mm3(nc, ring[0:TT, 2 * (t % 2) + h, :], (aT_hi[t % 2][:, tk], aT_lo[t % 2][:, tk]),
                                (whi[h][:, kb, :], wlo[h][:, kb, :]), kb == 0, kb == KB - 1)
                    if (m, t, h) == (0, NT - 1, 0):
                        o.then_inc(half_done, 1)
                o.then_inc(gemm_done, 1)

            turn(0)
            for t in range(NT):
                if t + 1 < NT:
                    turn(t + 1)
                gemm(t, 0)
            for t in range(NT):
                gemm(t, 1)


def phase_ffn(nc, mem, io, k):
    half = KB * HC * 4
    whi = [mem.at(f"f_whi{s}", [P, KB, HC], F32R, o) for s, o in enumerate((0, 4 * half))]
    wlo = [mem.at(f"f_wlo{s}", [P, KB, HC], F32R, o) for s, o in enumerate((half, 5 * half))]
    raw = k["raw"][0]
    mem.cursor = 3 * half
    y = k["y"]
    mem.cursor += 2 * 4 * D
    pre = [mem.next(f"f_pre{s}", [TT, HC], F32) for s in range(4)]
    mem.cursor = 6 * half
    yT_hi = mem.next("f_yT_hi", [P, KB, N], F32R)
    yT_lo = mem.next("f_yT_lo", [P, KB, N], F32R)
    mem.cursor = k["start"] + k["bytes"]
    cell = mem.next("f_cell", [TT, NT, HC], F32)
    x2h = [mem.next(f"f_x2h{s}", [TT, HC], F32) for s in range(2)]
    bias = [mem.at(f"f_bias{s}", [TT, HC], F32, k["edges_at"] + s * HC * 4) for s in range(2)]
    mv, rstd = k["mv"], k["rstd"]
    STEPS = 6

    with ExitStack() as ctx:
        def sem(name):
            return ctx.enter_context(nc.semaphore("f_" + name))

        ring = ctx.enter_context(nc.psum_tensor("f_ring", [P, 4, HC], F32))
        ps_t = [ctx.enter_context(nc.psum_tensor(f"f_ps_t{s}", [P, 2, HC], F32)) for s in range(2)]
        w_landed = k["lstm_landed"]
        bias_landed, x2_landed = ([sem(f"{n}{s}") for s in range(2)] for n in ("bias_landed", "x2_landed"))
        h_landed = [sem(f"h_landed{s}") for s in range(2)]
        w_hi, w_lo = sem("w_hi"), sem("w_lo")
        y_ready, turned, hi_ready, lo_ready = sem("y_ready"), sem("turned"), sem("hi_ready"), sem("lo_ready")
        gemm_done, pre_ready, gate_ready, cell_ready, out_ready = (
            sem(n) for n in ("gemm_done", "pre_ready", "gate_ready", "cell_ready", "out_ready"))
        dve_step = sem("dve_step")
        out_stored = [sem(f"out_stored{s}") for s in range(4)]
        block = ctx.enter_context(nc.Block())

        @block.sync
        def _(sp):
            def load(q):
                if q >= 1:
                    sp.wait_ge(w_lo, 4 * q)
                    sp.dma_start(raw[:, :, :], io["w"][STEP_LSTM + q]).then_inc(w_landed, 16)
                if q >= 2:
                    sp.wait_ge(pre_ready, NT * (q - 1))
                sp.dma_start(bias[q % 2][:, :], io["bias_lstm"][q:q + 1, :].to_broadcast([TT, HC])
                             ).then_inc(bias_landed[q % 2], 16)

            load(0)
            for t in range(2, NT):
                if t == 4:
                    load(1)
                if t == 2:
                    sp.wait_ge(k["x2_stored"], 16 * NT)
                sp.wait_ge(turned, t - 1)
                sp.dma_start(y[t % 2][:, :], io["x2"][t * TT:(t + 1) * TT, :]).then_inc(x2_landed[t % 2], 16)
            for q in range(2, STEPS):
                load(q)

        def slot_of(v):
            return (NT * (3 * (v // NT) + 2) + v % NT) % 4

        def stores_before(v):
            return sum(1 for w in range(v) if slot_of(w) == slot_of(v))

        def store(pool, v):
            c, t = divmod(v, NT)
            pool.wait_ge(out_ready, v + 1)
            pool.dma_start(io["out"][t * TT:(t + 1) * TT, c * HC:(c + 1) * HC], pre[slot_of(v)][:, :]
                           ).then_inc(out_stored[slot_of(v)], 16)

        @block.gpsimd
        def _(pool):
            for c in range(2):
                for t in range(NT):
                    v = NT * c + t
                    if v == 0:
                        pool.wait_ge(k["x2_stored"], 16 * NT)
                    if v >= 2:
                        pool.wait_ge(out_ready, v - 1)
                    pool.dma_start(x2h[t % 2][:, :], io["x2"][t * TT:(t + 1) * TT, c * HC:(c + 1) * HC]
                                   ).then_inc(h_landed[t % 2], 16)
                    if v >= 1:
                        store(pool, v - 1)
            store(pool, 2 * NT - 1)
            for s in range(4):
                pool.wait_ge(out_stored[s], 16 * sum(1 for v in range(2 * NT) if slot_of(v) == s))

        def split_w_hi(act, q):
            act.wait_ge(w_landed, 16 * (q + 1))
            if q >= 2:
                act.wait_ge(gemm_done, NT * (q - 1))
            for c in range(4):
                act.activation(whi[q % 2][:, 2 * c:2 * c + 2, :], raw[:, 2 * c:2 * c + 2, :], ACT.Copy).then_inc(w_hi, 1)

        def split_w_lo(dve, q):
            for c in range(4):
                dve.wait_ge(w_hi, 4 * q + c + 1)
                dve.tensor_tensor(wlo[q % 2][:, 2 * c:2 * c + 2, :], raw[:, 2 * c:2 * c + 2, :],
                                  whi[q % 2][:, 2 * c:2 * c + 2, :].bitcast(F32), ALU.subtract).then_inc(w_lo, 1)

        @block.scalar
        def _(act):
            split_w_hi(act, 0)

            def high(t):
                act.wait_ge(turned, t + 1)
                act.activation(yT_hi[:, :, t * TT:(t + 1) * TT].rearrange("p (b k) t -> p b k t", b=2),
                               ps_t[t % 2][:, :, 0:4 * TT].rearrange("p b (k t) -> p b k t", t=TT), ACT.Copy
                               ).then_inc(hi_ready, 1)

            high(0)
            for q in range(STEPS):
                c, gate = divmod(q, 3)
                for t in range(NT):
                    n = NT * q + t
                    if n + 1 < NT:
                        high(n + 1)
                    if n == 5:
                        split_w_hi(act, 1)
                    if gate == 2:
                        act.wait_ge(cell_ready, NT * c + t + 1)
                        act.activation(cell[:, t, :], cell[:, t, :], ACT.Tanh)
                    act.wait_ge(pre_ready, n + 1)
                    if gate == 0 and c == 1:
                        act.wait_ge(out_ready, t + 1)
                    act.activation(cell[:, t, :] if gate == 0 else pre[n % 4][:, :], pre[n % 4][:, :],
                                   ACT.Tanh if gate == 1 else ACT.Sigmoid).then_inc(gate_ready, 1)
                if q + 2 < STEPS:
                    split_w_hi(act, q + 2)

        @block.vector
        def _(dve):
            ch = Chain(dve, dve_step)
            split_w_lo(dve, 0)

            def normalise(t):
                dve.wait_ge(x2_landed[t % 2], 16 * (t // 2))
                dve.tensor_scalar(y[t % 2][:, :], y[t % 2][:, :], mv[:, t, 0:1], rstd[:, t:t + 1],
                                  ALU.subtract, ALU.mult).then_inc(y_ready, 1)

            def low(t):
                dve.wait_ge(hi_ready, t + 1)
                sl = slice(t * TT, (t + 1) * TT)
                dve.tensor_tensor(yT_lo[:, :, sl].rearrange("p (b k) t -> p b k t", b=2),
                                  ps_t[t % 2][:, :, 0:4 * TT].rearrange("p b (k t) -> p b k t", t=TT),
                                  yT_hi[:, :, sl].bitcast(F32).rearrange("p (b k) t -> p b k t", b=2), ALU.subtract
                                  ).then_inc(lo_ready, 1)

            def finish(n):
                q, t = divmod(n, NT)
                c, gate = divmod(q, 3)
                dve.wait_ge(gate_ready, n + 1)
                if gate == 1:
                    dve.tensor_tensor(cell[:, t, :], cell[:, t, :], pre[n % 4][:, :], ALU.mult).then_inc(cell_ready, 1)
                elif gate == 2:
                    ch.link(dve.tensor_tensor(pre[n % 4][:, :], pre[n % 4][:, :], cell[:, t, :], ALU.mult))
                    dve.wait_ge(h_landed[t % 2], 16 * (NT // 2 * c + t // 2 + 1))
                    dve.tensor_tensor(pre[n % 4][:, :], pre[n % 4][:, :], x2h[t % 2][:, :], ALU.add
                                      ).then_inc(out_ready, 1)

            def add_bias(n):
                q, t = divmod(n, NT)
                if t == 0:
                    dve.wait_ge(bias_landed[q % 2], 16 * (q // 2 + 1))
                dve.wait_ge(gemm_done, n + 1)
                if n >= 4:
                    before = n - 4
                    qb, tb = divmod(before, NT)
                    cb, gb = divmod(qb, 3)
                    if gb == 0:
                        dve.wait_ge(gate_ready, before + 1)
                    elif gb == 1:
                        dve.wait_ge(cell_ready, NT * cb + tb + 1)
                    else:
                        v = NT * cb + tb
                        dve.wait_ge(out_stored[slot_of(v)], 16 * (stores_before(v) + 1))
                dve.tensor_tensor(pre[n % 4][:, :], ring[0:TT, n % 4, :], bias[q % 2][:, :], ALU.add
                                  ).then_inc(pre_ready, 1)

            low(0)
            for n in range(NT * STEPS):
                if n + 1 < NT:
                    low(n + 1)
                if n + 2 < NT:
                    normalise(n + 2)
                if n == 5:
                    split_w_lo(dve, 1)
                add_bias(n)
                if n >= 1:
                    finish(n - 1)
                if n % NT == NT - 1 and n // NT + 2 < STEPS:
                    split_w_lo(dve, n // NT + 2)
            finish(NT * STEPS - 1)

        @block.tensor
        def _(pe):
            def turn(t):
                if t >= 2:
                    pe.wait_ge(y_ready, t - 1)
                    pe.wait_ge(lo_ready, t - 1)
                for kb in range(KB):
                    o = nc.tensor.transpose(ps_t[t % 2][:, kb // 4, (kb % 4) * TT:(kb % 4 + 1) * TT],
                                            y[t % 2][:, kb * P:(kb + 1) * P], k["ident"][0:TT, 0:TT])
                o.then_inc(turned, 1)

            turn(0)
            for q in range(STEPS):
                for t in range(NT):
                    if q == 0 and t + 1 < NT:
                        turn(t + 1)
                    n = NT * q + t
                    if q == 0:
                        pe.wait_ge(lo_ready, t + 1)
                    if n >= 4:
                        pe.wait_ge(pre_ready, n - 3)
                    for kb in range(KB):
                        if t == 0 and kb % 2 == 0:
                            pe.wait_ge(w_lo, 4 * q + kb // 2 + 1)
                        tk = slice(t * TT, (t + 1) * TT)
                        o = mm3(nc, ring[0:TT, n % 4, :], (yT_hi[:, kb, tk], yT_lo[:, kb, tk]),
                                (whi[q % 2][:, kb, :], wlo[q % 2][:, kb, :]), kb == 0, kb == KB - 1)
                    o.then_inc(gemm_done, 1)


def inverse_root(dve, ch, out, root, var, eps):
    ch.link(dve.reciprocal(out[:, :], root[:, :]))
    ch.link(dve.tensor_tensor(root[:, :], out[:, :], out[:, :], ALU.mult))
    ch.link(dve.scalar_tensor_tensor(root[:, :], var, eps, root[:, :], ALU.add, ALU.mult))
    ch.link(dve.tensor_scalar(root[:, :], root[:, :], -0.5, 1.5, ALU.mult, ALU.add))
    ch.link(dve.tensor_tensor(out[:, :], out[:, :], root[:, :], ALU.mult))


def slot_of_rank(dve, ch, k, tmp):
    ch.link(dve.tensor_scalar(tmp[:, :], k["rank"][:, :], float(P), None, ALU.is_ge))
    for c in range(2, CAP):
        ch.link(dve.scalar_tensor_tensor(tmp[:, :], k["rank"][:, :], float(c * P), tmp[:, :], ALU.is_ge, ALU.add))
    ch.add(dve.scalar_tensor_tensor(k["lo"][:, :], tmp[:, :], float(-P), k["rank"][:, :], ALU.mult, ALU.add))
    ch.link(dve.scalar_tensor_tensor(k["hi"][:, :], k["bkt"][:, :], float(CAP), tmp[:, :], ALU.mult, ALU.add))


def one_hots(dve, k, out, j):
    i16 = k["iota16"]
    col = {n: k[n][:, bass.ds(j, 1)] for n in ("lo", "hi", "srcf", "dl1", "dl", "bkt")}
    dve.tensor_scalar(out[:, 0:128], i16[0:EP, 0:128], col["lo"], col["srcf"], ALU.is_equal, ALU.mult)
    dve.tensor_scalar(out[:, 128:256], i16[0:EP, 0:128], col["lo"], col["dl1"], ALU.is_equal, ALU.mult)
    dve.tensor_scalar(out[:, 256:256 + NC], i16[0:EP, 0:NC], col["hi"], None, ALU.is_equal)
    dve.tensor_scalar(out[:, 496:496 + TT], i16[0:EP, 0:TT], col["dl"], None, ALU.is_equal)
    return dve.tensor_scalar(out[:, 622:622 + NB], i16[0:EP, 0:NB], col["bkt"], None, ALU.is_equal)


def table_products(nc, j, ps_src, ps_dst, ps_cnt):
    hi = j[:, 256:256 + NC]
    nc.tensor.matmul(ps_src[0:P, 0:NC], j[:, 0:128], hi, start=False, stop=False)
    o = nc.tensor.matmul(ps_dst[0:P, 0:NC], j[:, 128:256], hi, start=False, stop=False)
    if ps_cnt is not None:
        o = nc.tensor.matmul(ps_cnt[0:TT, 0:NB], j[:, 496:496 + TT], j[:, 622:622 + NB], start=False, stop=False)
    return o


def read_table(dve, k, ps_src, ps_dst):
    dve.tensor_copy(k["slot_src"][:, 0:NC], ps_src[:, 0:NC])
    dve.memset(k["slot_src"][:, NC:NC + 2 * CAP], 0.0)
    dve.tensor_scalar(k["slot_dst"][:, 0:NC], ps_dst[:, 0:NC], 1.0, None, ALU.subtract)
    return dve.memset(k["slot_dst"][:, NC:NC + 2 * CAP], -1.0)


def kept_tensors(mem):
    half = KB * HC * 4
    mem.cursor = 6 * half + 2 * KB * N * 4
    start = mem.cursor
    k = {
        "ident": mem.next("ident", [P, P], F32),
        "iota16": mem.next("iota16", [P, 256], F16),
        "slot_src": mem.next("slot_src", [P, NC + 2 * CAP], F32),
        "slot_dst": mem.next("slot_dst", [P, NC + 2 * CAP], F32),
        "rc": mem.next("rc", [TT, NB], F32),
        "rounds": mem.next("rounds", [P, 1], I32),
    }
    k["mv"] = mem.next("mv", [TT, NT, 2], F32)
    k["rstd"] = mem.next("rstd", [TT, NT], F32)
    k["edges_at"] = mem.cursor
    for n in ("srcf", "dl", "dl1", "bkt", "lo", "hi", "rank"):
        k[n] = mem.next("e_" + n, [EP, EJ], F32)
    k["start"], k["bytes"] = start, mem.cursor - start
    k["y"] = [mem.at(f"y{s}", [TT, D], F32, 3 * half + s * 4 * D) for s in range(2)]
    k["raw"] = [mem.at(f"raw{s}", [P, KB, HC], F32, (2 + s) * half) for s in range(2)]
    return k


def build(nc, io):
    mem = Memory(nc)
    keep = kept_tensors(mem)
    with ExitStack() as ctx:
        for name in ("rel_landed", "gate_landed"):
            keep[name] = [ctx.enter_context(nc.semaphore(f"{name}{h}")) for h in range(2)]
        keep["x2_stored"] = ctx.enter_context(nc.semaphore("x2_stored"))
        keep["lstm_landed"] = ctx.enter_context(nc.semaphore("lstm_landed"))
        phase_project(nc, mem, io, keep)
        phase_attend(nc, mem, io, keep)
        keep["u"] = phase_relate(nc, mem, io, keep)
        phase_update(nc, mem, io, keep)
        phase_ffn(nc, mem, io, keep)


def kernel(**inputs):
    import numpy as _np
    import concourse.bacc as _bacc
    from concourse import mybir as _mybir
    from concourse.bass_utils import run_bass_kernel_spmd as _run

    a = {n: _np.asarray(v) for n, v in inputs.items()}

    def halves(w):
        return w.reshape(KB, P, 2, HC).transpose(2, 1, 0, 3)

    gnn, mix, ffn = "L0_gnn_", "L0_mix_", "L0_ffn_"
    gate = a[gnn + "w_gate"]
    mats = [a[mix + "Wq"], a[mix + "Wk"], a[mix + "Wv"], a[gnn + "root"], gate[D:]]
    mats += [a[gnn + "weight"][r] for r in range(R)] + [gate[:D], a[mix + "Wo"]]
    steps = [s for w in mats for s in halves(w)]
    lstm = [halves(a[ffn + n][:, D:].T) for n in ("W_i", "W_c", "W_o")]
    steps += [w[h] for h in range(2) for w in lstm]
    edges = _np.zeros((3, EP * EJ), _np.int32)
    edges[2] = -1
    for i, n in enumerate(("src", "dst", "edge_type_8")):
        edges[i, :a[n].shape[0]] = a[n]
    host = {
        "x": a["x"],
        "w": _np.ascontiguousarray(_np.stack(steps)),
        "edges": _np.ascontiguousarray(edges.reshape(3, EP, EJ).transpose(1, 0, 2)),
        "bias_qk": _np.ascontiguousarray(_np.stack([a[mix + "bq"], a[mix + "bk"]]).reshape(2, KB, P).transpose(2, 0, 1)),
        "bias_tm": _np.ascontiguousarray(
            _np.stack([a[mix + "bv"], a[gnn + "bias"], a[gnn + "b_gate"]]).reshape(6, HC)),
        "bo": a[mix + "bo"].reshape(1, D),
        "bias_lstm": _np.ascontiguousarray(_np.stack([a[ffn + n] for n in ("b_i", "b_c", "b_o")]).reshape(3, 2, HC)
                                           .transpose(1, 0, 2).reshape(6, HC)),
        "rfT": _np.ascontiguousarray(a[mix + "rf"].T),
    }
    nc = _bacc.Bacc("TRN2", target_bir_lowering=False, num_devices=1)
    io, arrays = {}, {}
    for n, v in host.items():
        arrays["in_" + n] = v
        io[n] = nc.dram_tensor("in_" + n, v.shape, _mybir.dt.from_np(v.dtype), kind="ExternalInput").ap()
    for n, shape, dt in (("qkT", (2 * D, NPAD), F32), ("tm", (3 * NPAD, D), F32), ("rows", (N, 2 * D), F16),
                         ("xn", (N, D), F32), ("attnT", (D, NPAD), F32), ("x2", (N, D), F32)):
        io[n] = nc.dram_tensor("mid_" + n, shape, dt, kind=MID).ap()
    io["out"] = nc.dram_tensor("out_0_dram", (N, D), F32, kind="ExternalOutput").ap()
    build(nc, io)
    r = _run(nc, [arrays], core_ids=[0])
    return r.results[0]["out_0_dram"]
```
